# Optimizing a Trainium2 kernel written in Bass

```python
import numpy as np
import jax
import jax.numpy as jnp

def _softmax(x, axis=-1):
    return jax.nn.softmax(x, axis=axis)

def _gelu(x):
    return jax.nn.gelu(x, approximate=True)

def _silu(x):
    return jax.nn.silu(x)

def _sigmoid(x):
    return jax.nn.sigmoid(x)

def _layernorm(x, axis=-1, eps=1e-05):
    m = jnp.mean(x, axis=axis, keepdims=True)
    v = jnp.var(x, axis=axis, keepdims=True)
    return (x - m) / jnp.sqrt(v + eps)

def _scatter_add(tgt, idx, src, axis=0):
    return tgt.at[idx].add(src)

def _segment_sum(src, seg, n):
    return jax.ops.segment_sum(src, seg, n)
kernel_name = 'mk_prb_d2_jaxref_r8_6027f0'

def setup_inputs(seed: int=0):
    np.random.seed(seed)
    _w = jnp.asarray

    def _L0_attn_setup():
        import jax, jax.numpy as jnp
        import numpy as np
        B, T, D = (1, 512, 256)
        H, HKV = (16, 4)
        DH = D // H
        GROUP = H // HKV
        ROPE_BASE = 10000.0

        def _rope_sincos(t, half):
            inv_freq = 1.0 / ROPE_BASE ** (jnp.arange(half, dtype=jnp.float32) / half)
            ang = jnp.arange(t, dtype=jnp.float32)[:, None] * inv_freq
            return (jnp.sin(ang)[None, :, None, :], jnp.cos(ang)[None, :, None, :])

        def _apply_rope(x, sin, cos, half):
            x1, x2 = (x[..., :half], x[..., half:])
            return jnp.concatenate([x1 * cos - x2 * sin, x1 * sin + x2 * cos], axis=-1)
        key = jax.random.key(seed)
        kx, kq, kk, kv, ko = jax.random.split(key, 5)
        s = 0.02
        return {'x': jax.random.normal(kx, (B, T, D), dtype=jnp.float32), 'Wq': jax.random.normal(kq, (D, D), dtype=jnp.float32) * s, 'Wk': jax.random.normal(kk, (D, HKV * DH), dtype=jnp.float32) * s, 'Wv': jax.random.normal(kv, (D, HKV * DH), dtype=jnp.float32) * s, 'Wo': jax.random.normal(ko, (D, D), dtype=jnp.float32) * s}
    _L0_attn_in = _L0_attn_setup()

    def _L0_ffn_setup():
        import jax, jax.numpy as jnp
        import numpy as np
        B, L, D = (2, 128, 256)
        E, K = (8, 2)
        H, HS = (176, 352)
        key = jax.random.key(seed)
        ks = jax.random.split(key, 9)
        s = 0.02
        return {'x': jax.random.normal(ks[0], (B, L, D), dtype=jnp.float32), 'gate_w': jax.random.normal(ks[1], (E, D), dtype=jnp.float32) * s, 'w_gate': jax.random.normal(ks[2], (E, D, H), dtype=jnp.float32) * s, 'w_up': jax.random.normal(ks[3], (E, D, H), dtype=jnp.float32) * s, 'w_down': jax.random.normal(ks[4], (E, H, D), dtype=jnp.float32) * s, 'shgate_w': jax.random.normal(ks[5], (D,), dtype=jnp.float32) * s, 'shw_gate': jax.random.normal(ks[6], (D, HS), dtype=jnp.float32) * s, 'shw_up': jax.random.normal(ks[7], (D, HS), dtype=jnp.float32) * s, 'shw_down': jax.random.normal(ks[8], (HS, D), dtype=jnp.float32) * s}
    _L0_ffn_in = _L0_ffn_setup()

    def _L1_attn_setup():
        import jax, jax.numpy as jnp
        import numpy as np
        DIM = 256
        HEADS = 16
        HEAD_DIM = DIM // HEADS
        CHUNK = 128
        B, N = (4, 256)

        def _rmsnorm(x, w, eps):
            return x * jax.lax.rsqrt(jnp.mean(x * x, axis=-1, keepdims=True) + eps) * w

        def _weight_quant(w):
            scale = 1.0 / jnp.clip(jnp.mean(jnp.abs(w)), 1e-05, None)
            q = jnp.clip(jnp.round(w * scale), -1.0, 1.0) / scale
            return w + jax.lax.stop_gradient(q - w)

        def _forward(x, qkv_w, qkv_norm_w, proj_w, proj_norm_w, norm_w, s):
            Bb, Nn, C = x.shape
            H, D, T = (HEADS, HEAD_DIM, CHUNK)
            nc = Nn // T
            eps = jnp.finfo(x.dtype).eps
            scale = D ** (-0.5)
            h = _rmsnorm(x, qkv_norm_w, eps)
            qkv = h @ _weight_quant(qkv_w).T
            qkv = qkv.reshape(Bb, Nn, 3, H, D)
            q, k, v = (qkv[:, :, 0], qkv[:, :, 1], qkv[:, :, 2])

            def chunks(t):
                return t.reshape(Bb, nc, T, H, D).transpose(1, 0, 3, 2, 4)
            qc, kc, vc = (chunks(q), chunks(k), chunks(v))
            tt = jnp.arange(T, dtype=x.dtype)
            lam_t = jnp.exp(-s[:, None] * tt)
            lam_rev = jnp.exp(-s[:, None] * (T - tt))
            diff = tt[:, None] - tt[None, :]
            mask = jnp.where(diff >= 0, jnp.exp(-s[:, None, None] * diff), 0.0)
            lam_T = jnp.exp(-s * T)[:, None, None]

            def step(S, qkv_c):
                qi, ki, vi = qkv_c
                scores = jnp.einsum('bhtd,bhsd,hts->bhts', qi, ki, mask)
                intra = jnp.einsum('bhts,bhsd->bhtd', scores, vi)
                cross = jnp.einsum('bhtd,ht,bhde->bhte', qi, lam_t, S)
                o = scale * (intra + cross)
                kv = jnp.einsum('bhtd,ht,bhte->bhde', ki, lam_rev, vi)
                return (lam_T * S + kv, o)
            S0 = jnp.zeros((Bb, H, D, D), x.dtype)
            _, outs = jax.lax.scan(step, S0, (qc, kc, vc))
            out = outs.transpose(1, 0, 3, 2, 4).reshape(Bb, Nn, C)
            out = _rmsnorm(out, norm_w, 1e-06)
            out = _rmsnorm(out, proj_norm_w, eps) @ _weight_quant(proj_w).T
            return out
        key = jax.random.key(seed)
        ks = jax.random.split(key, 3)
        x = jax.random.normal(ks[0], (B, N, DIM), jnp.float32)
        bound = float(1.0 / np.sqrt(DIM))
        qkv_w = jax.random.uniform(ks[1], (3 * DIM, DIM), jnp.float32, -bound, bound)
        proj_w = jax.random.uniform(ks[2], (DIM, DIM), jnp.float32, -bound, bound)
        return {'x': x, 'qkv_w': qkv_w, 'qkv_norm_w': jnp.ones((DIM,), jnp.float32), 'proj_w': proj_w, 'proj_norm_w': jnp.ones((DIM,), jnp.float32), 'norm_w': jnp.ones((DIM,), jnp.float32), 's': jnp.full((HEADS,), 0.02, jnp.float32)}
    _L1_attn_in = _L1_attn_setup()

    def _L1_ffn_setup():
        import jax, jax.numpy as jnp
        import numpy as np
        B, S, D = (4, 256, 256)
        E = 8
        N_SHARE = 2
        N_ROUTED = E - N_SHARE
        H = 1024 // E
        key = jax.random.key(seed)
        ks = jax.random.split(key, 12)
        s = 0.02
        return {'x': jax.random.normal(ks[0], (B, S, D), jnp.float32), 'Wg': jax.random.normal(ks[1], (D, E), jnp.float32) * s, 'bg': jnp.zeros((E,), jnp.float32), 'Wgate': jax.random.normal(ks[2], (N_ROUTED, D, H), jnp.float32) * s, 'bgate': jnp.zeros((N_ROUTED, H), jnp.float32), 'Wup': jax.random.normal(ks[3], (N_ROUTED, D, H), jnp.float32) * s, 'bup': jnp.zeros((N_ROUTED, H), jnp.float32), 'Wdown': jax.random.normal(ks[4], (N_ROUTED, H, D), jnp.float32) * s, 'bdown': jnp.zeros((N_ROUTED, D), jnp.float32), 'Ws_up': jax.random.normal(ks[5], (D, N_SHARE * H), jnp.float32) * s, 'bs_up': jnp.zeros((N_SHARE * H,), jnp.float32), 'Ws_down': jax.random.normal(ks[6], (N_SHARE * H, D), jnp.float32) * s, 'bs_down': jnp.zeros((D,), jnp.float32)}
    _L1_ffn_in = _L1_ffn_setup()
    _d = {'L0_attn_x': _L0_attn_in['x'], 'L0_attn_Wq': _L0_attn_in['Wq'], 'L0_attn_Wk': _L0_attn_in['Wk'], 'L0_attn_Wv': _L0_attn_in['Wv'], 'L0_attn_Wo': _L0_attn_in['Wo'], 'L0_ffn_gate_w': _L0_ffn_in['gate_w'], 'L0_ffn_w_gate': _L0_ffn_in['w_gate'], 'L0_ffn_w_up': _L0_ffn_in['w_up'], 'L0_ffn_w_down': _L0_ffn_in['w_down'], 'L0_ffn_shgate_w': _L0_ffn_in['shgate_w'], 'L0_ffn_shw_gate': _L0_ffn_in['shw_gate'], 'L0_ffn_shw_up': _L0_ffn_in['shw_up'], 'L0_ffn_shw_down': _L0_ffn_in['shw_down'], 'L1_attn_qkv_w': _L1_attn_in['qkv_w'], 'L1_attn_qkv_norm_w': _L1_attn_in['qkv_norm_w'], 'L1_attn_proj_w': _L1_attn_in['proj_w'], 'L1_attn_proj_norm_w': _L1_attn_in['proj_norm_w'], 'L1_attn_norm_w': _L1_attn_in['norm_w'], 'L1_attn_s': _L1_attn_in['s'], 'L1_ffn_Wg': _L1_ffn_in['Wg'], 'L1_ffn_bg': _L1_ffn_in['bg'], 'L1_ffn_Wgate': _L1_ffn_in['Wgate'], 'L1_ffn_bgate': _L1_ffn_in['bgate'], 'L1_ffn_Wup': _L1_ffn_in['Wup'], 'L1_ffn_bup': _L1_ffn_in['bup'], 'L1_ffn_Wdown': _L1_ffn_in['Wdown'], 'L1_ffn_bdown': _L1_ffn_in['bdown'], 'L1_ffn_Ws_up': _L1_ffn_in['Ws_up'], 'L1_ffn_bs_up': _L1_ffn_in['bs_up'], 'L1_ffn_Ws_down': _L1_ffn_in['Ws_down'], 'L1_ffn_bs_down': _L1_ffn_in['bs_down']}
    _x0 = _d['L0_attn_x']
    _d['L0_attn_x'] = jax.random.normal(jax.random.fold_in(jax.random.key(seed), 1), (4, 256, 256), dtype=_x0.dtype)
    del _x0
    return _d

def reference(L0_attn_x, L0_attn_Wq, L0_attn_Wk, L0_attn_Wv, L0_attn_Wo, L0_ffn_gate_w, L0_ffn_w_gate, L0_ffn_w_up, L0_ffn_w_down, L0_ffn_shgate_w, L0_ffn_shw_gate, L0_ffn_shw_up, L0_ffn_shw_down, L1_attn_qkv_w, L1_attn_qkv_norm_w, L1_attn_proj_w, L1_attn_proj_norm_w, L1_attn_norm_w, L1_attn_s, L1_ffn_Wg, L1_ffn_bg, L1_ffn_Wgate, L1_ffn_bgate, L1_ffn_Wup, L1_ffn_bup, L1_ffn_Wdown, L1_ffn_bdown, L1_ffn_Ws_up, L1_ffn_bs_up, L1_ffn_Ws_down, L1_ffn_bs_down):

    def _L0_attn_ref(x, Wq, Wk, Wv, Wo):
        import jax, jax.numpy as jnp
        import numpy as np
        B, T, D = (1, 512, 256)
        H, HKV = (16, 4)
        DH = D // H
        GROUP = H // HKV
        ROPE_BASE = 10000.0

        def _rope_sincos(t, half):
            inv_freq = 1.0 / ROPE_BASE ** (jnp.arange(half, dtype=jnp.float32) / half)
            ang = jnp.arange(t, dtype=jnp.float32)[:, None] * inv_freq
            return (jnp.sin(ang)[None, :, None, :], jnp.cos(ang)[None, :, None, :])

        def _apply_rope(x, sin, cos, half):
            x1, x2 = (x[..., :half], x[..., half:])
            return jnp.concatenate([x1 * cos - x2 * sin, x1 * sin + x2 * cos], axis=-1)
        b, t, d = x.shape
        q = (x @ Wq).reshape(b, t, H, DH)
        k = (x @ Wk).reshape(b, t, HKV, DH)
        v = (x @ Wv).reshape(b, t, HKV, DH)
        half = DH // 2
        sin, cos = _rope_sincos(t, half)
        q = _apply_rope(q, sin, cos, half)
        k = _apply_rope(k, sin, cos, half)
        qg = q.reshape(b, t, HKV, GROUP, DH)
        att = jnp.einsum('bthgd,bshd->bhgts', qg, k) / np.float32(np.sqrt(DH))
        causal = jnp.tril(jnp.ones((t, t), dtype=bool))
        att = jnp.where(causal[None, None, None, :, :], att, -jnp.inf)
        att = jax.nn.softmax(att, axis=-1)
        y = jnp.einsum('bhgts,bshd->bthgd', att, v).reshape(b, t, d)
        return y @ Wo

    def _L0_ffn_ref(x, gate_w, w_gate, w_up, w_down, shgate_w, shw_gate, shw_up, shw_down):
        import jax, jax.numpy as jnp
        import numpy as np
        B, L, D = (2, 128, 256)
        E, K = (8, 2)
        H, HS = (176, 352)
        b, l, d = x.shape
        xf = x.reshape(-1, d)
        logits = jnp.einsum('td,ed->te', xf.astype(jnp.float32), gate_w)
        probs = jax.nn.softmax(logits.astype(jnp.float32), axis=-1)
        weights, indices = jax.lax.top_k(probs, K)
        weights = (weights / weights.sum(-1, keepdims=True)).astype(x.dtype)
        onehot = jax.nn.one_hot(indices, E, dtype=x.dtype)
        combine = jnp.einsum('tk,tke->te', weights, onehot)
        g = jnp.einsum('td,edh->teh', xf, w_gate)
        u = jnp.einsum('td,edh->teh', xf, w_up)
        h = jax.nn.silu(g) * u
        out = jnp.einsum('teh,ehd,te->td', h.astype(jnp.float32), w_down.astype(jnp.float32), combine.astype(jnp.float32))
        sgate = jax.nn.sigmoid(xf @ shgate_w)[:, None]
        sh = jax.nn.silu(xf @ shw_gate) * (xf @ shw_up) @ shw_down
        out = out + (sgate * sh).astype(jnp.float32)
        return out.astype(x.dtype).reshape(b, l, d)

    def _L1_attn_ref(x, qkv_w, qkv_norm_w, proj_w, proj_norm_w, norm_w, s):
        import jax, jax.numpy as jnp
        import numpy as np
        DIM = 256
        HEADS = 16
        HEAD_DIM = DIM // HEADS
        CHUNK = 128
        B, N = (4, 256)

        def _rmsnorm(x, w, eps):
            return x * jax.lax.rsqrt(jnp.mean(x * x, axis=-1, keepdims=True) + eps) * w

        def _weight_quant(w):
            scale = 1.0 / jnp.clip(jnp.mean(jnp.abs(w)), 1e-05, None)
            q = jnp.clip(jnp.round(w * scale), -1.0, 1.0) / scale
            return w + jax.lax.stop_gradient(q - w)

        def _forward(x, qkv_w, qkv_norm_w, proj_w, proj_norm_w, norm_w, s):
            Bb, Nn, C = x.shape
            H, D, T = (HEADS, HEAD_DIM, CHUNK)
            nc = Nn // T
            eps = jnp.finfo(x.dtype).eps
            scale = D ** (-0.5)
            h = _rmsnorm(x, qkv_norm_w, eps)
            qkv = h @ _weight_quant(qkv_w).T
            qkv = qkv.reshape(Bb, Nn, 3, H, D)
            q, k, v = (qkv[:, :, 0], qkv[:, :, 1], qkv[:, :, 2])

            def chunks(t):
                return t.reshape(Bb, nc, T, H, D).transpose(1, 0, 3, 2, 4)
            qc, kc, vc = (chunks(q), chunks(k), chunks(v))
            tt = jnp.arange(T, dtype=x.dtype)
            lam_t = jnp.exp(-s[:, None] * tt)
            lam_rev = jnp.exp(-s[:, None] * (T - tt))
            diff = tt[:, None] - tt[None, :]
            mask = jnp.where(diff >= 0, jnp.exp(-s[:, None, None] * diff), 0.0)
            lam_T = jnp.exp(-s * T)[:, None, None]

            def step(S, qkv_c):
                qi, ki, vi = qkv_c
                scores = jnp.einsum('bhtd,bhsd,hts->bhts', qi, ki, mask)
                intra = jnp.einsum('bhts,bhsd->bhtd', scores, vi)
                cross = jnp.einsum('bhtd,ht,bhde->bhte', qi, lam_t, S)
                o = scale * (intra + cross)
                kv = jnp.einsum('bhtd,ht,bhte->bhde', ki, lam_rev, vi)
                return (lam_T * S + kv, o)
            S0 = jnp.zeros((Bb, H, D, D), x.dtype)
            _, outs = jax.lax.scan(step, S0, (qc, kc, vc))
            out = outs.transpose(1, 0, 3, 2, 4).reshape(Bb, Nn, C)
            out = _rmsnorm(out, norm_w, 1e-06)
            out = _rmsnorm(out, proj_norm_w, eps) @ _weight_quant(proj_w).T
            return out
        return _forward(x, qkv_w, qkv_norm_w, proj_w, proj_norm_w, norm_w, s)

    def _L1_ffn_ref(x, Wg, bg, Wgate, bgate, Wup, bup, Wdown, bdown, Ws_up, bs_up, Ws_down, bs_down):
        import jax, jax.numpy as jnp
        import numpy as np
        B, S, D = (4, 256, 256)
        E = 8
        N_SHARE = 2
        N_ROUTED = E - N_SHARE
        H = 1024 // E
        b, s, d = x.shape
        T = b * s
        n = Wgate.shape[0]
        xf = x.reshape(T, d)
        gate = xf @ Wg + bg
        vals, ids = jax.lax.top_k(gate, n)
        rows = jnp.arange(T)[:, None]
        masked = jnp.full_like(gate, -jnp.inf).at[rows, ids].set(vals)
        probs = jax.nn.softmax(masked, axis=-1)
        routed_mask = (ids[:, :, None] == jnp.arange(n)).any(axis=1)
        w = probs[:, :n] * routed_mask
        g = jnp.einsum('td,ndh->tnh', xf, Wgate) + bgate
        u = jnp.einsum('td,ndh->tnh', xf, Wup) + bup
        h = jax.nn.silu(g) * u
        eo = jnp.einsum('tnh,nhd->tnd', h, Wdown) + bdown
        routed_out = jnp.einsum('tnd,tn->td', eo, w)
        share = jax.nn.silu(xf @ Ws_up + bs_up) @ Ws_down + bs_down
        return (routed_out + share).reshape(b, s, d)
    x = L0_attn_x
    xn = _layernorm(x, axis=-1)
    x = x + _L0_attn_ref(xn, L0_attn_Wq, L0_attn_Wk, L0_attn_Wv, L0_attn_Wo) + _L0_ffn_ref(xn, L0_ffn_gate_w, L0_ffn_w_gate, L0_ffn_w_up, L0_ffn_w_down, L0_ffn_shgate_w, L0_ffn_shw_gate, L0_ffn_shw_up, L0_ffn_shw_down)
    xn = _layernorm(x, axis=-1)
    x = x + _L1_attn_ref(xn, L1_attn_qkv_w, L1_attn_qkv_norm_w, L1_attn_proj_w, L1_attn_proj_norm_w, L1_attn_norm_w, L1_attn_s) + _L1_ffn_ref(xn, L1_ffn_Wg, L1_ffn_bg, L1_ffn_Wgate, L1_ffn_bgate, L1_ffn_Wup, L1_ffn_bup, L1_ffn_Wdown, L1_ffn_bdown, L1_ffn_Ws_up, L1_ffn_bs_up, L1_ffn_Ws_down, L1_ffn_bs_down)
    return x

_drawn_inputs = setup_inputs


def setup_inputs(seed=0):
    import zlib

    import numpy as np

    out = dict(_drawn_inputs(seed))
    spreads = {'L1_attn_qkv_norm_w': (1.0, 0.544),
     'L1_attn_proj_norm_w': (1.0, 0.6),
     'L1_attn_norm_w': (1.0, 0.6),
     'L1_attn_s': (0.019999999552965164, 0.6),
     'L1_ffn_bg': (0.0, 0.8),
     'L1_ffn_bgate': (0.0, 0.8),
     'L1_ffn_bup': (0.0, 0.8),
     'L1_ffn_bdown': (0.0, 0.8),
     'L1_ffn_bs_up': (0.0, 2.0),
     'L1_ffn_bs_down': (0.0, 0.483)}
    factors = {'L0_attn_Wq': 8.0,
     'L0_attn_Wk': 8.0,
     'L0_attn_Wv': 2.797,
     'L0_attn_Wo': 2.868,
     'L0_ffn_gate_w': 5.951,
     'L0_ffn_w_gate': 5.205,
     'L0_ffn_w_up': 5.161,
     'L0_ffn_w_down': 5.163,
     'L0_ffn_shgate_w': 8.0,
     'L0_ffn_shw_gate': 5.262,
     'L0_ffn_shw_up': 5.153,
     'L0_ffn_shw_down': 5.176,
     'L1_ffn_Wg': 3.294,
     'L1_ffn_Wgate': 8.0,
     'L1_ffn_Wup': 8.0,
     'L1_ffn_Wdown': 8.0,
     'L1_ffn_Ws_up': 5.615,
     'L1_ffn_Ws_down': 3.103}
    for name, (base, spread) in spreads.items():
        noise = np.random.default_rng([zlib.crc32(name.encode()), seed]).standard_normal(out[name].shape)
        drawn = base * np.exp(spread * noise) if base else spread * noise
        out[name] = jnp.asarray(drawn.astype(out[name].dtype))
    for name, factor in factors.items():
        out[name] = (out[name] * factor).astype(out[name].dtype)
    return out
```

```python
import concourse.bass as bass
from concourse import mybir
from contextlib import ExitStack

import numpy as np

P = 128
NB, TOK, D = 4, 256, 256
TT = TOK // P
KT = D // P
H, HKV, DH = 16, 4, 16
QKV = H * DH + 2 * HKV * DH
E0, HE0, HS0 = 8, 176, 352
HID0 = E0 * HE0 + HS0
NT0 = -(-HID0 // P)
GATES = E0 + 2
NQ = QKV + GATES
E1, R1, H1, HS1 = 8, 6, 128, 256
NT1 = R1 + HS1 // P
NPAIR = H // 2
CAUSAL = -1.0e30
TILE_W = 1024
D0_AT = NT0 * TILE_W


def tile_rows(i):
    return min(P, HID0 - i * P)


CONSTS = {}
_at = 0
for _name, _n in (("ident", P), ("rope", TT * 3 * 8), ("mask", 2 * P), ("decay", 2 * P), ("block", 8),
                  ("iota", 8), ("tcol", 2)):
    CONSTS[_name] = (_at, _n)
    _at += _n
CONST_W = _at


def constants():
    c = np.zeros((P, CONST_W), np.float32)

    def put(name, a):
        at, n = CONSTS[name]
        c[:, at:at + n] = np.asarray(a, np.float32).reshape(P, n)

    put("ident", np.eye(P))
    half = DH // 2
    inv_freq = (1.0 / np.float32(10000.0) ** (np.arange(half, dtype=np.float32) / np.float32(half))).astype(np.float32)
    ang = (np.arange(TOK, dtype=np.float32)[:, None] * inv_freq).astype(np.float32)
    sin, cos = np.sin(ang), np.cos(ang)
    put("rope", np.stack([cos, -sin, sin], 1).reshape(TT, P, 3 * half).transpose(1, 0, 2))
    t, s = np.arange(P)[:, None], np.arange(P)[None, :]
    put("mask", np.concatenate([np.zeros((P, P)), np.where(s <= t, 0.0, CAUSAL)], 1))
    put("decay", np.concatenate([np.maximum(s - t, 0), np.where(s >= t, DH ** -0.5, 0.0)], 1))
    put("block", (np.arange(P)[:, None] // DH == np.arange(8)))
    put("iota", np.tile(np.arange(8), (P, 1)))
    put("tcol", np.stack([-np.arange(P), -(P - np.arange(P))], 1))
    ex = np.zeros((32, NT0 * P + R1 * H1), np.float32)
    owner = np.minimum(np.arange(HID0) // HE0, E0)
    for base in (0, 16):
        ex[base + owner, np.arange(HID0)] = 0.5
        ex[base + np.arange(R1 * H1) // H1, NT0 * P + np.arange(R1 * H1)] = 1.0
    return c, ex


def bass_two_layer_kernel(nc, x, wq, wk, wv, wo, gate_w, w_gate, w_up, w_down, shgate_w, shw_gate, shw_up,
                          shw_down, qkv_w, qkv_norm_w, proj_w, proj_norm_w, norm_w, decay_s, wg1, bg1,
                          wgate1, bgate1, wup1, bup1, wdown1, bdown1, ws_up, bs_up, ws_down, bs_down,
                          const_in, spread_in, out):
    f32, f32r = mybir.dt.float32, mybir.dt.float32r
    bf16, f16, u32 = mybir.dt.bfloat16, mybir.dt.float16, mybir.dt.uint32
    ALU, ACT, AX = mybir.AluOpType, mybir.ActivationFunctionType, mybir.AxisListType

    ctx = ExitStack()
    with ctx:
        def sb(name, shape, dt=f32):
            return ctx.enter_context(nc.sbuf_tensor(name, shape, dt))

        def bank(name):
            return ctx.enter_context(nc.psum_tensor(name, [P, 512], f32))

        x_all = sb("x_all", [P, NB, TT, D])
        cst = sb("cst", [P, CONST_W])

        def const(name):
            at, n = CONSTS[name]
            return cst[:, at:at + n]

        ident = const("ident")
        xn = sb("xn", [P, TT, D])
        st = sb("st", [P, TT, 6])
        mv = sb("mv", [P, TT, 2])
        ve = sb("ve", [P, TT])
        rstd = sb("rstd", [P, TT])
        powers = sb("powers", [P, 2])
        WR = sb("WR", [P, NT0 * TILE_W + NT0 * 2 * D], f32r)
        gu_w = WR[:, 0:D0_AT].rearrange("p (t l q c) -> p t l q c", t=NT0, l=2, q=2 * KT)
        dn_w = WR[:, D0_AT:].rearrange("p (t l n) -> p t l n", t=NT0, l=2)
        wqkv = sb("wqkv", [P, 2, KT, NQ], f32r)
        wo_r = sb("wo_r", [P, 2, KT, D], f32r)
        spread = sb("spread", [P, NT0 * P + R1 * H1], f32r)
        xT = sb("xT", [P, 2, KT, TOK], f32r)
        stack = sb("stack", [P, TT, (H + HKV) * 4 * DH], f32r)
        qT = sb("qT", [P, NPAIR, TOK], f32r)
        kTz = sb("kTz", [P, 2, 2, TOK], f32r)
        cw = sb("cw", [P, TT, P], f32r)
        cwT = sb("cwT", [P, TOK], f32r)
        hT = sb("hT", [P, 2, 2, TOK], f32r)
        yT = stack[:, 0, 0:2 * KT * TOK].rearrange("p (l k n) -> p l k n", l=2, k=KT)
        v3 = sb("v3", [P, TT, HKV, 3, DH], bf16)
        pT = sb("pT", [P, 2, 3 * TOK], f16)
        rot = sb("rot", [P, TT, (H + HKV) * DH])
        rope_a = sb("rope_a", [P, (H + HKV) * DH])
        rope_b = sb("rope_b", [P, (H + HKV) * DH])
        vr = sb("vr", [P, 2, HKV * DH])
        lg = sb("lg", [P, TT, GATES])
        top = sb("top", [P, TT, 8])
        top_ix = sb("top_ix", [P, TT, 8], u32)
        ixf = sb("ixf", [P, TT, 8])
        dz = sb("dz", [P, TT, 2])
        ez = sb("ez", [P, TT, 2])
        ez1 = sb("ez1", [P, TT, 2])
        rc = sb("rc", [P, TT, 2])
        w2nd = sb("w2nd", [P, TT])
        oh = sb("oh", [P, TT, 2, 8])
        c9 = sb("c9", [P, TT, E0 + 1])
        sm = sb("sm", [P, 3 * TOK])
        mx = sb("mx", [P, 4])
        nmax = sb("nmax", [P, 2, 4])
        pm = sb("pm", [P, 2, 3 * TOK])
        rs = sb("rs", [P, NPAIR * 4])
        rinv = sb("rinv", [P, NPAIR * 4])
        y = sb("y", [P, NPAIR, 4, DH])
        yn = sb("yn", [P, TT, D])
        th = sb("th", [P, 2, TOK])
        s2 = sb("s2", [P, 2, TOK])
        hs = sb("hs", [P, 2, TOK])
        SLOTS, SLOT_W = 4, 768
        stage = sb("stage", [P, SLOTS, SLOT_W])
        gates_nat = sb("gates_nat", [GATES, D])

        small_rows = sb("small_rows", [18, P])
        cols = sb("cols", [P, 18])
        s_b = sb("s_b", [P, H])
        ns_b = sb("ns_b", [P, H])
        nw_b = sb("nw_b", [P, D])
        bg_b = sb("bg_b", [P, E1])
        ones = sb("ones", [P, P])
        abs_sum = sb("abs_sum", [P, 3])
        w_mean = sb("w_mean", [P, 2])
        w_inv = sb("w_inv", [P, 2])
        nwm = sb("nwm", [P, 2, KT])
        lam = sb("lam", [P, 2, H])
        dm = sb("dm", [P, H, P])
        proj_t = sb("proj_t", [P, KT, D], f32r)
        bias_w = sb("bias_w", [P, 2, D], f32r)
        router_w = sb("router_w", [P, KT, 2, E1], f32r)
        qkv_t = wqkv[:, :, :, :].rearrange("p l k n -> p (l k n)")[:, 0:KT * 3 * D].rearrange("p (k n) -> p k n", k=KT)
        GU_BLOCK, DN_BLOCK = [0, 1, 3, 4, 6, 7], [2, 2, 5, 5, 8, 8, 10, 10]

        def block_of(n, at=0, width=TILE_W):
            return WR[:, n * TILE_W + at:n * TILE_W + at + width]

        def gu1_w(i):
            return block_of(GU_BLOCK[i]).rearrange("p (l q c) -> p l q c", l=2, q=4)

        def up1_w(i):
            return block_of(9, 512 * i, 512).rearrange("p (l q c) -> p l q c", l=2, q=2)

        def dn1_w(i):
            return block_of(DN_BLOCK[i], 512 * (i % 2), 512).rearrange("p (l n) -> p l n", l=2)

        qT1 = block_of(11).rearrange("p (l g n) -> p l g n", l=2, g=2)
        kT1 = block_of(12).rearrange("p (l g n) -> p l g n", l=2, g=2)
        kd = block_of(13, 0, 512).rearrange("p (l n) -> p l n", l=2)
        state = block_of(13, 512, 512).rearrange("p (l g n) -> p l g n", l=2, g=2)

        def q_pad(j):
            at = D0_AT + 5120 * (j % 2)
            return WR[:, at:at + 2048].rearrange("p (l h n) -> p l h n", l=2, h=8)

        aT = WR[:, D0_AT + 2048:D0_AT + 4096].rearrange("p (a l n) -> p a l n", a=2, l=2)
        v2 = WR[:, D0_AT + 4096:D0_AT + 5120].rearrange("p (t h l d) -> p t h l d", t=TT, h=H, l=2)
        hT1 = qT[:, 0:4, :].rearrange("p (l k) n -> p l k n", l=2)
        oT = qT[:, 4:8, :].rearrange("p (l k) n -> p l k n", l=2)
        o_tok = y[:, :, :, :].rearrange("p a b c -> p (a b c)").rearrange("p (t n) -> p t n", t=TT)
        og = sm[:, 0:TT * D].rearrange("p (t n) -> p t n", t=TT)
        cross = rope_a[:, 0:D]
        kdf = rot[:, 0, 0:D]
        stf = rot[:, 1, 0:D]
        bias_f = sm[:, 0:D]
        rh = sb("rh", [P, TT])
        ra = sb("ra", [P, TT])

        def af_at(u):
            return pm[:, u % 2, 0:4 * P]

        sq = rope_b[:, 0:D]
        ss = sb("ss", [P, 2, TT])
        r1 = sb("r1", [P, 2, TT])
        r2 = sb("r2", [P, 2, TT])
        lg1 = sb("lg1", [P, TT, E1])
        e1 = sb("e1", [P, TT, E1])
        em = sb("em", [P, 2, TT, E1])
        esum = sb("esum", [P, TT])
        erec = sb("erec", [P, TT])
        ntop = sb("ntop", [P, TT])
        c1 = sb("c1", [P, TT, R1 + 1])

        GU = [bank("gu0"), bank("gu1")]
        CB, OB = bank("cb"), bank("ob")
        X = [bank(f"x{i}") for i in range(4)]

        class Steps:

            def __init__(self, name, per):
                self.sem = ctx.enter_context(nc.semaphore(name))
                self.per = per
                self.count = 0

            def at(self, b, k):
                return self.per * b + k

        def wait(eng, steps, b, k):
            eng.wait_ge(steps.sem, steps.at(b, k))

        PREP_POOL, PREP_VEC, SMALL_IN = 6, 4, 16 * 11
        x_in = [Steps(f"x_in{b}", 0) for b in range(NB)]
        cst_in = Steps("cst_in", 0)
        gates_in = Steps("gates_in", 0)
        stage_in = [Steps(f"stage_in{k}", 0) for k in range(SLOTS)]
        w_hi, w_lo = Steps("w_hi", 0), Steps("w_lo", 0)
        prep_pool, prep_pe, prep_vec = Steps("prep_pool", 0), Steps("prep_pe", 0), Steps("prep_vec", 0)
        stats_vec = Steps("stats_vec", 4)
        rstd_pool = Steps("rstd_pool", 2)
        norm_vec = Steps("norm_vec", TT)
        xT_pe = Steps("xT_pe", 1)
        xT_hi, xT_lo = Steps("xT_hi", 1), Steps("xT_lo", 1)
        qkv_pe = Steps("qkv_pe", TT)
        rope_vec = Steps("rope_vec", 3 * TT)
        rope_pool = Steps("rope_pool", TT)
        stack_hi = Steps("stack_hi", 2 * TT)
        stack_lo = Steps("stack_lo", 2 * TT)
        v_vec = Steps("v_vec", 5 * TT)
        route_vec = Steps("route_vec", 3 * TT)
        route_pool = Steps("route_pool", 14)
        route_act = Steps("route_act", 1)
        qkT_pe = Steps("qkT_pe", 5)
        qkT_act = Steps("qkT_act", 6)
        cwT_pe, cwT_vec = Steps("cwT_pe", 1), Steps("cwT_vec", 1)
        score_pe = Steps("score_pe", 2 * NPAIR)
        max_vec = Steps("max_vec", 5 * NPAIR)
        exp_act = Steps("exp_act", 4 * NPAIR)
        pT_pe = Steps("pT_pe", 2 * NPAIR)
        pT_hi, pT_lo = Steps("pT_hi", 2 * NPAIR), Steps("pT_lo", 2 * NPAIR)
        pv_pe = Steps("pv_pe", NPAIR)
        y_vec = Steps("y_vec", NPAIR)
        yn_vec = Steps("yn_vec", 1 + TT)
        yT_pe, yT_hi, yT_lo = Steps("yT_pe", 1), Steps("yT_hi", 1), Steps("yT_lo", 1)
        gu_pe = Steps("gu_pe", NT0)
        cb_pe = Steps("cb_pe", NT0)
        dn_pe = Steps("dn_pe", NT0)
        wo_pe = Steps("wo_pe", 1)
        tanh_act = Steps("tanh_act", NT0)
        ffn_vec = Steps("ffn_vec", 3 * NT0)
        h_hi, h_lo = Steps("h_hi", NT0), Steps("h_lo", NT0)
        res_vec = Steps("res_vec", 1)
        small_in = Steps("small_in", 0)
        small_pe, small_vec = Steps("small_pe", 0), Steps("small_vec", 0)
        tern_vec, tern_pe, tern_round, tern_act = (Steps(n, 0) for n in ("tern_vec", "tern_pe", "tern_round", "tern_act"))
        decay_act, decay_vec = Steps("decay_act", 0), Steps("decay_vec", 0)
        stats1_vec, rstd1_pool, norm1_vec = Steps("stats1_vec", 4), Steps("rstd1_pool", 6), Steps("norm1_vec", 2 * TT)
        xT1_pe, xT1_hi, xT1_lo = Steps("xT1_pe", 2), Steps("xT1_hi", 3), Steps("xT1_lo", 3)
        qk1_pe, qk1_hi, qk1_lo = Steps("qk1_pe", 2), Steps("qk1_hi", 2), Steps("qk1_lo", 2)
        kv1_pe, v1_hi, v1_lo = Steps("kv1_pe", TT), Steps("v1_hi", TT), Steps("v1_lo", TT)
        kd_vec, kd_hi, kd_lo = Steps("kd_vec", 1), Steps("kd_hi", 1), Steps("kd_lo", 1)
        state_pe, state_vec, state_hi, state_lo = (Steps(n, 1) for n in ("state_pe", "state_vec", "state_hi", "state_lo"))
        cross_pe, cross_vec = Steps("cross_pe", 1), Steps("cross_vec", 1)
        route1_pe, route1_vec, route1_pool, route1_act = (Steps("route1_pe", TT), Steps("route1_vec", 17),
                                                          Steps("route1_pool", 2), Steps("route1_act", TT))
        cw1_pe, cw1_vec = Steps("cw1_pe", 1), Steps("cw1_vec", 1)
        pad_hi, pad_lo = Steps("pad_hi", 4), Steps("pad_lo", 4)
        ret_pe, ret_vec, ret_hi, ret_lo, rv_pe = (Steps(n, 8) for n in ("ret_pe", "ret_vec", "ret_hi", "ret_lo", "rv_pe"))
        o_vec, o_pool, og_vec = Steps("o_vec", 3 + 3 * TT), Steps("o_pool", 7), Steps("og_vec", TT)
        oT_pe, oT_hi, oT_lo, proj_pe = Steps("oT_pe", 1), Steps("oT_hi", 2), Steps("oT_lo", 2), Steps("proj_pe", 1)
        gu1_pe, silu_act, ffn1_vec = Steps("gu1_pe", NT1), Steps("silu_act", NT1), Steps("ffn1_vec", 2 * R1)
        cb1_pe, dn1_pe = Steps("cb1_pe", R1), Steps("dn1_pe", NT1 + 1)
        h1_hi, h1_lo = Steps("h1_hi", NT1), Steps("h1_lo", NT1)
        res1_vec = Steps("res1_vec", 1)
        out_done = Steps("out_done", 0)

        def staged(slot, n, shape):
            return stage[:, slot, 0:n].rearrange(shape[0], **shape[1])

        pieces = []

        def qkv_piece(slot):
            v = stage[:, slot, 0:KT * QKV].rearrange("p (k n) -> p k n", k=KT)
            loads = [(v[:, :, 0:256], wq.rearrange("(k p) n -> p k n", p=P)),
                     (v[:, :, 256:320], wk.rearrange("(k p) n -> p k n", p=P)),
                     (v[:, :, 320:384], wv.rearrange("(k p) n -> p k n", p=P))]
            splits = []
            for k in range(KT):
                for gp in range(2):
                    src = v[:, k, gp * 128:gp * 128 + 128].rearrange("p (r j d) -> p r j d", r=2, j=4)
                    dst = [wqkv[:, l, k, gp * 128:gp * 128 + 128].rearrange("p (j r d) -> p r j d", j=4, r=2)
                           for l in range(2)]
                    splits.append((src, *dst))
            splits.append((v[:, :, 256:384], wqkv[:, 0, :, 256:384], wqkv[:, 1, :, 256:384]))
            return loads, splits

        def gu_piece(e):
            def make(slot):
                v = stage[:, slot, 0:4 * HE0].rearrange("p (q c) -> p q c", q=4)
                if e < E0:
                    src = [w[e].rearrange("(k p) h -> p k h", p=P) for w in (w_gate, w_up)]
                else:
                    a = (e - E0) * HE0
                    src = [w[:, a:a + HE0].rearrange("(k p) h -> p k h", p=P) for w in (shw_gate, shw_up)]
                loads = [(v[:, 2 * n:2 * n + 2, :], src[n]) for n in range(2)]
                splits, at = [], e * HE0
                while at < (e + 1) * HE0:
                    t, o = divmod(at, P)
                    n = min(P - o, (e + 1) * HE0 - at)
                    s = v[:, :, at - e * HE0:at - e * HE0 + n]
                    splits.append((s, gu_w[:, t, 0, :, o:o + n], gu_w[:, t, 1, :, o:o + n]))
                    at += n
                return loads, splits
            return make

        def dn_piece(t0, n):
            def make(slot):
                v = stage[:, slot, 0:n * D].rearrange("p (t c) -> p t c", t=n)
                flat = w_down.rearrange("e h c -> (e h) c")
                loads, splits = [], []
                full = E0 * HE0 // P
                a = min(n, max(0, full - t0))
                if a:
                    loads.append((v[:, 0:a, :], flat[t0 * P:(t0 + a) * P, :].rearrange("(t p) c -> p t c", p=P)))
                for k in range(a, n):
                    r0, m = (t0 + k - full) * P, tile_rows(t0 + k)
                    loads.append((v[0:m, k, :], shw_down[r0:r0 + m, :]))
                whole = [k for k in range(n) if tile_rows(t0 + k) == P]
                if whole:
                    k = len(whole)
                    splits.append((v[:, 0:k, :], dn_w[:, t0:t0 + k, 0, :], dn_w[:, t0:t0 + k, 1, :]))
                if len(whole) < n:
                    m = tile_rows(t0 + n - 1)
                    splits.append((v[0:m, n - 1, :], dn_w[0:m, t0 + n - 1, 0, :], dn_w[0:m, t0 + n - 1, 1, :]))
                return loads, splits
            return make

        def wo_piece(slot):
            v = stage[:, slot, 0:KT * D].rearrange("p (k c) -> p k c", k=KT)
            loads = []
            for gp in range(2):
                for r in range(2):
                    for j in range(4):
                        head = (2 * gp + r) * 4 + j
                        at = (2 * j + r) * DH
                        loads.append((v[at:at + DH, gp, :], wo[head * DH:(head + 1) * DH, :]))
            return loads, [(v, wo_r[:, 0], wo_r[:, 1])]

        def spread_piece(c0, n):
            def make(slot):
                v = stage[0:32, slot, 0:n]
                return [(v, spread_in[:, c0:c0 + n])], [(v, spread[0:32, c0:c0 + n], None)]
            return make

        def ternary_piece(w, r0, n):
            def make(slot):
                v = stage[:, slot, 0:n * D].rearrange("p (r c) -> p r c", r=n)
                return [(v, w[r0 * P:(r0 + n) * P, :].rearrange("(r p) c -> p r c", p=P))], []
            return make

        def expert1_piece(e):
            def make(slot):
                v = stage[:, slot, 0:SLOT_W]
                q = v[:, 0:4 * P].rearrange("p (q c) -> p q c", q=4)
                loads = [(q[:, 2 * n:2 * n + 2, :], w[e].rearrange("(k p) h -> p k h", p=P)) for n, w in enumerate((wgate1, wup1))]
                loads.append((v[:, 4 * P:SLOT_W], wdown1[e]))
                return loads, [(q, gu1_w(e)[:, 0], gu1_w(e)[:, 1]), (v[:, 4 * P:SLOT_W], dn1_w(e)[:, 0, :], dn1_w(e)[:, 1, :])]
            return make

        def shared_up_piece(slot):
            v = stage[:, slot, 0:KT * HS1].rearrange("p (k n) -> p k n", k=KT)
            return ([(v, ws_up.rearrange("(k p) n -> p k n", p=P))],
                    [(v[:, :, i * P:(i + 1) * P], up1_w(i)[:, 0], up1_w(i)[:, 1]) for i in range(2)])

        def shared_down_piece(slot):
            v = stage[:, slot, 0:2 * D].rearrange("p (k n) -> p k n", k=2)
            return ([(v, ws_down.rearrange("(k p) n -> p k n", p=P))],
                    [(v[:, i, :], dn1_w(R1 + i)[:, 0, :], dn1_w(R1 + i)[:, 1, :]) for i in range(2)])

        def router_piece(slot):
            v = stage[:, slot, 0:KT * E1].rearrange("p (k n) -> p k n", k=KT)
            return [(v, wg1.rearrange("(k p) n -> p k n", p=P))], [(v, router_w[:, :, 0, :], router_w[:, :, 1, :])]

        order = [("qkv", qkv_piece), ("gu0", gu_piece(0)), ("sp0", spread_piece(0, 768)), ("gu1", gu_piece(1)),
                 ("dn0", dn_piece(0, 3)), ("gu2", gu_piece(2)), ("gu3", gu_piece(3)), ("dn3", dn_piece(3, 3)),
                 ("sp1", spread_piece(768, 768)), ("gu4", gu_piece(4)), ("gu5", gu_piece(5)), ("dn6", dn_piece(6, 3)), ("gu6", gu_piece(6)),
                 ("gu7", gu_piece(7)), ("wo", wo_piece), ("dn9", dn_piece(9, 3)), ("gu8", gu_piece(8)), ("sp2", spread_piece(1536, 256)),
                 ("gu9", gu_piece(9)), ("dn12", dn_piece(12, 2)),
                 ("tern0", ternary_piece(qkv_w, 0, 3)), ("tern1", ternary_piece(qkv_w, 3, 3)), ("tern2", ternary_piece(proj_w, 0, 2)),
                 ("router", router_piece), ("sp3", spread_piece(NT0 * P, R1 * H1)),
                 ("x0", expert1_piece(0)), ("x1", expert1_piece(1)), ("x2", expert1_piece(2)), ("x3", expert1_piece(3)),
                 ("x4", expert1_piece(4)), ("x5", expert1_piece(5)), ("xup", shared_up_piece), ("xdn", shared_down_piece)]
        pieces, need, arrived = {}, {}, [0] * SLOTS
        n_hi = n_lo = 0
        for n, (name, make) in enumerate(order):
            slot = n % SLOTS
            loads, splits = make(slot)
            arrived[slot] += 16 * len(loads)
            prev = order[n - SLOTS][0] if n >= SLOTS else None
            lo_splits = [s for s in splits if s[2] is not None]
            n_hi, n_lo = n_hi + len(splits), n_lo + len(lo_splits)
            pieces[name] = (slot, arrived[slot], loads, splits, lo_splits, prev)
            need[name] = (n_hi, n_lo)

        def load_piece(eng, name):
            slot, _, loads, _, _, prev = pieces[name]
            if prev is not None:
                eng.wait_ge(w_hi.sem, need[prev][0])
                eng.wait_ge(w_lo.sem, need[prev][1])
                if prev.startswith("tern"):
                    eng.wait_ge(tern_pe.sem, 1 + 4)
            for dst, src in loads:
                eng.dma_start(dst, src).then_inc(stage_in[slot].sem, 16)

        def split_hi(eng, name):
            slot, landed, _, splits, _, _ = pieces[name]
            eng.wait_ge(stage_in[slot].sem, landed)
            if name in FREED_BY:
                wait(eng, gu_pe, NB - 1, FREED_BY[name] + 1)
            for src, hi, _ in splits:
                eng.activation(hi, src, ACT.Copy).then_inc(w_hi.sem, 1)

        def split_lo(eng, name):
            _, _, _, _, lo_splits, _ = pieces[name]
            eng.wait_ge(w_hi.sem, need[name][0])
            for src, hi, lo in lo_splits:
                eng.tensor_tensor(lo, src, hi.bitcast(f32), ALU.subtract).then_inc(w_lo.sem, 1)

        def weights_ready(eng, *names):
            for name in names:
                eng.wait_ge(w_hi.sem, need[name][0])
                eng.wait_ge(w_lo.sem, need[name][1])

        slot_of = {name: pieces[name][0] for name in pieces}
        MAGIC = 1.5 * 2.0 ** 23
        TERN_VEC, TERN_ROUND = 8, 9
        NORM_SLOT = 10
        EPS32 = float(np.finfo(np.float32).eps)

        BEFORE = ["qkv", "gu0", "sp0", "gu1", "dn0"]
        IN_SLOT = {0: ["gu2"], 1: ["gu3", "dn3"], 2: ["sp1", "gu4"], 3: [], 4: ["gu5", "dn6"], 5: ["gu6"], 6: ["gu7"],
                   7: ["wo", "dn9"], 8: ["gu8"], 9: ["sp2", "gu9"], 10: ["dn12"]}
        LAST_SLOT = {0: ["router"], 1: ["sp3"], 3: ["x0"], 4: ["x1"], 6: ["x2"], 7: ["x3"], 9: ["x4"], 10: ["x5"], 11: ["xup"], 12: ["xdn"]}
        FREED_BY = {"x0": 2, "x1": 2, "x2": 5, "x3": 5, "x4": 8, "x5": 8, "xup": 9, "xdn": 10}
        assert BEFORE + sum((IN_SLOT[k] for k in sorted(IN_SLOT)), []) == [n for n, _ in order][:20]

        def gu_needs(i):
            last = min((i * P + tile_rows(i) - 1) // HE0, 9)
            return ["gu0"] if i == 0 else [f"gu{last}"]

        def dn_needs(i):
            return [f"dn{3 * (i // 3)}"]

        block = ctx.enter_context(nc.Block())

        @block.sync
        def _(sp):
            sp.dma_start(x_all[:, 0], x[0].rearrange("(t p) d -> p t d", p=P)).then_inc(x_in[0].sem, 16)
            sp.dma_start(cst[:, :], const_in).then_inc(cst_in.sem, 16)
            sp.dma_start(gates_nat[0:E0, :], gate_w).then_inc(gates_in.sem, 16)
            for row in range(E0, GATES):
                sp.dma_start(gates_nat[row:row + 1, :], shgate_w.rearrange("(a n) -> a n", a=1)).then_inc(gates_in.sem, 16)
            for n, (name, _) in enumerate(order):
                if n == 5:
                    for at, w in ((0, bgate1), (6, bup1)):
                        sp.dma_start(small_rows[at:at + R1, :], w).then_inc(small_in.sem, 16)
                    for at, w in ((12, bs_up), (14, qkv_norm_w), (16, proj_norm_w)):
                        sp.dma_start(small_rows[at:at + 2, :], w.rearrange("(a n) -> a n", a=2)).then_inc(small_in.sem, 16)
                    for dst, w, m in ((s_b, decay_s, H), (nw_b, norm_w, D), (bg_b, bg1, E1)):
                        sp.dma_start(dst[:, :], w.rearrange("(a n) -> a n", a=1).broadcast_to([P, m])).then_inc(small_in.sem, 16)
                    sp.wait_ge(prep_pool.sem, PREP_POOL)
                    for at in (0, 16):
                        sp.dma_start(bias_f[at:at + R1, :], bdown1).then_inc(small_in.sem, 16)
                    sp.dma_start(bias_f[R1:R1 + 1, :], bs_down.rearrange("(a n) -> a n", a=1)).then_inc(small_in.sem, 16)
                load_piece(sp, name)
                if n == 4:
                    for b in range(1, NB):
                        sp.dma_start(x_all[:, b], x[b].rearrange("(t p) d -> p t d", p=P)).then_inc(x_in[b].sem, 16)
            for b in range(NB):
                wait(sp, res1_vec, b, 1)
                sp.dma_start(out[b].rearrange("(t p) d -> p t d", p=P), x_all[:, b]).then_inc(out_done.sem, 16)
            sp.wait_ge(out_done.sem, 16 * NB)

        @block.gpsimd
        def _(pool):
            pool.memset(powers[:, 0:1], -0.5).then_inc(prep_pool.sem, 1)
            pool.memset(powers[:, 1:2], -1.0).then_inc(prep_pool.sem, 1)
            pool.memset(cw[:, :, :].bitcast(f32), 0.0).then_inc(prep_pool.sem, 1)
            pool.memset(kTz[:, :, :, :].bitcast(f32), 0.0).then_inc(prep_pool.sem, 1)
            pool.memset(ones[:, :], 1.0).then_inc(prep_pool.sem, 1)
            pool.memset(bias_f[:, :], 0.0).then_inc(prep_pool.sem, 1)
            pool.wait_ge(prep_pool.sem, PREP_POOL)

            def rsqrt_steps(b, steps, base, eps, src, tmp, dst):
                pool.tensor_scalar(tmp, src, eps, None, ALU.add).then_inc(steps.sem, 1)
                wait(pool, steps, b, base + 1)
                pool.tensor_tensor(dst, tmp, powers[:, 0:1].broadcast_to([P, TT]), ALU.pow).then_inc(steps.sem, 1)

            half = powers[:, 0:1].broadcast_to([P, TT])

            def norm_factors(b):
                wait(pool, stats_vec, b, 4)
                if b:
                    wait(pool, norm_vec, b - 1, TT)
                rsqrt_steps(b, rstd_pool, 0, 1e-5, mv[:, :, 1], ve[:, :], rstd[:, :])

            def norm1_factors(b):
                wait(pool, stats1_vec, b, 4)
                if b:
                    wait(pool, norm1_vec, b - 1, 2 * TT)
                else:
                    wait(pool, norm_vec, NB - 1, TT)
                rsqrt_steps(b, rstd1_pool, 0, 1e-5, mv[:, :, 1], ve[:, :], rstd[:, :])
                wait(pool, rstd1_pool, b, 2)
                pool.tensor_tensor(ve[:, :], rstd[:, :], rstd[:, :], ALU.mult).then_inc(rstd1_pool.sem, 1)
                wait(pool, rstd1_pool, b, 3)
                pool.tensor_tensor(ve[:, :], ve[:, :], mv[:, :, 1], ALU.mult).then_inc(rstd1_pool.sem, 1)
                wait(pool, rstd1_pool, b, 4)
                pool.tensor_scalar(ve[:, :], ve[:, :], EPS32, None, ALU.add).then_inc(rstd1_pool.sem, 1)
                wait(pool, rstd1_pool, b, 5)
                pool.tensor_tensor(rh[:, :], ve[:, :], half, ALU.pow).then_inc(rstd1_pool.sem, 1)

            def out_factors(b):
                wait(pool, o_vec, b, 3 + 3 * TT)
                k = 0

                def step1(ins):
                    nonlocal k
                    k += 1
                    ins.then_inc(o_pool.sem, 1)
                    wait(pool, o_pool, b, k)

                step1(pool.tensor_scalar(r1[:, 0, :], ss[:, 0, :], 1.0 / D, 1e-6, ALU.mult, ALU.add))
                step1(pool.tensor_tensor(r1[:, 1, :], r1[:, 0, :], half, ALU.pow))
                step1(pool.tensor_tensor(r2[:, 0, :], r1[:, 1, :], r1[:, 1, :], ALU.mult))
                step1(pool.tensor_tensor(r2[:, 0, :], r2[:, 0, :], ss[:, 1, :], ALU.mult))
                step1(pool.tensor_scalar(r2[:, 0, :], r2[:, 0, :], 1.0 / D, EPS32, ALU.mult, ALU.add))
                step1(pool.tensor_tensor(r2[:, 1, :], r2[:, 0, :], half, ALU.pow))
                step1(pool.tensor_tensor(ra[:, :], r2[:, 1, :], r1[:, 1, :], ALU.mult))

            norm_factors(0)
            for b in range(NB):
                if b == 0:
                    for name in BEFORE:
                        split_lo(pool, name)
                for t in range(TT):
                    wait(pool, rope_vec, b, 3 * t + 3)
                    if b:
                        wait(pool, stack_lo, b - 1, 2 * TT)
                    pool.tensor_tensor(rot[:, t, :], rope_a[:, :], rope_b[:, :], ALU.add).then_inc(rope_pool.sem, 1)
                wait(pool, route_vec, b, 3 * TT)
                k = 0

                def step(ins):
                    nonlocal k
                    k += 1
                    ins.then_inc(route_pool.sem, 1)

                step(pool.tensor_tensor(dz[:, :, 0], top[:, :, 1], top[:, :, 0], ALU.subtract))
                step(pool.tensor_scalar(dz[:, :, 1], lg[:, :, E0], -1.0, None, ALU.mult))
                step(pool.tensor_copy(ixf[:, :, :], top_ix[:, :, :]))
                wait(pool, route_act, b, 1)
                step(pool.tensor_scalar(ez1[:, :, :], ez[:, :, :], 1.0, None, ALU.add))
                wait(pool, route_pool, b, k)
                step(pool.tensor_tensor(rc[:, :, :], ez1[:, :, :],
                                        powers[:, 1:2].unsqueeze(2).broadcast_to([P, TT, 2]), ALU.pow))
                wait(pool, route_pool, b, k)
                step(pool.tensor_tensor(w2nd[:, :], ez[:, :, 0], rc[:, :, 0], ALU.mult))
                wait(pool, route_pool, b, k)
                for t in range(TT):
                    step(pool.tensor_scalar(oh[:, t, 0, :], const("iota"), ixf[:, t, 0:1], rc[:, t, 0:1],
                                            ALU.is_equal, ALU.mult))
                    step(pool.tensor_scalar(oh[:, t, 1, :], const("iota"), ixf[:, t, 1:2], w2nd[:, t:t + 1],
                                            ALU.is_equal, ALU.mult))
                wait(pool, route_pool, b, k)
                step(pool.tensor_tensor(c9[:, :, 0:E0], oh[:, :, 0, :], oh[:, :, 1, :], ALU.add))
                step(pool.tensor_copy(c9[:, :, E0], rc[:, :, 1]))
                wait(pool, route_pool, b, k)
                if b:
                    wait(pool, cwT_pe, b - 1, 1)
                step(pool.tensor_copy(cw[:, :, 0:E0 + 1], c9[:, :, :]))
                wait(pool, route_pool, b, k)
                step(pool.tensor_tensor(cw[:, :, 16:16 + E0 + 1], c9[:, :, :], cw[:, :, 0:E0 + 1].bitcast(f32), ALU.subtract))
                assert k == route_pool.per, k
                for i in range(NT0):
                    if b in (0, NB - 1):
                        for name in (IN_SLOT if b == 0 else LAST_SLOT).get(i, []):
                            split_lo(pool, name)
                    if i == NORM_SLOT:
                        norm_factors(b + 1) if b + 1 < NB else norm1_factors(0)
                    m = tile_rows(i)
                    wait(pool, h_hi, b, i + 1)
                    pool.tensor_tensor(hT[0:m, i % 2, 1, :], hs[0:m, i % 2, :], hT[0:m, i % 2, 0, :].bitcast(f32),
                                       ALU.subtract).then_inc(h_lo.sem, 1)

            for b in range(NB):
                if b:
                    out_factors(b - 1)
                wait(pool, kd_hi, b, 1)
                pool.tensor_tensor(kd[:, 1, :], kdf, kd[:, 0, :].bitcast(f32), ALU.subtract).then_inc(kd_lo.sem, 1)
                wait(pool, route1_vec, b, 8)
                pool.tensor_scalar(ntop[:, :], top[:, :, 0], -1.0, None, ALU.mult).then_inc(route1_pool.sem, 1)
                pool.tensor_copy(ixf[:, :, :], top_ix[:, :, :]).then_inc(route1_pool.sem, 1)
                wait(pool, state_hi, b, 1)
                pool.tensor_tensor(state[:, 1, :, :].rearrange("p g n -> p (g n)"), stf, state[:, 0, :, :].rearrange("p g n -> p (g n)").bitcast(f32),
                                   ALU.subtract).then_inc(state_lo.sem, 1)

                def pad_queries(j):
                    t, g = divmod(j, 2)
                    if j >= 2:
                        wait(pool, ret_pe, b, 2 * (j - 1))
                    elif b:
                        wait(pool, ret_pe, b - 1, 8)
                    else:
                        wait(pool, dn_pe, NB - 1, NT0)
                    wait(pool, qk1_lo, b, 1)
                    pool.tensor_tensor(q_pad(j)[:, 1, :, :], qT1[:, 1, g, t * P:(t + 1) * P].bitcast(f32).unsqueeze(1).broadcast_to([P, 8, P]),
                                       const("block").unsqueeze(2).broadcast_to([P, 8, P]), ALU.mult).then_inc(pad_lo.sem, 1)

                pad_queries(0)
                pad_queries(1)
                for u in range(8):
                    wait(pool, ret_hi, b, u + 1)
                    pool.tensor_tensor(aT[:, u % 2, 1, :], af_at(u), aT[:, u % 2, 0, :].bitcast(f32), ALU.subtract).then_inc(ret_lo.sem, 1)
                    wait(pool, h1_hi, b, u + 1)
                    pool.tensor_tensor(hT[:, u % 2, 1, :], hs[:, u % 2, :], hT[:, u % 2, 0, :].bitcast(f32),
                                       ALU.subtract).then_inc(h1_lo.sem, 1)
                    if u in (2, 4):
                        pad_queries(u // 2 + 1)
                    if u == 3 and b + 1 < NB:
                        norm1_factors(b + 1)
            out_factors(NB - 1)

        @block.scalar
        def _(act):
            def tokens_hi(b):
                wait(act, xT_pe, b, 1)
                if b:
                    wait(act, gu_pe, b - 1, NT0)
                    wait(act, qkv_pe, b - 1, TT)
                act.activation(xT[:, 0, :, :], X[1][:, :].rearrange("p (k n) -> p k n", k=KT), ACT.Copy).then_inc(xT_hi.sem, 1)

            def tokens1_hi(b):
                wait(act, xT1_pe, b, 1)
                if b:
                    wait(act, gu1_pe, b - 1, NT1)
                    wait(act, route1_pe, b - 1, TT)
                else:
                    wait(act, gu_pe, NB - 1, NT0)
                act.activation(xT[:, 0, :, :], GU[0][:, :].rearrange("p (k n) -> p k n", k=KT), ACT.Copy).then_inc(xT1_hi.sem, 1)

            def qkv_tokens1_hi(b):
                wait(act, xT1_pe, b, 2)
                if b:
                    wait(act, kv1_pe, b - 1, TT)
                for k in range(KT):
                    act.activation(hT1[:, 0, k, :], GU[1][:, k * TOK:(k + 1) * TOK], ACT.Copy, scale=nwm[:, 0, k:k + 1]).then_inc(xT1_hi.sem, 1)

            def out_hi(b):
                wait(act, oT_pe, b, 1)
                for k in range(KT):
                    act.activation(oT[:, 0, k, :], X[2][:, k * TOK:(k + 1) * TOK], ACT.Copy, scale=nwm[:, 1, k:k + 1]).then_inc(oT_hi.sem, 1)

            for b in range(NB):
                if b == 0:
                    split_hi(act, "qkv")
                    act.wait_ge(prep_pe.sem, 1)
                    tokens_hi(0)
                    for name in BEFORE[1:]:
                        split_hi(act, name)

                def ternary_out(first):
                    for n in range(first, first + 2):
                        act.wait_ge(tern_pe.sem, 2 + n)
                        src = X[3 if n % 2 == 0 else 0][:, :].rearrange("p (r k c) -> p k r c", r=2, k=KT)
                        dst = (proj_t[:, :, :] if n == 3 else qkv_t[:, :, n * D:(n + 1) * D]).rearrange("p k (r c) -> p k r c", r=2)
                        wait(act, qkv_pe, b, TT)
                        act.activation(dst, src, ACT.Copy).then_inc(tern_act.sem, 1)

                if b == NB - 1:
                    ternary_out(0)
                for t in range(TT):
                    wait(act, rope_pool, b, t + 1)
                    if b:
                        wait(act, qkT_pe, b - 1, 5)
                        wait(act, yT_pe, b - 1, 1)
                        wait(act, wo_pe, b - 1, 1)
                    q4 = stack[:, t, 0:H * 64].rearrange("p (h r d) -> p h r d", h=H, r=4)
                    k4 = stack[:, t, H * 64:].rearrange("p (h r l d) -> p h r l d", h=HKV, r=2, l=2)
                    rq = rot[:, t, 0:H * DH].rearrange("p (h d) -> p h d", h=H).unsqueeze(2).broadcast_to([P, H, 2, DH])
                    rk = rot[:, t, H * DH:].rearrange("p (h d) -> p h d", h=HKV).unsqueeze(2).broadcast_to([P, HKV, 2, DH])
                    act.activation(q4[:, :, 0:2, :], rq, ACT.Copy).then_inc(stack_hi.sem, 1)
                    act.activation(k4[:, :, :, 0, :], rk, ACT.Copy).then_inc(stack_hi.sem, 1)
                if b == NB - 1:
                    ternary_out(2)
                wait(act, route_pool, b, 3)
                act.activation(ez[:, :, :], dz[:, :, :], ACT.Exp).then_inc(route_act.sem, 1)
                for n in range(4):
                    wait(act, qkT_pe, b, n + 1)
                    if n == 0 and b:
                        wait(act, score_pe, b - 1, 2 * NPAIR)
                    t, half = divmod(n, 2)
                    act.activation(qT[:, 4 * half:4 * half + 4, t * P:(t + 1) * P],
                                   X[3 if n % 2 == 0 else 0][:, :].rearrange("p (r n) -> p r n", r=4), ACT.Copy).then_inc(qkT_act.sem, 1)
                wait(act, qkT_pe, b, 5)
                for r in range(2):
                    rows = slice(64 * r, 64 * r + 64)
                    src = X[3][rows, :].rearrange("p (t g n) -> p g t n", t=TT, g=2)
                    dst = kTz[rows, :, r, :].rearrange("p g (t n) -> p g t n", t=TT)
                    act.activation(dst, src, ACT.Copy).then_inc(qkT_act.sem, 1)
                for i in range(NT0 + 1):
                    if b in (0, NB - 1):
                        for name in (IN_SLOT if b == 0 else LAST_SLOT).get(i, []):
                            split_hi(act, name)
                    if i == NT0 - 1 and b + 1 < NB:
                        tokens_hi(b + 1)
                    if i < NT0:
                        m = tile_rows(i)
                        wait(act, gu_pe, b, i + 1)
                        act.activation(th[0:m, i % 2, :], GU[i % 2][0:m, 0:TOK], ACT.Tanh, scale=0.5).then_inc(tanh_act.sem, 1)
                    if 2 <= i < 2 + NPAIR:
                        p = i - 2
                        wait(act, pT_pe, b, 2 * p + 1)
                        if p or b:
                            wait(act, pv_pe, b, p) if p else wait(act, pv_pe, b - 1, NPAIR)
                        act.activation(pT[:, 0, TOK:3 * TOK], X[2][:, :], ACT.Copy).then_inc(pT_hi.sem, 1)
                    if 1 <= i <= NT0:
                        j = i - 1
                        m = tile_rows(j)
                        wait(act, ffn_vec, b, 3 * j + 3)
                        if j >= 2:
                            wait(act, dn_pe, b, j - 1)
                        elif b:
                            wait(act, dn_pe, b - 1, NT0 - 1 + j)
                        act.activation(hT[0:m, j % 2, 0, :], hs[0:m, j % 2, :], ACT.Copy).then_inc(h_hi.sem, 1)
                    if 2 <= i < 2 + NPAIR:
                        p = i - 2
                        wait(act, pT_pe, b, 2 * p + 2)
                        act.activation(pT[:, 0, 0:TOK], X[2][:, 0:TOK], ACT.Copy).then_inc(pT_hi.sem, 1)
                    if 1 <= i < 1 + NPAIR:
                        p = i - 1
                        wait(act, max_vec, b, 5 * p + 5)
                        if p >= 2:
                            wait(act, pT_pe, b, 2 * (p - 1))
                        elif b:
                            wait(act, pT_pe, b - 1, 2 * (NPAIR - 1 + p))
                        for t in range(TT):
                            for r in range(2):
                                n = (t + 1) * P
                                at = r * P if t == 0 else TOK + r * TOK
                                k = 2 * t + r
                                act.activation(pm[:, p % 2, at:at + n], sm[:, at:at + n], ACT.Exp,
                                               bias=nmax[:, p % 2, k:k + 1], scale=DH ** -0.5,
                                               accum_out=rs[:, 4 * p + k:4 * p + k + 1]).then_inc(exp_act.sem, 1)
                    if i == 11:
                        wait(act, yT_pe, b, 1)
                        act.activation(yT[:, 0, :, :], X[0][:, :].rearrange("p (k n) -> p k n", k=KT), ACT.Copy).then_inc(yT_hi.sem, 1)
                    if b == 2 and i == 11:
                        act.wait_ge(decay_vec.sem, 1)
                        for n in range(2):
                            act.activation(lam[:, n, :], s_b[:, :], ACT.Exp, scale=const("tcol")[:, n:n + 1]).then_inc(decay_act.sem, 1)
                        for h in range(H):
                            act.activation(dm[:, h, :], const("decay")[:, 0:P], ACT.Exp, scale=ns_b[:, h:h + 1]).then_inc(decay_act.sem, 1)

            tokens1_hi(0)
            qkv_tokens1_hi(0)
            for b in range(NB):
                for n, dst in enumerate((qT1, kT1)):
                    wait(act, qk1_pe, b, n + 1)
                    if n == 0:
                        if b:
                            wait(act, ret_pe, b - 1, 8)
                            wait(act, pad_lo, b - 1, 4)
                            wait(act, pad_hi, b - 1, 4)
                        else:
                            wait(act, gu_pe, NB - 1, NT0)
                    act.activation(dst[:, 0, :, :], X[2 + n][:, :].rearrange("p (g n) -> p g n", g=2), ACT.Copy).then_inc(qk1_hi.sem, 1)
                for t in range(TT):
                    wait(act, kv1_pe, b, t + 1)
                    wait(act, kd_vec, b, 1)
                    if b:
                        wait(act, rv_pe, b - 1, 8)
                    else:
                        wait(act, dn_pe, NB - 1, NT0)
                    src = X[t][:, D:2 * D] if t == 0 else X[t][:, 0:D]
                    act.activation(v2[:, t, :, 0, :], src.rearrange("p (h d) -> p h d", h=H), ACT.Copy).then_inc(v1_hi.sem, 1)
                wait(act, kd_vec, b, 1)
                act.activation(kd[:, 0, :], kdf, ACT.Copy).then_inc(kd_hi.sem, 1)
                if b:
                    out_hi(b - 1)
                wait(act, route1_pool, b, 2)
                for t in range(TT):
                    act.activation(e1[:, t, :], lg1[:, t, :], ACT.Exp, bias=ntop[:, t:t + 1]).then_inc(route1_act.sem, 1)
                wait(act, state_vec, b, 1)
                act.activation(state[:, 0, :, :].rearrange("p g n -> p (g n)"), stf, ACT.Copy).then_inc(state_hi.sem, 1)
                for u in range(8):
                    wait(act, gu1_pe, b, u + 1)
                    if u >= 2:
                        wait(act, h1_lo, b, u - 1)
                    elif b:
                        wait(act, h1_lo, b - 1, NT1 - 1 + u)
                    if u < R1:
                        act.activation(th[:, u % 2, :], GU[u % 2][:, 0:TOK], ACT.Silu, bias=cols[:, u:u + 1]).then_inc(silu_act.sem, 1)
                    else:
                        act.activation(hs[:, u % 2, :], GU[u % 2][:, 0:TOK], ACT.Silu, bias=cols[:, 6 + u:7 + u]).then_inc(silu_act.sem, 1)
                    wait(act, ret_vec, b, u + 1)
                    if u >= 2:
                        wait(act, rv_pe, b, u - 1)
                    act.activation(aT[:, u % 2, 0, :], af_at(u), ACT.Copy).then_inc(ret_hi.sem, 1)
                    if u < R1:
                        wait(act, ffn1_vec, b, 2 * u + 2)
                    else:
                        wait(act, silu_act, b, u + 1)
                    if u >= 2:
                        wait(act, dn1_pe, b, u - 1)
                    elif b:
                        wait(act, dn1_pe, b - 1, NT1 - 1 + u)
                    else:
                        wait(act, dn_pe, NB - 1, NT0 - 1 + u)
                    act.activation(hT[:, u % 2, 0, :], hs[:, u % 2, :], ACT.Copy).then_inc(h1_hi.sem, 1)
                    if u == 7 and b + 1 < NB:
                        tokens1_hi(b + 1)
                        qkv_tokens1_hi(b + 1)
            out_hi(NB - 1)

        @block.vector
        def _(dve):
            def norm_stats(b, steps):
                for t in range(TT):
                    dve.bn_stats(st[:, t, :], x_all[:, b, t, :]).then_inc(steps.sem, 1)
                for t in range(TT):
                    wait(dve, steps, b, t + 1)
                    dve.bn_aggr(mv[:, t, :], st[:, t, :]).then_inc(steps.sem, 1)

            for rows in (slice(32, 64), slice(64, P)):
                dve.memset(spread[rows, :].bitcast(f32), 0.0).then_inc(prep_vec.sem, 1)
            dve.wait_ge(cst_in.sem, 16)
            def token_stats(b):
                dve.wait_ge(x_in[b].sem, 16)
                if b:
                    wait(dve, norm_vec, b - 1, TT)
                norm_stats(b, stats_vec)

            def normalise(b):
                wait(dve, rstd_pool, b, 2)
                if b:
                    wait(dve, xT_pe, b - 1, 1)
                for t in range(TT):
                    dve.tensor_scalar(xn[:, t, :], x_all[:, b, t, :], mv[:, t, 0:1], rstd[:, t:t + 1],
                                      ALU.subtract, ALU.mult).then_inc(norm_vec.sem, 1)

            def tokens_lo(b):
                wait(dve, xT_hi, b, 1)
                dve.tensor_tensor(xT[:, 1, :, :], X[1][:, :].rearrange("p (k n) -> p k n", k=KT),
                                  xT[:, 0, :, :].bitcast(f32), ALU.subtract).then_inc(xT_lo.sem, 1)

            def residual(b):
                wait(dve, dn_pe, b, NT0)
                wait(dve, wo_pe, b, 1)
                dve.tensor_tensor(x_all[:, b], x_all[:, b], OB[:, :].rearrange("p (t d) -> p t d", t=TT), ALU.add).then_inc(res_vec.sem, 1)

            def token_stats1(b):
                wait(dve, res_vec, b, 1)
                if b:
                    wait(dve, norm1_vec, b - 1, 2 * TT)
                else:
                    wait(dve, norm_vec, NB - 1, TT)
                norm_stats(b, stats1_vec)

            def normalise1(b):
                wait(dve, rstd1_pool, b, 2)
                if b:
                    wait(dve, xT1_pe, b - 1, 2)
                else:
                    wait(dve, xT_pe, NB - 1, 1)
                    wait(dve, yT_pe, NB - 1, 1)
                for t in range(TT):
                    dve.tensor_scalar(xn[:, t, :], x_all[:, b, t, :], mv[:, t, 0:1], rstd[:, t:t + 1],
                                      ALU.subtract, ALU.mult).then_inc(norm1_vec.sem, 1)
                wait(dve, rstd1_pool, b, 6)
                wait(dve, norm1_vec, b, TT)
                for t in range(TT):
                    dve.tensor_scalar(yn[:, t, :], xn[:, t, :], rh[:, t:t + 1], None, ALU.mult).then_inc(norm1_vec.sem, 1)

            def tokens1_lo(b):
                wait(dve, xT1_hi, b, 1)
                dve.tensor_tensor(xT[:, 1, :, :], GU[0][:, :].rearrange("p (k n) -> p k n", k=KT),
                                  xT[:, 0, :, :].bitcast(f32), ALU.subtract).then_inc(xT1_lo.sem, 1)
                for k in range(KT):
                    wait(dve, xT1_hi, b, 1 + KT)
                    dve.scalar_tensor_tensor(hT1[:, 1, k, :], GU[1][:, k * TOK:(k + 1) * TOK], nwm[:, 0, k:k + 1],
                                             hT1[:, 0, k, :].bitcast(f32), ALU.mult, ALU.subtract).then_inc(xT1_lo.sem, 1)

            def out_scaled(b):
                wait(dve, o_pool, b, 7)
                for t in range(TT):
                    dve.tensor_scalar(og[:, t, :], og[:, t, :], ra[:, t:t + 1], None, ALU.mult).then_inc(og_vec.sem, 1)

            def out_lo(b):
                for k in range(KT):
                    wait(dve, oT_hi, b, KT)
                    dve.scalar_tensor_tensor(oT[:, 1, k, :], X[2][:, k * TOK:(k + 1) * TOK], nwm[:, 1, k:k + 1],
                                             oT[:, 0, k, :].bitcast(f32), ALU.mult, ALU.subtract).then_inc(oT_lo.sem, 1)

            def residual1(b):
                wait(dve, proj_pe, b, 1)
                wait(dve, dn1_pe, b, NT1 + 1)
                dve.tensor_tensor(x_all[:, b], x_all[:, b], OB[:, :].rearrange("p (t d) -> p t d", t=TT), ALU.add).then_inc(res1_vec.sem, 1)

            token_stats(0)
            normalise(0)
            for b in range(NB):
                if b == 0:
                    dve.wait_ge(prep_pe.sem, 1)
                    dve.wait_ge(prep_pool.sem, PREP_POOL)
                    gsrc = X[3][:, 0:2 * 16].rearrange("p (k n) -> p k n", k=KT)[:, :, 0:GATES]
                    dve.tensor_copy(wqkv[:, 0, :, QKV:NQ], gsrc).then_inc(prep_vec.sem, 1)
                    dve.wait_ge(prep_vec.sem, PREP_VEC - 1)
                    dve.tensor_tensor(wqkv[:, 1, :, QKV:NQ], gsrc, wqkv[:, 0, :, QKV:NQ].bitcast(f32), ALU.subtract).then_inc(prep_vec.sem, 1)
                    tokens_lo(0)
                for t in range(TT):
                    wait(dve, qkv_pe, b, t + 1)
                    if t:
                        wait(dve, rope_pool, b, t)
                    elif b:
                        wait(dve, rope_pool, b - 1, TT)
                    n = H + HKV
                    half = DH // 2
                    qk = X[1 + t][:, 0:n * DH].rearrange("p (h s d) -> p h s d", h=n, s=2)
                    tab = const("rope").rearrange("p (t c d) -> p t c d", t=TT, c=3)
                    a = rope_a[:, :].rearrange("p (h d) -> p h d", h=2 * n)
                    bb = rope_b[:, :].rearrange("p (h s d) -> p h s d", h=n, s=2)
                    dve.tensor_tensor(a, X[1 + t][:, 0:n * DH].rearrange("p (h d) -> p h d", h=2 * n),
                                      tab[:, t, 0, :].unsqueeze(1).broadcast_to([P, 2 * n, half]), ALU.mult).then_inc(rope_vec.sem, 1)
                    for s in range(2):
                        dve.tensor_tensor(bb[:, :, s, :], qk[:, :, 1 - s, :],
                                          tab[:, t, 1 + s, :].unsqueeze(1).broadcast_to([P, n, half]), ALU.mult).then_inc(rope_vec.sem, 1)
                    if b:
                        wait(dve, pv_pe, b - 1, NPAIR)
                    vp = X[1 + t][:, H * DH + HKV * DH:QKV].rearrange("p (g d) -> p g d", g=HKV)
                    k = 5 * t
                    va, vb = (vr[:, m, :].rearrange("p (g d) -> p g d", g=HKV) for m in range(2))
                    dve.tensor_copy(v3[:, t, :, 0, :], vp).then_inc(v_vec.sem, 1)
                    dve.tensor_copy(lg[:, t, :], X[1 + t][:, QKV:NQ]).then_inc(route_vec.sem, 1)
                    wait(dve, v_vec, b, k + 1)
                    dve.tensor_tensor(va, vp, v3[:, t, :, 0, :], ALU.subtract).then_inc(v_vec.sem, 1)
                    wait(dve, route_vec, b, 3 * t + 1)
                    dve.max(top[:, t, :], lg[:, t, 0:8]).then_inc(route_vec.sem, 1)
                    wait(dve, v_vec, b, k + 2)
                    dve.tensor_copy(v3[:, t, :, 1, :], va).then_inc(v_vec.sem, 1)
                    wait(dve, route_vec, b, 3 * t + 2)
                    dve.max_index(top_ix[:, t, :], top[:, t, :], lg[:, t, 0:8]).then_inc(route_vec.sem, 1)
                    wait(dve, v_vec, b, k + 3)
                    dve.tensor_tensor(vb, va, v3[:, t, :, 1, :], ALU.subtract).then_inc(v_vec.sem, 1)
                    wait(dve, v_vec, b, k + 4)
                    dve.tensor_copy(v3[:, t, :, 2, :], vb).then_inc(v_vec.sem, 1)
                if b == 0:
                    dve.wait_ge(small_pe.sem, 1)
                    dve.tensor_copy(cols[:, :], X[3][:, 64:64 + 18]).then_inc(small_vec.sem, 1)
                    dve.wait_ge(small_in.sem, SMALL_IN)
                    dve.tensor_scalar(ns_b[:, :], s_b[:, :], -1.0, None, ALU.mult).then_inc(decay_vec.sem, 1)
                    dve.tensor_copy(bias_w[:, 0, :], bias_f[:, :]).then_inc(small_vec.sem, 1)
                    dve.wait_ge(small_vec.sem, 2)
                    dve.tensor_tensor(bias_w[:, 1, :], bias_f[:, :], bias_w[:, 0, :].bitcast(f32), ALU.subtract).then_inc(small_vec.sem, 1)
                if b:
                    residual(b - 1)
                if b == 2:
                    dve.wait_ge(tern_pe.sem, 1)
                    dve.tensor_copy(abs_sum[:, :], X[3][:, 0:3]).then_inc(tern_vec.sem, 1)
                    dve.wait_ge(tern_vec.sem, 4)
                    dve.tensor_tensor(w_mean[:, 0:1], abs_sum[:, 0:1], abs_sum[:, 1:2], ALU.add).then_inc(tern_vec.sem, 1)
                    dve.wait_ge(tern_vec.sem, 5)
                    dve.tensor_scalar(w_mean[:, 0:1], w_mean[:, 0:1], 1.0 / (3 * D * D), 1e-5, ALU.mult, ALU.max).then_inc(tern_vec.sem, 1)
                    dve.tensor_scalar(w_mean[:, 1:2], abs_sum[:, 2:3], 1.0 / (D * D), 1e-5, ALU.mult, ALU.max).then_inc(tern_vec.sem, 1)
                    dve.wait_ge(tern_vec.sem, 7)
                    dve.reciprocal(w_inv[:, :], w_mean[:, :]).then_inc(tern_vec.sem, 1)
                    for n in range(2):
                        dve.tensor_scalar(nwm[:, n, :], cols[:, 14 + 2 * n:16 + 2 * n], w_mean[:, n:n + 1], None, ALU.mult).then_inc(small_vec.sem, 1)
                if b == NB - 1:
                    dve.wait_ge(decay_act.sem, 2 + H)
                    dve.tensor_tensor(dm[:, :, :], dm[:, :, :], const("decay")[:, P:2 * P].unsqueeze(1).broadcast_to([P, H, P]), ALU.mult).then_inc(decay_vec.sem, 1)
                    dve.tensor_scalar(lam[:, 0, :], lam[:, 0, :], DH ** -0.5, None, ALU.mult).then_inc(decay_vec.sem, 1)
                for t in range(TT):
                    q4 = stack[:, t, 0:H * 64].rearrange("p (h r d) -> p h r d", h=H, r=4)
                    k4 = stack[:, t, H * 64:].rearrange("p (h r l d) -> p h r l d", h=HKV, r=2, l=2)
                    rq = rot[:, t, 0:H * DH].rearrange("p (h d) -> p h d", h=H).unsqueeze(2).broadcast_to([P, H, 2, DH])
                    rk = rot[:, t, H * DH:].rearrange("p (h d) -> p h d", h=HKV).unsqueeze(2).broadcast_to([P, HKV, 2, DH])
                    wait(dve, stack_hi, b, 2 * t + 2)
                    dve.tensor_tensor(q4[:, :, 2:4, :], rq, q4[:, :, 0:2, :].bitcast(f32), ALU.subtract).then_inc(stack_lo.sem, 1)
                    dve.tensor_tensor(k4[:, :, :, 1, :], rk, k4[:, :, :, 0, :].bitcast(f32), ALU.subtract).then_inc(stack_lo.sem, 1)
                wait(dve, cwT_pe, b, 1)
                if b:
                    wait(dve, cb_pe, b - 1, NT0)
                dve.tensor_copy(cwT[:, :], CB[:, 0:TOK]).then_inc(cwT_vec.sem, 1)
                for i in range(NT0):
                    if i == NORM_SLOT:
                        token_stats(b + 1) if b + 1 < NB else token_stats1(0)
                    if i == NT0 - 1 and b + 1 < NB:
                        tokens_lo(b + 1)
                    if 1 <= i < 1 + NPAIR:
                        p = i - 1
                        if p:
                            wait(dve, exp_act, b, 4 * p)
                        elif b:
                            wait(dve, exp_act, b - 1, 4 * NPAIR)
                        for t in range(TT):
                            wait(dve, score_pe, b, 2 * p + t + 1)
                            for r in range(2):
                                n = (t + 1) * P
                                at = r * P if t == 0 else TOK + r * TOK
                                dve.tensor_tensor_reduce(out=sm[:, at:at + n], in0=X[t][:, r * n:(r + 1) * n],
                                                         in1=const("mask")[:, 2 * P - n:2 * P], scale=1.0, scalar=-3.0e38,
                                                         op0=ALU.add, op1=ALU.max,
                                                         accum_out=mx[:, 2 * t + r:2 * t + r + 1]).then_inc(max_vec.sem, 1)
                        wait(dve, max_vec, b, 5 * p + 4)
                        dve.tensor_scalar(nmax[:, p % 2, :], mx[:, :], -(DH ** -0.5), None, ALU.mult).then_inc(max_vec.sem, 1)
                    if 2 <= i < 2 + NPAIR:
                        p = i - 2
                        wait(dve, pT_hi, b, 2 * p + 1)
                        dve.tensor_tensor(pT[:, 1, TOK:3 * TOK], X[2][:, :], pT[:, 0, TOK:3 * TOK], ALU.subtract).then_inc(pT_lo.sem, 1)
                    m = tile_rows(i)
                    wait(dve, tanh_act, b, i + 1)
                    dve.scalar_tensor_tensor(th[0:m, i % 2, :], th[0:m, i % 2, :], 1.0, GU[i % 2][0:m, 0:TOK],
                                         ALU.add, ALU.mult).then_inc(ffn_vec.sem, 1)
                    wait(dve, ffn_vec, b, 3 * i + 1)
                    dve.tensor_tensor(s2[0:m, i % 2, :], th[0:m, i % 2, :], GU[i % 2][0:m, TOK:2 * TOK], ALU.mult).then_inc(ffn_vec.sem, 1)
                    wait(dve, ffn_vec, b, 3 * i + 2)
                    wait(dve, cb_pe, b, i + 1)
                    if i >= 2:
                        wait(dve, h_lo, b, i - 1)
                    elif b:
                        wait(dve, h_lo, b - 1, NT0 - 1 + i)
                    dve.tensor_tensor(hs[0:m, i % 2, :], s2[0:m, i % 2, :], CB[0:m, 0:TOK], ALU.mult).then_inc(ffn_vec.sem, 1)
                    if 3 <= i < 3 + NPAIR:
                        p = i - 3
                        wait(dve, pv_pe, b, p + 1)
                        src = X[3][:, 0:4 * 3 * DH].rearrange("p (q j d) -> p q d j", q=4, j=3)
                        dve.tensor_reduce(y[:, p, :, :], src, AX.X, ALU.add).then_inc(y_vec.sem, 1)
                    if 2 <= i < 2 + NPAIR:
                        p = i - 2
                        wait(dve, pT_hi, b, 2 * p + 2)
                        dve.tensor_tensor(pT[:, 1, 0:TOK], X[2][:, 0:TOK], pT[:, 0, 0:TOK], ALU.subtract).then_inc(pT_lo.sem, 1)
                    if i == 10:
                        wait(dve, exp_act, b, 4 * NPAIR)
                        dve.reciprocal(rinv[:, :], rs[:, :]).then_inc(yn_vec.sem, 1)
                        wait(dve, yn_vec, b, 1)
                        wait(dve, y_vec, b, NPAIR)
                        for t in range(TT):
                            r4 = rinv[:, :].rearrange("p (q t r) -> p q t r", q=NPAIR, t=TT)
                            y5 = y[:, :, :, :].rearrange("p q (t r) d -> p q t r d", t=TT)
                            dve.tensor_tensor(yn[:, t, :].rearrange("p (q r d) -> p q r d", q=NPAIR, r=2), y5[:, :, t, :, :],
                                              r4[:, :, t, :].unsqueeze(3).broadcast_to([P, NPAIR, 2, DH]), ALU.mult).then_inc(yn_vec.sem, 1)
                    if i == 11:
                        wait(dve, yT_hi, b, 1)
                        dve.tensor_tensor(yT[:, 1, :, :], X[0][:, :].rearrange("p (k n) -> p k n", k=KT),
                                          yT[:, 0, :, :].bitcast(f32), ALU.subtract).then_inc(yT_lo.sem, 1)
                    if i == NORM_SLOT + 1:
                        normalise(b + 1) if b + 1 < NB else normalise1(0)
                    if b == 1 and 10 <= i < 13:
                        n = i - 10
                        slot, landed = pieces[f"tern{n}"][0:2]
                        dve.wait_ge(stage_in[slot].sem, landed)
                        dve.tensor_reduce(abs_sum[:, n:n + 1], stage[:, slot, 0:(3, 3, 2)[n] * D], AX.X, ALU.add,
                                          apply_absolute_value=True).then_inc(tern_vec.sem, 1)
                    if b == 2 and 10 <= i < 13:
                        n = i - 10
                        w = stage[:, slot_of[f"tern{n}"], 0:(3, 3, 2)[n] * D]
                        for k, (s1, s2_, *ops) in enumerate(((w_inv[:, n // 2:n // 2 + 1], 1.0, ALU.mult, ALU.min),
                                                            (-1.0, MAGIC, ALU.max, ALU.add), (-MAGIC, None, ALU.add))):
                            dve.wait_ge(tern_round.sem, 3 * n + k) if k else dve.wait_ge(tern_vec.sem, TERN_VEC)
                            dve.tensor_scalar(w, w, s1, s2_, *ops).then_inc(tern_round.sem, 1)

            tokens1_lo(0)
            residual(NB - 1)
            for b in range(NB):
                for n, dst in enumerate((qT1, kT1)):
                    wait(dve, qk1_hi, b, n + 1)
                    dve.tensor_tensor(dst[:, 1, :, :], X[2 + n][:, :].rearrange("p (g n) -> p g n", g=2),
                                      dst[:, 0, :, :].bitcast(f32), ALU.subtract).then_inc(qk1_lo.sem, 1)
                wait(dve, kv1_pe, b, 1)
                if b:
                    wait(dve, kd_lo, b - 1, 1)
                dve.tensor_tensor(kdf.rearrange("p (h d) -> p h d", h=H), X[0][:, 0:D].rearrange("p (h d) -> p h d", h=H),
                                  lam[:, 1, :].unsqueeze(2).broadcast_to([P, H, DH]), ALU.mult).then_inc(kd_vec.sem, 1)
                for t in range(TT):
                    wait(dve, v1_hi, b, t + 1)
                    src = X[t][:, D:2 * D] if t == 0 else X[t][:, 0:D]
                    dve.tensor_tensor(v2[:, t, :, 1, :], src.rearrange("p (h d) -> p h d", h=H), v2[:, t, :, 0, :].bitcast(f32),
                                      ALU.subtract).then_inc(v1_lo.sem, 1)
                if b:
                    out_scaled(b - 1)
                k = 0

                def rstep(ins):
                    nonlocal k
                    k += 1
                    ins.then_inc(route1_vec.sem, 1)

                for t in range(TT):
                    wait(dve, route1_pe, b, t + 1)
                    rstep(dve.tensor_tensor(lg1[:, t, :], CB[:, 16 * t:16 * t + 8], bg_b[:, :], ALU.add))
                wait(dve, route1_vec, b, k)
                for t in range(TT):
                    rstep(dve.tensor_tensor(lg1[:, t, :], CB[:, 16 * t + 8:16 * t + 16], lg1[:, t, :], ALU.add))
                wait(dve, route1_vec, b, k)
                for t in range(TT):
                    rstep(dve.max(top[:, t, :], lg1[:, t, :]))
                wait(dve, route1_vec, b, k)
                for t in range(TT):
                    rstep(dve.max_index(top_ix[:, t, :], top[:, t, :], lg1[:, t, :]))
                if b:
                    out_lo(b - 1)
                wait(dve, route1_pool, b, 2)
                for n in range(2):
                    for t in range(TT):
                        wait(dve, route1_act, b, t + 1)
                        rstep(dve.scalar_tensor_tensor(em[:, n, t, :], const("iota"), ixf[:, t, 6 + n:7 + n], e1[:, t, :] if n == 0 else em[:, 0, t, :],
                                                       ALU.not_equal, ALU.mult))
                    wait(dve, route1_vec, b, k)
                rstep(dve.tensor_reduce(esum[:, :], em[:, 1, :, :], AX.X, ALU.add))
                wait(dve, route1_vec, b, k)
                rstep(dve.reciprocal(erec[:, :], esum[:, :]))
                wait(dve, route1_vec, b, k)
                rstep(dve.tensor_tensor(c1[:, :, 0:R1], em[:, 1, :, 0:R1], erec[:, :].unsqueeze(2).broadcast_to([P, TT, R1]), ALU.mult))
                wait(dve, route1_vec, b, k)
                if b:
                    wait(dve, cw1_pe, b - 1, 1)
                rstep(dve.tensor_copy(cw[:, :, 0:R1], c1[:, :, 0:R1]))
                wait(dve, route1_vec, b, k)
                rstep(dve.tensor_tensor(cw[:, :, 16:16 + R1], c1[:, :, 0:R1], cw[:, :, 0:R1].bitcast(f32), ALU.subtract))
                assert k == route1_vec.per, k
                if b == 0:
                    dve.memset(cw[:, :, R1:R1 + 1].bitcast(f32), 1.0).then_inc(small_vec.sem, 1)
                wait(dve, state_pe, b, 1)
                if b:
                    wait(dve, state_lo, b - 1, 1)
                dve.tensor_tensor(stf.rearrange("p (g h d) -> p g h d", g=2, h=8), X[0][:, 0:2 * P].rearrange("p (g h d) -> p g h d", g=2, h=8),
                                  const("block").unsqueeze(1).unsqueeze(3).broadcast_to([P, 2, 8, DH]), ALU.mult).then_inc(state_vec.sem, 1)
                if b:
                    residual1(b - 1)
                wait(dve, cw1_pe, b, 1)
                if b:
                    wait(dve, cb1_pe, b - 1, R1)
                    wait(dve, dn1_pe, b - 1, NT1 + 1)
                dve.tensor_copy(cwT[:, :], CB[:, 0:TOK]).then_inc(cw1_vec.sem, 1)

                def pad_queries(j):
                    t, g = divmod(j, 2)
                    if j >= 2:
                        wait(dve, ret_pe, b, 2 * (j - 1))
                    else:
                        wait(dve, qk1_hi, b, 1)
                    dve.tensor_tensor(q_pad(j)[:, 0, :, :], qT1[:, 0, g, t * P:(t + 1) * P].bitcast(f32).unsqueeze(1).broadcast_to([P, 8, P]),
                                      const("block").unsqueeze(2).broadcast_to([P, 8, P]), ALU.mult).then_inc(pad_hi.sem, 1)

                pad_queries(0)
                pad_queries(1)
                wait(dve, cross_pe, b, 1)
                dve.tensor_tensor(cross.rearrange("p (h d) -> p h d", h=H), X[1][:, 0:D].rearrange("p (h d) -> p h d", h=H),
                                  lam[:, 0, :].unsqueeze(2).broadcast_to([P, H, DH]), ALU.mult).then_inc(cross_vec.sem, 1)
                for u in range(8):
                    if u < R1:
                        wait(dve, silu_act, b, u + 1)
                        dve.scalar_tensor_tensor(s2[:, u % 2, :], GU[u % 2][:, TOK:2 * TOK], cols[:, 6 + u:7 + u], th[:, u % 2, :],
                                                 ALU.add, ALU.mult).then_inc(ffn1_vec.sem, 1)
                    wait(dve, ret_pe, b, u + 1)
                    if u >= 2:
                        wait(dve, ret_lo, b, u - 1)
                    elif b:
                        wait(dve, ret_lo, b - 1, 7 + u)
                    h0 = (u // 2 % 2) * 8 + (u % 2) * 4
                    dve.tensor_tensor(af_at(u).rearrange("p (h n) -> p h n", h=4), X[u % 2][:, :].rearrange("p (h n) -> p h n", h=4),
                                      dm[:, h0:h0 + 4, :], ALU.mult).then_inc(ret_vec.sem, 1)
                    if u < R1:
                        wait(dve, ffn1_vec, b, 2 * u + 1)
                        wait(dve, cb1_pe, b, u + 1)
                        if u >= 2:
                            wait(dve, h1_lo, b, u - 1)
                        elif b:
                            wait(dve, h1_lo, b - 1, NT1 - 1 + u)
                        else:
                            wait(dve, h_lo, NB - 1, NT0 - 1 + u)
                        dve.tensor_tensor(hs[:, u % 2, :], s2[:, u % 2, :], CB[:, 0:TOK], ALU.mult).then_inc(ffn1_vec.sem, 1)
                    if u in (2, 4):
                        pad_queries(u // 2 + 1)
                    if b + 1 < NB:
                        if u == 2:
                            token_stats1(b + 1)
                        elif u == 4:
                            normalise1(b + 1)
                        elif u == 7:
                            tokens1_lo(b + 1)
                wait(dve, rv_pe, b, 8)
                for t in range(TT):
                    dve.tensor_reduce(o_tok[:, t, :].rearrange("p (h d) -> p h d", h=H),
                                      X[2 + t][:, :].rearrange("p (h l d) -> p h d l", h=H, l=2), AX.X, ALU.add).then_inc(o_vec.sem, 1)
                wait(dve, o_vec, b, 2)
                dve.tensor_tensor(o_tok[:, 1, :], o_tok[:, 1, :], cross, ALU.add).then_inc(o_vec.sem, 1)
                wait(dve, o_vec, b, 3)
                if b:
                    wait(dve, oT_pe, b - 1, 1)
                for t in range(TT):
                    dve.tensor_tensor(og[:, t, :], o_tok[:, t, :], nw_b[:, :], ALU.mult).then_inc(o_vec.sem, 1)
                for t in range(TT):
                    dve.tensor_tensor_reduce(out=sq, in0=o_tok[:, t, :], in1=o_tok[:, t, :], scale=1.0, scalar=0.0,
                                             op0=ALU.mult, op1=ALU.add, accum_out=ss[:, 0, t:t + 1]).then_inc(o_vec.sem, 1)
                    wait(dve, o_vec, b, 3 + TT + 2 * t + 1)
                    dve.tensor_tensor_reduce(out=sq, in0=og[:, t, :], in1=og[:, t, :], scale=1.0, scalar=0.0,
                                             op0=ALU.mult, op1=ALU.add, accum_out=ss[:, 1, t:t + 1]).then_inc(o_vec.sem, 1)
                    wait(dve, o_vec, b, 3 + TT + 2 * t + 2)
            out_scaled(NB - 1)
            out_lo(NB - 1)
            residual1(NB - 1)

        @block.tensor
        def _(pe):
            PASSES = ((0, 0), (1, 0), (0, 1))
            pe.wait_ge(cst_in.sem, 16)
            pe.wait_ge(gates_in.sem, 48)
            for k in range(KT):
                mm = pe.transpose(X[3][:, 16 * k:16 * k + GATES], gates_nat[:, k * P:(k + 1) * P], ident[0:GATES, 0:GATES])
            mm.then_inc(prep_pe.sem, 1)

            opened = [False]

            def add_to_out(t, lhsT, rhs):
                mm = pe.matmul(OB[:, t * D:(t + 1) * D], lhsT, rhs, start=not opened[0], stop=True,
                               skip_group_check=opened[0])
                opened[0] = True
                return mm

            def transpose_tokens(b):
                wait(pe, norm_vec, b, TT)
                if b:
                    wait(pe, max_vec, b - 1, 5 * NPAIR)
                for k in range(KT):
                    for t in range(TT):
                        mm = pe.transpose(X[1][:, k * TOK + t * P:k * TOK + (t + 1) * P], xn[:, t, k * P:(k + 1) * P], ident)
                mm.then_inc(xT_pe.sem, 1)

            def down(b, i):
                m = tile_rows(i)
                if i == 0:
                    opened[0] = False
                wait(pe, h_lo, b, i + 1)
                if b == 0:
                    weights_ready(pe, *dn_needs(i))
                elif i == 0:
                    wait(pe, res_vec, b - 1, 1)
                for t in range(TT):
                    for l, r in PASSES:
                        mm = add_to_out(t, hT[0:m, i % 2, l, t * P:(t + 1) * P], dn_w[0:m, i, r, :])
                mm.then_inc(dn_pe.sem, 1)

            transpose_tokens(0)
            for b in range(NB):
                wait(pe, xT_lo, b, 1)
                if b == 0:
                    weights_ready(pe, "qkv")
                    pe.wait_ge(prep_vec.sem, PREP_VEC)
                else:
                    wait(pe, pT_lo, b - 1, 2 * NPAIR)
                    wait(pe, max_vec, b - 1, 5 * NPAIR)
                for t in range(TT):
                    for n, (l, r) in enumerate((PASSES[m][0], PASSES[m][1]) for m in range(3)):
                        for k in range(KT):
                            mm = pe.matmul(X[1 + t][:, 0:NQ], xT[:, l, k, t * P:(t + 1) * P], wqkv[:, r, k, :],
                                           start=(n == 0 and k == 0), stop=(n == 2 and k == KT - 1))
                    mm.then_inc(qkv_pe.sem, 1)

                if b == 0:
                    pe.wait_ge(small_in.sem, SMALL_IN)
                    pe.transpose(X[3][:, 64:64 + 18], small_rows[:, :], ident[0:18, 0:18]).then_inc(small_pe.sem, 1)
                if b:
                    down(b - 1, NT0 - 1)

                def transpose_ternary(first):
                    pe.wait_ge(tern_round.sem, TERN_ROUND)
                    wait(pe, y_vec, b - 1, NPAIR)
                    for n in range(first, first + 2):
                        if n >= 2:
                            pe.wait_ge(tern_act.sem, n - 1)
                        for m in range(4):
                            r, k = divmod(m, 2)
                            r += 2 * (n % 3)
                            name, row = ("tern2", r) if n == 3 else (f"tern{r // 3}", r % 3)
                            mm = pe.transpose(X[3 if n % 2 == 0 else 0][:, m * P:(m + 1) * P],
                                              stage[:, slot_of[name], row * D + k * P:row * D + (k + 1) * P], ident)
                        mm.then_inc(tern_pe.sem, 1)

                def gate_up(i):
                    m = tile_rows(i)
                    if b == 0:
                        weights_ready(pe, *gu_needs(i))
                    if i >= 2:
                        wait(pe, ffn_vec, b, 3 * (i - 2) + 2)
                    elif b:
                        wait(pe, ffn_vec, b - 1, 3 * (NT0 - 2 + i) + 2)
                    for g in range(2):
                        for n, (l, r) in enumerate(PASSES):
                            for k in range(KT):
                                mm = pe.matmul(GU[i % 2][0:m, g * TOK:(g + 1) * TOK], gu_w[:, i, l, 2 * g + k, 0:m], xT[:, r, k, :],
                                               start=(n == 0 and k == 0), stop=(n == 2 and k == KT - 1))
                    mm.then_inc(gu_pe.sem, 1)

                def spread_weights(i):
                    m = tile_rows(i)
                    wait(pe, cwT_vec, b, 1)
                    if b == 0:
                        pe.wait_ge(w_hi.sem, need[f"sp{i * P // 768}"][0])
                    if i:
                        wait(pe, ffn_vec, b, 3 * i)
                    pe.matmul(CB[0:m, 0:TOK], spread[:, i * P:i * P + m], cwT[:, :], start=True, stop=True).then_inc(cb_pe.sem, 1)

                def scores(p):
                    gp = p // 4
                    if p:
                        wait(pe, max_vec, b, 5 * (p - 1) + 4)
                    for t in range(TT):
                        n = (t + 1) * P
                        pe.matmul(X[t][:, 0:2 * n], qT[:, p, t * P:(t + 1) * P], kTz[:, gp, :, 0:n],
                                  start=True, stop=True).then_inc(score_pe.sem, 1)

                def prob_transposes(p, t):
                    if t == 1:
                        wait(pe, exp_act, b, 4 * p + 4)
                        if p:
                            wait(pe, pT_lo, b, 2 * p)
                    else:
                        wait(pe, pT_lo, b, 2 * p + 1)
                    n = 0
                    for r in range(2):
                        for s in range(t + 1):
                            at = (r * P if t == 0 else TOK + r * TOK) + s * P
                            mm = pe.transpose(X[2][:, n * P:(n + 1) * P], pm[:, p % 2, at:at + P], ident)
                            n += 1
                    mm.then_inc(pT_pe.sem, 1)

                def prob_values(p):
                    gp = p // 4
                    wait(pe, pT_lo, b, 2 * p + 2)
                    if p:
                        wait(pe, y_vec, b, p)
                    first = True
                    for t in range(TT):
                        for r in range(2):
                            q = 2 * t + r
                            o = X[3][:, q * 3 * DH:(q + 1) * 3 * DH]
                            for s in range(t + 1):
                                at = (r * P if t == 0 else TOK + r * TOK) + s * P
                                vv = v3[:, s, 2 * gp + r, :, :].rearrange("p j d -> p (j d)")
                                for l in range(2):
                                    mm = pe.matmul(o, pT[:, l, at:at + P], vv, start=first, stop=True, skip_group_check=not first)
                                    first = False
                    mm.then_inc(pv_pe.sem, 1)

                if b == NB - 1:
                    transpose_ternary(0)
                gate_up(0)
                if b == NB - 1:
                    transpose_ternary(2)
                    pe.wait_ge(tern_act.sem, 4)
                gate_up(1)
                wait(pe, stack_lo, b, 2 * TT)
                if b:
                    wait(pe, y_vec, b - 1, NPAIR)
                else:
                    pe.wait_ge(prep_vec.sem, PREP_VEC)
                    pe.wait_ge(small_vec.sem, 1)
                if b == 2:
                    pe.wait_ge(tern_vec.sem, 4)
                for n in range(4):
                    t, half = divmod(n, 2)
                    if n >= 2:
                        wait(pe, qkT_act, b, n - 1)
                    for m in range(4):
                        at = (4 * half + m) * P
                        mm = pe.transpose(X[3 if n % 2 == 0 else 0][:, m * P:(m + 1) * P], stack[:, t, at:at + P].bitcast(f32), ident)
                    mm.then_inc(qkT_pe.sem, 1)
                wait(pe, qkT_act, b, 3)
                for t in range(TT):
                    for g in range(2):
                        at = H * 64 + g * P
                        mm = pe.transpose(X[3][:, (2 * t + g) * P:(2 * t + g + 1) * P], stack[:, t, at:at + P].bitcast(f32), ident)
                mm.then_inc(qkT_pe.sem, 1)
                wait(pe, route_pool, b, route_pool.per)
                if b:
                    wait(pe, ffn_vec, b - 1, 3 * NT0)
                else:
                    pe.wait_ge(prep_pool.sem, PREP_POOL)
                for t in range(TT):
                    mm = pe.transpose(CB[:, t * P:(t + 1) * P], cw[:, t, :].bitcast(f32), ident)
                mm.then_inc(cwT_pe.sem, 1)
                wait(pe, qkT_act, b, 6)
                wait(pe, v_vec, b, 5 * TT)
                wait(pe, rope_vec, b, 3 * TT)
                wait(pe, route_vec, b, 3 * TT)
                for i in range(NT0):
                    if 1 <= i < 1 + NPAIR:
                        scores(i - 1)
                    if 2 <= i < 2 + NPAIR:
                        prob_transposes(i - 2, 1)
                    spread_weights(i)
                    if i + 1 < NT0 and i:
                        gate_up(i + 1)
                    if 2 <= i < 2 + NPAIR:
                        prob_transposes(i - 2, 0)
                    if i == 11:
                        wait(pe, yn_vec, b, 1 + TT)
                        for k in range(KT):
                            for t in range(TT):
                                mm = pe.transpose(X[0][:, k * TOK + t * P:k * TOK + (t + 1) * P], yn[:, t, k * P:(k + 1) * P], ident)
                        mm.then_inc(yT_pe.sem, 1)
                    if i == 12 and b + 1 < NB:
                        transpose_tokens(b + 1)
                    if i >= 1:
                        down(b, i - 1)
                    if 2 <= i < 2 + NPAIR:
                        prob_values(i - 2)
                    if i == 12 and b == 1:
                        pe.wait_ge(tern_vec.sem, 3)
                        wait(pe, y_vec, b, NPAIR)
                        pe.matmul(X[3][:, 0:3], ones[:, :], abs_sum[:, :], start=True, stop=True).then_inc(tern_pe.sem, 1)
                wait(pe, yT_lo, b, 1)
                if b == 0:
                    weights_ready(pe, "wo")
                for t in range(TT):
                    for l, r in PASSES:
                        for k in range(KT):
                            mm = add_to_out(t, yT[:, l, k, t * P:(t + 1) * P], wo_r[:, r, k, :])
                mm.then_inc(wo_pe.sem, 1)

            HALVES = (0, 1)

            def transpose_tokens1(b, k1):
                wait(pe, norm1_vec, b, (k1 + 1) * TT)
                if b:
                    wait(pe, silu_act, b - 1, NT1 - 1 + k1)
                else:
                    wait(pe, ffn_vec, NB - 1, 3 * (NT0 - 2 + k1) + 2)
                src = (xn, yn)[k1]
                for k in range(KT):
                    for t in range(TT):
                        mm = pe.transpose(GU[k1][:, k * TOK + t * P:k * TOK + (t + 1) * P], src[:, t, k * P:(k + 1) * P], ident)
                mm.then_inc(xT1_pe.sem, 1)

            def project(b, half):
                if half == 0:
                    wait(pe, og_vec, b, TT)
                    for k in range(KT):
                        for t in range(TT):
                            mm = pe.transpose(X[2][:, k * TOK + t * P:k * TOK + (t + 1) * P], og[:, t, k * P:(k + 1) * P], ident)
                    mm.then_inc(oT_pe.sem, 1)
                else:
                    wait(pe, oT_lo, b, KT)
                    for t in range(TT):
                        for l in HALVES:
                            for k in range(KT):
                                mm = add_to_out(t, oT[:, l, k, t * P:(t + 1) * P], proj_t[:, k, :])
                    mm.then_inc(proj_pe.sem, 1)

            transpose_tokens1(0, 0)
            transpose_tokens1(0, 1)
            down(NB - 1, NT0 - 1)
            for b in range(NB):
                def gate_up(i):
                    if i < 2:
                        wait(pe, xT1_lo, b, 1 if i == 0 else 1 + KT)
                    if b == 0:
                        weights_ready(pe, f"x{i}" if i < R1 else "xup")
                    if i >= 2:
                        wait(pe, ffn1_vec, b, 2 * (i - 2) + 1)
                    for g in range(2 if i < R1 else 1):
                        for n, (l, r) in enumerate(PASSES):
                            for k in range(KT):
                                w = gu1_w(i)[:, l, 2 * g + k, :] if i < R1 else up1_w(i - R1)[:, l, k, :]
                                mm = pe.matmul(GU[i % 2][:, g * TOK:(g + 1) * TOK], w, xT[:, r, k, :],
                                               start=(n == 0 and k == 0), stop=(n == 2 and k == KT - 1))
                    mm.then_inc(gu1_pe.sem, 1)

                gate_up(0)
                if b:
                    wait(pe, ffn1_vec, b - 1, 2 * R1)
                else:
                    wait(pe, ffn_vec, NB - 1, 3 * NT0)
                    weights_ready(pe, "router")
                for t in range(TT):
                    for m, (l, k) in enumerate((l, k) for l in HALVES for k in range(KT)):
                        mm = pe.matmul(CB[:, 16 * t:16 * t + 16], xT[:, l, k, t * P:(t + 1) * P], router_w[:, k, :, :].rearrange("p l n -> p (l n)"),
                                       start=m == 0, stop=m == 3)
                    mm.then_inc(route1_pe.sem, 1)
                wait(pe, xT1_lo, b, 1 + KT)
                if b:
                    wait(pe, o_vec, b - 1, 2)
                else:
                    wait(pe, y_vec, NB - 1, NPAIR)
                for n in range(2):
                    for g in range(2):
                        for m, (l, k) in enumerate((l, k) for l in HALVES for k in range(KT)):
                            mm = pe.matmul(X[2 + n][:, g * TOK:(g + 1) * TOK], qkv_t[:, k, n * D + g * P:n * D + (g + 1) * P], hT1[:, l, k, :],
                                           start=m == 0, stop=m == 3)
                    mm.then_inc(qk1_pe.sem, 1)
                if b:
                    wait(pe, ret_vec, b - 1, 8)
                for t in range(TT):
                    c0, n = (D, 2 * D) if t == 0 else (2 * D, D)
                    for m, (l, k) in enumerate((l, k) for l in HALVES for k in range(KT)):
                        mm = pe.matmul(X[t][:, 0:n], hT1[:, l, k, t * P:(t + 1) * P], qkv_t[:, k, c0:c0 + n], start=m == 0, stop=m == 3)
                    mm.then_inc(kv1_pe.sem, 1)

                def spread_weights(i):
                    wait(pe, cw1_vec, b, 1)
                    if b == 0:
                        pe.wait_ge(w_hi.sem, need["sp3"][0])
                    if i:
                        wait(pe, ffn1_vec, b, 2 * i)
                    pe.matmul(CB[:, 0:TOK], spread[:, NT0 * P + i * P:NT0 * P + (i + 1) * P], cwT[:, :], start=True, stop=True).then_inc(cb1_pe.sem, 1)

                def down1(i):
                    wait(pe, h1_lo, b, i + 1)
                    if b == 0:
                        weights_ready(pe, f"x{i}" if i < R1 else "xdn")
                        if i == 0:
                            wait(pe, res_vec, NB - 1, 1)
                    elif i == 0:
                        wait(pe, res1_vec, b - 1, 1)
                    if i == 0:
                        opened[0] = False
                    for t in range(TT):
                        for l, r in PASSES:
                            mm = add_to_out(t, hT[:, i % 2, l, t * P:(t + 1) * P], dn1_w(i)[:, r, :])
                    mm.then_inc(dn1_pe.sem, 1)

                def retention_scores(u):
                    t, g, half = u // 4, u // 2 % 2, u % 2
                    wait(pe, pad_hi, b, u // 2 + 1)
                    wait(pe, pad_lo, b, u // 2 + 1)
                    wait(pe, qk1_lo, b, 2)
                    if u >= 2:
                        wait(pe, ret_vec, b, u - 1)
                    for m, (l, r) in enumerate(PASSES):
                        mm = pe.matmul(X[u % 2][:, :], kT1[:, l, g, t * P:(t + 1) * P], q_pad(u // 2)[:, r, 4 * half:4 * half + 4, :],
                                       start=m == 0, stop=m == 2)
                    mm.then_inc(ret_pe.sem, 1)

                def retention_values(u):
                    t = u // 4
                    h0 = (u // 2 % 2) * 8 + (u % 2) * 4
                    wait(pe, ret_lo, b, u + 1)
                    for hh in range(4):
                        h = h0 + hh
                        for l in HALVES:
                            first = u % 4 == 0 and hh == 0 and l == 0
                            mm = pe.matmul(X[2 + t][:, 2 * DH * h:2 * DH * (h + 1)], aT[:, u % 2, l, hh * P:(hh + 1) * P],
                                           v2[:, t, h, :, :].rearrange("p l d -> p (l d)"), start=first, stop=True, skip_group_check=not first)
                    mm.then_inc(rv_pe.sem, 1)

                gate_up(1)
                if b:
                    wait(pe, qk1_lo, b, 1)
                    project(b - 1, 0)
                wait(pe, kd_lo, b, 1)
                wait(pe, v1_lo, b, TT)
                for g in range(2):
                    for m, (l, r) in enumerate(PASSES):
                        mm = pe.matmul(X[0][:, g * P:(g + 1) * P], kd[:, l, g * P:(g + 1) * P], v2[:, 0, 8 * g:8 * g + 8, r, :],
                                       start=m == 0, stop=m == 2)
                mm.then_inc(state_pe.sem, 1)
                if b:
                    project(b - 1, 1)
                wait(pe, route1_vec, b, route1_vec.per)
                if b == 0:
                    pe.wait_ge(small_vec.sem, 6)
                for t in range(TT):
                    mm = pe.transpose(CB[:, t * P:(t + 1) * P], cw[:, t, :].bitcast(f32), ident)
                mm.then_inc(cw1_pe.sem, 1)
                wait(pe, state_lo, b, 1)
                wait(pe, qk1_lo, b, 2)
                for g in range(2):
                    for m, (l, r) in enumerate(PASSES):
                        mm = pe.matmul(X[1][:, g * P:(g + 1) * P], qT1[:, l, g, P:2 * P], state[:, r, g, :], start=m == 0, stop=m == 2)
                mm.then_inc(cross_pe.sem, 1)
                for u in range(8):
                    if u == 1:
                        wait(pe, cross_vec, b, 1)
                    retention_scores(u)
                    if u < R1:
                        spread_weights(u)
                    if u:
                        retention_values(u - 1)
                        down1(u - 1)
                    if u + 2 < NT1:
                        gate_up(u + 2)
                if b + 1 < NB:
                    transpose_tokens1(b + 1, 0)
                retention_values(7)
                if b + 1 < NB:
                    transpose_tokens1(b + 1, 1)
                down1(7)
                for t in range(TT):
                    for r in HALVES:
                        mm = add_to_out(t, cwT[:, t * P:(t + 1) * P], bias_w[:, r, :])
                mm.then_inc(dn1_pe.sem, 1)
            project(NB - 1, 0)
            project(NB - 1, 1)


_INS = ['L0_attn_x', 'L0_attn_Wq', 'L0_attn_Wk', 'L0_attn_Wv', 'L0_attn_Wo', 'L0_ffn_gate_w', 'L0_ffn_w_gate',
        'L0_ffn_w_up', 'L0_ffn_w_down', 'L0_ffn_shgate_w', 'L0_ffn_shw_gate', 'L0_ffn_shw_up', 'L0_ffn_shw_down',
        'L1_attn_qkv_w', 'L1_attn_qkv_norm_w', 'L1_attn_proj_w', 'L1_attn_proj_norm_w', 'L1_attn_norm_w',
        'L1_attn_s', 'L1_ffn_Wg', 'L1_ffn_bg', 'L1_ffn_Wgate', 'L1_ffn_bgate', 'L1_ffn_Wup', 'L1_ffn_bup',
        'L1_ffn_Wdown', 'L1_ffn_bdown', 'L1_ffn_Ws_up', 'L1_ffn_bs_up', 'L1_ffn_Ws_down', 'L1_ffn_bs_down']
_OUTS = [((4, 256, 256), 'float32')]


def kernel(**inputs):
    import numpy as _np
    import concourse.bacc as _bacc
    from concourse import mybir as _mybir
    from concourse.bass_utils import run_bass_kernel_spmd as _run

    nc = _bacc.Bacc("TRN2", target_bir_lowering=False, num_devices=1)
    consts, spread = constants()
    named = [(name, inputs[name]) for name in _INS] + [("consts", consts), ("spread", spread)]
    arrays, args = {}, []
    for name, a in named:
        a = _np.ascontiguousarray(a)
        arrays[f"in_{name}_dram"] = a
        args.append(nc.dram_tensor(f"in_{name}_dram", a.shape, _mybir.dt.from_np(a.dtype), kind="ExternalInput").ap())
    for i, (shape, dtype) in enumerate(_OUTS):
        dt = _mybir.dt.from_np(_np.dtype(dtype))
        args.append(nc.dram_tensor(f"out_{i}_dram", shape, dt, kind="ExternalOutput").ap())
    bass_two_layer_kernel(nc, *args)
    r = _run(nc, [arrays], core_ids=[0])
    got = tuple(r.results[0][f"out_{i}_dram"] for i in range(len(_OUTS)))
    return got[0]
```

```python
import concourse.bass as bass
from concourse import mybir
from contextlib import ExitStack

import numpy as np

P = 128
NB, TOK, D = 4, 256, 256
TT = TOK // P
KT = D // P
H, HKV, DH = 16, 4, 16
QKV = H * DH + 2 * HKV * DH
E0, HE0, HS0 = 8, 176, 352
HID0 = E0 * HE0 + HS0
NT0 = -(-HID0 // P)
GATES = E0 + 2
NQ = QKV + GATES
E1, R1, H1, HS1 = 8, 6, 128, 256
NT1 = R1 + HS1 // P
NPAIR = H // 2
CAUSAL = -1.0e30
TILE_W = 1024
D0_AT = NT0 * TILE_W


def tile_rows(i):
    return min(P, HID0 - i * P)


CONSTS = {}
_at = 0
for _name, _n in (("ident", P), ("rope", TT * 3 * 8), ("mask", 2 * P), ("decay", 2 * P), ("block", 8),
                  ("iota", 8), ("tcol", 2)):
    CONSTS[_name] = (_at, _n)
    _at += _n
CONST_W = _at


def constants():
    c = np.zeros((P, CONST_W), np.float32)

    def put(name, a):
        at, n = CONSTS[name]
        c[:, at:at + n] = np.asarray(a, np.float32).reshape(P, n)

    put("ident", np.eye(P))
    half = DH // 2
    inv_freq = (1.0 / np.float32(10000.0) ** (np.arange(half, dtype=np.float32) / np.float32(half))).astype(np.float32)
    ang = (np.arange(TOK, dtype=np.float32)[:, None] * inv_freq).astype(np.float32)
    sin, cos = np.sin(ang), np.cos(ang)
    put("rope", np.stack([cos, -sin, sin], 1).reshape(TT, P, 3 * half).transpose(1, 0, 2))
    t, s = np.arange(P)[:, None], np.arange(P)[None, :]
    put("mask", np.concatenate([np.zeros((P, P)), np.where(s <= t, 0.0, CAUSAL)], 1))
    put("decay", np.concatenate([np.maximum(s - t, 0), np.where(s >= t, DH ** -0.5, 0.0)], 1))
    put("block", (np.arange(P)[:, None] // DH == np.arange(8)))
    put("iota", np.tile(np.arange(8), (P, 1)))
    put("tcol", np.stack([-np.arange(P), -(P - np.arange(P))], 1))
    ex = np.zeros((32, NT0 * P + R1 * H1), np.float32)
    owner = np.minimum(np.arange(HID0) // HE0, E0)
    for base in (0, 16):
        ex[base + owner, np.arange(HID0)] = 0.5
        ex[base + np.arange(R1 * H1) // H1, NT0 * P + np.arange(R1 * H1)] = 1.0
    return c, ex


def bass_two_layer_kernel(nc, x, wq, wk, wv, wo, gate_w, w_gate, w_up, w_down, shgate_w, shw_gate, shw_up,
                          shw_down, qkv_w, qkv_norm_w, proj_w, proj_norm_w, norm_w, decay_s, wg1, bg1,
                          wgate1, bgate1, wup1, bup1, wdown1, bdown1, ws_up, bs_up, ws_down, bs_down,
                          const_in, spread_in, out):
    f32, f32r = mybir.dt.float32, mybir.dt.float32r
    bf16, f16, u32 = mybir.dt.bfloat16, mybir.dt.float16, mybir.dt.uint32
    ALU, ACT, AX = mybir.AluOpType, mybir.ActivationFunctionType, mybir.AxisListType

    ctx = ExitStack()
    with ctx:
        def sb(name, shape, dt=f32):
            return ctx.enter_context(nc.sbuf_tensor(name, shape, dt))

        def bank(name):
            return ctx.enter_context(nc.psum_tensor(name, [P, 512], f32))

        x_all = sb("x_all", [P, NB, TT, D])
        cst = sb("cst", [P, CONST_W])

        def const(name):
            at, n = CONSTS[name]
            return cst[:, at:at + n]

        ident = const("ident")
        norms = sb("norms", [P, 2, TT, D])
        xn, yn = norms[:, 0], norms[:, 1]
        st = sb("st", [P, TT, 6])
        mv = sb("mv", [P, TT, 2])
        ve = sb("ve", [P, TT])
        rstd = sb("rstd", [P, TT])
        powers = sb("powers", [P, 2])
        WR = sb("WR", [P, NT0 * TILE_W + NT0 * 2 * D], f32r)
        gu_w = WR[:, 0:D0_AT].rearrange("p (t l q c) -> p t l q c", t=NT0, l=2, q=2 * KT)
        dn_w = WR[:, D0_AT:].rearrange("p (t l n) -> p t l n", t=NT0, l=2)
        wqkv = sb("wqkv", [P, 2, KT, NQ], f32r)
        wo_r = sb("wo_r", [P, 2, KT, D], f32r)
        spread = sb("spread", [P, NT0 * P + R1 * H1], f32r)
        xT = sb("xT", [P, 2, KT, TOK], f32r)
        stack = sb("stack", [P, TT, (H + HKV) * 4 * DH], f32r)
        qT = sb("qT", [P, NPAIR, TOK], f32r)
        kTz = sb("kTz", [P, 2, 2, TOK], f32r)
        cw = sb("cw", [P, TT, P], f32r)
        cwT = sb("cwT", [P, TOK], f32r)
        hT = sb("hT", [P, 2, 2, TOK], f32r)
        yT = stack[:, 0, 0:2 * KT * TOK].rearrange("p (l k n) -> p l k n", l=2, k=KT)
        v3 = sb("v3", [P, TT, HKV, 3, DH], bf16)
        pT = sb("pT", [P, 2, 3 * TOK], f16)
        rot = sb("rot", [P, TT, (H + HKV) * DH])
        rope_n = (H + HKV) * DH
        rope_a = sb("rope_a", [P, rope_n])
        rope_b = sb("rope_b", [P, rope_n])
        vr = sb("vr", [P, TT, 2, HKV * DH])
        lg = sb("lg", [P, TT, GATES])
        top = sb("top", [P, TT, 8])
        top_ix = sb("top_ix", [P, TT, 8], u32)
        ixf = sb("ixf", [P, TT, 8])
        dz = sb("dz", [P, TT, 2])
        ez = sb("ez", [P, TT, 2])
        ez1 = sb("ez1", [P, TT, 2])
        rc = sb("rc", [P, TT, 2])
        w2nd = sb("w2nd", [P, TT])
        oh = sb("oh", [P, TT, 2, 8])
        c9 = sb("c9", [P, TT, E0 + 1])
        sm = sb("sm", [P, 3 * TOK])
        nmax = sb("nmax", [P, 2, 4])
        pm = sb("pm", [P, 2, 3 * TOK])

        def sm_at(p):
            return sm[:, :] if p % 2 == 0 else norms[:, :, :, :].rearrange("p a t d -> p (a t d)")[:, 0:3 * TOK]

        def rope_at(t, k):
            return (rope_a, rope_b)[k][:, :] if t == 0 else pm[:, 1, k * rope_n:(k + 1) * rope_n]

        rs = sb("rs", [P, NPAIR * 4])
        rinv = sb("rinv", [P, NPAIR * 4])
        y = sb("y", [P, NPAIR, 4, DH])
        th = sb("th", [P, 2, TOK])
        s2 = sb("s2", [P, 2, TOK])
        hs = sb("hs", [P, 2, TOK])
        SLOTS, SLOT_W = 4, 768
        stage = sb("stage", [P, SLOTS, SLOT_W])
        gates_nat = sb("gates_nat", [GATES, D])

        small_rows = sb("small_rows", [18, P])
        cols = sb("cols", [P, 18])
        s_b = sb("s_b", [P, H])
        ns_b = sb("ns_b", [P, H])
        nw_b = sb("nw_b", [P, D])
        bg_b = sb("bg_b", [P, E1])
        ones = sb("ones", [P, P])
        abs_sum = sb("abs_sum", [P, 3])
        w_mean = sb("w_mean", [P, 2])
        w_inv = sb("w_inv", [P, 2])
        nwm = sb("nwm", [P, 2, KT])
        lam = sb("lam", [P, 2, H])
        dm = sb("dm", [P, H, P])
        proj_t = sb("proj_t", [P, KT, D], f32r)
        bias_w = sb("bias_w", [P, 2, D], f32r)
        router_w = sb("router_w", [P, KT, 2, E1], f32r)
        qkv_t = wqkv[:, :, :, :].rearrange("p l k n -> p (l k n)")[:, 0:KT * 3 * D].rearrange("p (k n) -> p k n", k=KT)
        GU_BLOCK, DN_BLOCK = [0, 1, 3, 4, 6, 7], [2, 2, 5, 5, 8, 8, 10, 10]

        def block_of(n, at=0, width=TILE_W):
            return WR[:, n * TILE_W + at:n * TILE_W + at + width]

        def gu1_w(i):
            return block_of(GU_BLOCK[i]).rearrange("p (l q c) -> p l q c", l=2, q=4)

        def up1_w(i):
            return block_of(9, 512 * i, 512).rearrange("p (l q c) -> p l q c", l=2, q=2)

        def dn1_w(i):
            return block_of(DN_BLOCK[i], 512 * (i % 2), 512).rearrange("p (l n) -> p l n", l=2)

        qT1 = block_of(11).rearrange("p (l g n) -> p l g n", l=2, g=2)
        kT1 = block_of(12).rearrange("p (l g n) -> p l g n", l=2, g=2)
        kd = block_of(13, 0, 512).rearrange("p (l n) -> p l n", l=2)
        state = block_of(13, 512, 512).rearrange("p (l g n) -> p l g n", l=2, g=2)

        def q_pad(j):
            at = D0_AT + 5120 * (j % 2)
            return WR[:, at:at + 2048].rearrange("p (l h n) -> p l h n", l=2, h=8)

        aT = WR[:, D0_AT + 2048:D0_AT + 4096].rearrange("p (a l n) -> p a l n", a=2, l=2)
        v2 = WR[:, D0_AT + 4096:D0_AT + 5120].rearrange("p (t h l d) -> p t h l d", t=TT, h=H, l=2)
        hT1 = qT[:, 0:4, :].rearrange("p (l k) n -> p l k n", l=2)
        oT = qT[:, 4:8, :].rearrange("p (l k) n -> p l k n", l=2)
        o_tok = y[:, :, :, :].rearrange("p a b c -> p (a b c)").rearrange("p (t n) -> p t n", t=TT)
        og = sm[:, 0:TT * D].rearrange("p (t n) -> p t n", t=TT)
        cross = rope_a[:, 0:D]
        kdf = rot[:, 0, 0:D]
        stf = rot[:, 1, 0:D]
        bias_f = sm[:, 0:D]
        rh = sb("rh", [P, TT])
        ra = sb("ra", [P, TT])

        def af_at(u):
            return pm[:, u % 2, 0:4 * P]

        sq = rope_b[:, 0:D]
        ss = sb("ss", [P, 2, TT])
        r1 = sb("r1", [P, 2, TT])
        r2 = sb("r2", [P, 2, TT])
        lg1 = sb("lg1", [P, TT, E1])
        e1 = sb("e1", [P, TT, E1])
        em = sb("em", [P, 2, TT, E1])
        esum = sb("esum", [P, TT])
        erec = sb("erec", [P, TT])
        ntop = sb("ntop", [P, TT])
        c1 = sb("c1", [P, TT, R1 + 1])

        GU = [bank("gu0"), bank("gu1")]
        CB, OB = bank("cb"), bank("ob")
        X = [bank(f"x{i}") for i in range(4)]

        class Steps:

            def __init__(self, name, per):
                self.sem = ctx.enter_context(nc.semaphore(name))
                self.per = per

            def at(self, b, k):
                return self.per * b + k

        def is_first(b):
            return isinstance(b, int) and b == 0

        def is_last(b):
            return isinstance(b, int) and b == NB - 1

        def batches(eng, program):
            program(0)
            with eng.Fori(1, NB - 1) as b:
                program(b)
            program(NB - 1)

        def tokens_of(b):
            return x_all[:, b] if isinstance(b, int) else x_all[:, bass.ds(b, 1)].squeeze(1)

        def wait(eng, steps, b, k):
            eng.wait_ge(steps.sem, steps.at(b, k))

        def wait_apart(eng, steps, b, k):
            wait(eng, steps, b, k)
            if not isinstance(b, int):
                eng.nop(nofuse=True)

        PREP_POOL, PREP_VEC, SMALL_IN = 6, 4, 16 * 11
        x_in = [Steps(f"x_in{b}", 0) for b in range(NB)]
        cst_in = Steps("cst_in", 0)
        gates_in = Steps("gates_in", 0)
        stage_in = [Steps(f"stage_in{k}", 0) for k in range(SLOTS)]
        w_hi, w_lo = Steps("w_hi", 0), Steps("w_lo", 0)
        prep_pool, prep_pe, prep_vec = Steps("prep_pool", 0), Steps("prep_pe", 0), Steps("prep_vec", 0)
        stats_vec = Steps("stats_vec", 4)
        rstd_pool = Steps("rstd_pool", 2)
        norm_vec = Steps("norm_vec", TT)
        xT_pe = Steps("xT_pe", 1)
        xT_hi, xT_lo = Steps("xT_hi", 1), Steps("xT_lo", 1)
        qkv_pe = Steps("qkv_pe", TT)
        rope_vec = Steps("rope_vec", 3 * TT)
        rope_pool = Steps("rope_pool", TT)
        stack_hi = Steps("stack_hi", 2 * TT)
        stack_lo = Steps("stack_lo", 2 * TT)
        v_vec = Steps("v_vec", 5 * TT)
        route_vec = Steps("route_vec", 3 * TT)
        route_pool = Steps("route_pool", 14)
        route_act = Steps("route_act", 1)
        qkT_pe = Steps("qkT_pe", 5)
        qkT_act = Steps("qkT_act", 6)
        cwT_pe, cwT_vec = Steps("cwT_pe", 1), Steps("cwT_vec", 1)
        score_pe = Steps("score_pe", 2 * NPAIR)
        max_vec = Steps("max_vec", 4 * NPAIR)
        exp_act = Steps("exp_act", 4 * NPAIR)
        pT_pe = Steps("pT_pe", 2 * NPAIR)
        pT_hi, pT_lo = Steps("pT_hi", 2 * NPAIR), Steps("pT_lo", 2 * NPAIR)
        pv_pe = Steps("pv_pe", NPAIR)
        y_vec = Steps("y_vec", NPAIR)
        yn_vec = Steps("yn_vec", 1 + TT)
        yT_pe, yT_hi, yT_lo = Steps("yT_pe", 1), Steps("yT_hi", 1), Steps("yT_lo", 1)
        gu_pe = Steps("gu_pe", NT0)
        cb_pe = Steps("cb_pe", NT0)
        dn_pe = Steps("dn_pe", NT0)
        wo_pe = Steps("wo_pe", 1)
        tanh_act = Steps("tanh_act", NT0)
        ffn_vec = Steps("ffn_vec", 3 * NT0)
        h_hi, h_lo = Steps("h_hi", NT0), Steps("h_lo", NT0)
        res_vec = Steps("res_vec", 1)
        small_in = Steps("small_in", 0)
        small_pe, small_vec = Steps("small_pe", 0), Steps("small_vec", 0)
        tern_vec, tern_pe, tern_round, tern_act = (Steps(n, 0) for n in ("tern_vec", "tern_pe", "tern_round", "tern_act"))
        decay_act, decay_vec = Steps("decay_act", 0), Steps("decay_vec", 0)
        stats1_vec, rstd1_pool, norm1_vec = Steps("stats1_vec", 4), Steps("rstd1_pool", 6), Steps("norm1_vec", 2 * TT)
        xT1_pe, xT1_hi, xT1_lo = Steps("xT1_pe", 2), Steps("xT1_hi", 3), Steps("xT1_lo", 3)
        qk1_pe, qk1_hi, qk1_lo = Steps("qk1_pe", 2), Steps("qk1_hi", 2), Steps("qk1_lo", 2)
        kv1_pe, v1_hi, v1_lo = Steps("kv1_pe", TT), Steps("v1_hi", TT), Steps("v1_lo", TT)
        kd_vec, kd_hi, kd_lo = Steps("kd_vec", 1), Steps("kd_hi", 1), Steps("kd_lo", 1)
        state_pe, state_vec, state_hi, state_lo = (Steps(n, 1) for n in ("state_pe", "state_vec", "state_hi", "state_lo"))
        cross_pe, cross_vec = Steps("cross_pe", 1), Steps("cross_vec", 1)
        route1_pe, route1_vec, route1_pool, route1_act = (Steps("route1_pe", TT), Steps("route1_vec", 17),
                                                          Steps("route1_pool", 2), Steps("route1_act", TT))
        cw1_pe, cw1_vec = Steps("cw1_pe", 1), Steps("cw1_vec", 1)
        pad_first, pad_hi, pad_lo = Steps("pad_first", 2), Steps("pad_hi", 2), Steps("pad_lo", 4)
        ret_pe, ret_vec, ret_hi, ret_lo, rv_pe = (Steps(n, 8) for n in ("ret_pe", "ret_vec", "ret_hi", "ret_lo", "rv_pe"))
        o_vec, o_act, o_pool = Steps("o_vec", 5), Steps("o_act", 2 * TT), Steps("o_pool", 7)
        oT_pe, oT_hi, oT_lo, proj_pe = Steps("oT_pe", 1), Steps("oT_hi", 2), Steps("oT_lo", 2), Steps("proj_pe", 1)
        gu1_pe, silu_act, ffn1_vec = Steps("gu1_pe", NT1), Steps("silu_act", NT1), Steps("ffn1_vec", 2 * R1)
        cb1_pe, dn1_pe = Steps("cb1_pe", R1), Steps("dn1_pe", NT1 + 1)
        h1_hi, h1_lo = Steps("h1_hi", NT1), Steps("h1_lo", NT1)
        res1_vec = Steps("res1_vec", 1 + TT)
        out_done = Steps("out_done", 0)

        def qkv_piece(slot):
            v = stage[:, slot, 0:KT * QKV].rearrange("p (k n) -> p k n", k=KT)
            loads = [(v[:, :, 0:256], wq.rearrange("(k p) n -> p k n", p=P)),
                     (v[:, :, 256:320], wk.rearrange("(k p) n -> p k n", p=P)),
                     (v[:, :, 320:384], wv.rearrange("(k p) n -> p k n", p=P))]
            splits = []
            for k in range(KT):
                for gp in range(2):
                    src = v[:, k, gp * 128:gp * 128 + 128].rearrange("p (r j d) -> p r j d", r=2, j=4)
                    dst = [wqkv[:, l, k, gp * 128:gp * 128 + 128].rearrange("p (j r d) -> p r j d", j=4, r=2)
                           for l in range(2)]
                    splits.append((src, *dst))
            splits.append((v[:, :, 256:384], wqkv[:, 0, :, 256:384], wqkv[:, 1, :, 256:384]))
            return loads, splits

        def gu_piece(e):
            def make(slot):
                v = stage[:, slot, 0:4 * HE0].rearrange("p (q c) -> p q c", q=4)
                if e < E0:
                    src = [w[e].rearrange("(k p) h -> p k h", p=P) for w in (w_gate, w_up)]
                else:
                    a = (e - E0) * HE0
                    src = [w[:, a:a + HE0].rearrange("(k p) h -> p k h", p=P) for w in (shw_gate, shw_up)]
                loads = [(v[:, 2 * n:2 * n + 2, :], src[n]) for n in range(2)]
                splits, at = [], e * HE0
                while at < (e + 1) * HE0:
                    t, o = divmod(at, P)
                    n = min(P - o, (e + 1) * HE0 - at)
                    s = v[:, :, at - e * HE0:at - e * HE0 + n]
                    splits.append((s, gu_w[:, t, 0, :, o:o + n], gu_w[:, t, 1, :, o:o + n]))
                    at += n
                return loads, splits
            return make

        def dn_piece(t0, n):
            def make(slot):
                v = stage[:, slot, 0:n * D].rearrange("p (t c) -> p t c", t=n)
                flat = w_down.rearrange("e h c -> (e h) c")
                loads, splits = [], []
                full = E0 * HE0 // P
                a = min(n, max(0, full - t0))
                if a:
                    loads.append((v[:, 0:a, :], flat[t0 * P:(t0 + a) * P, :].rearrange("(t p) c -> p t c", p=P)))
                for k in range(a, n):
                    r0, m = (t0 + k - full) * P, tile_rows(t0 + k)
                    loads.append((v[0:m, k, :], shw_down[r0:r0 + m, :]))
                whole = [k for k in range(n) if tile_rows(t0 + k) == P]
                if whole:
                    k = len(whole)
                    splits.append((v[:, 0:k, :], dn_w[:, t0:t0 + k, 0, :], dn_w[:, t0:t0 + k, 1, :]))
                if len(whole) < n:
                    m = tile_rows(t0 + n - 1)
                    splits.append((v[0:m, n - 1, :], dn_w[0:m, t0 + n - 1, 0, :], dn_w[0:m, t0 + n - 1, 1, :]))
                return loads, splits
            return make

        def wo_piece(slot):
            v = stage[:, slot, 0:KT * D].rearrange("p (k c) -> p k c", k=KT)
            loads = []
            for gp in range(2):
                for r in range(2):
                    for j in range(4):
                        head = (2 * gp + r) * 4 + j
                        at = (2 * j + r) * DH
                        loads.append((v[at:at + DH, gp, :], wo[head * DH:(head + 1) * DH, :]))
            return loads, [(v, wo_r[:, 0], wo_r[:, 1])]

        def spread_piece(c0, n):
            def make(slot):
                v = stage[0:32, slot, 0:n]
                return [(v, spread_in[:, c0:c0 + n])], [(v, spread[0:32, c0:c0 + n], None)]
            return make

        def ternary_piece(w, r0, n):
            def make(slot):
                v = stage[:, slot, 0:n * D].rearrange("p (r c) -> p r c", r=n)
                return [(v, w[r0 * P:(r0 + n) * P, :].rearrange("(r p) c -> p r c", p=P))], []
            return make

        def expert1_piece(e):
            def make(slot):
                v = stage[:, slot, 0:SLOT_W]
                q = v[:, 0:4 * P].rearrange("p (q c) -> p q c", q=4)
                loads = [(q[:, 2 * n:2 * n + 2, :], w[e].rearrange("(k p) h -> p k h", p=P)) for n, w in enumerate((wgate1, wup1))]
                loads.append((v[:, 4 * P:SLOT_W], wdown1[e]))
                return loads, [(q, gu1_w(e)[:, 0], gu1_w(e)[:, 1]), (v[:, 4 * P:SLOT_W], dn1_w(e)[:, 0, :], dn1_w(e)[:, 1, :])]
            return make

        def shared_up_piece(slot):
            v = stage[:, slot, 0:KT * HS1].rearrange("p (k n) -> p k n", k=KT)
            return ([(v, ws_up.rearrange("(k p) n -> p k n", p=P))],
                    [(v[:, :, i * P:(i + 1) * P], up1_w(i)[:, 0], up1_w(i)[:, 1]) for i in range(2)])

        def shared_down_piece(slot):
            v = stage[:, slot, 0:2 * D].rearrange("p (k n) -> p k n", k=2)
            return ([(v, ws_down.rearrange("(k p) n -> p k n", p=P))],
                    [(v[:, i, :], dn1_w(R1 + i)[:, 0, :], dn1_w(R1 + i)[:, 1, :]) for i in range(2)])

        def router_piece(slot):
            v = stage[:, slot, 0:KT * E1].rearrange("p (k n) -> p k n", k=KT)
            return [(v, wg1.rearrange("(k p) n -> p k n", p=P))], [(v, router_w[:, :, 0, :], router_w[:, :, 1, :])]

        order = [("qkv", qkv_piece), ("gu0", gu_piece(0)), ("sp0", spread_piece(0, 768)), ("gu1", gu_piece(1)),
                 ("dn0", dn_piece(0, 3)), ("gu2", gu_piece(2)), ("gu3", gu_piece(3)), ("dn3", dn_piece(3, 3)),
                 ("sp1", spread_piece(768, 768)), ("gu4", gu_piece(4)), ("gu5", gu_piece(5)), ("dn6", dn_piece(6, 3)), ("gu6", gu_piece(6)),
                 ("gu7", gu_piece(7)), ("wo", wo_piece), ("dn9", dn_piece(9, 3)), ("gu8", gu_piece(8)), ("sp2", spread_piece(1536, 256)),
                 ("gu9", gu_piece(9)), ("dn12", dn_piece(12, 2)),
                 ("tern0", ternary_piece(qkv_w, 0, 3)), ("tern1", ternary_piece(qkv_w, 3, 3)), ("tern2", ternary_piece(proj_w, 0, 2)),
                 ("router", router_piece), ("sp3", spread_piece(NT0 * P, R1 * H1)),
                 ("x0", expert1_piece(0)), ("x1", expert1_piece(1)), ("x2", expert1_piece(2)), ("x3", expert1_piece(3)),
                 ("x4", expert1_piece(4)), ("x5", expert1_piece(5)), ("xup", shared_up_piece), ("xdn", shared_down_piece)]
        pieces, need, arrived = {}, {}, [0] * SLOTS
        n_hi = n_lo = 0
        for n, (name, make) in enumerate(order):
            slot = n % SLOTS
            loads, splits = make(slot)
            arrived[slot] += 16 * len(loads)
            prev = order[n - SLOTS][0] if n >= SLOTS else None
            lo_splits = [s for s in splits if s[2] is not None]
            n_hi, n_lo = n_hi + len(splits), n_lo + len(lo_splits)
            pieces[name] = (slot, arrived[slot], loads, splits, lo_splits, prev)
            need[name] = (n_hi, n_lo)

        def load_piece(eng, name):
            slot, _, loads, _, _, prev = pieces[name]
            if prev is not None:
                eng.wait_ge(w_hi.sem, need[prev][0])
                eng.wait_ge(w_lo.sem, need[prev][1])
                if prev.startswith("tern"):
                    eng.wait_ge(tern_pe.sem, 1 + 4)
            for dst, src in loads:
                eng.dma_start(dst, src).then_inc(stage_in[slot].sem, 16)

        def split_hi(eng, name):
            slot, landed, _, splits, _, _ = pieces[name]
            eng.wait_ge(stage_in[slot].sem, landed)
            if name in FREED_BY:
                wait(eng, gu_pe, NB - 1, FREED_BY[name] + 1)
            for src, hi, _ in splits:
                eng.activation(hi, src, ACT.Copy).then_inc(w_hi.sem, 1)

        def split_lo(eng, name):
            _, _, _, _, lo_splits, _ = pieces[name]
            eng.wait_ge(w_hi.sem, need[name][0])
            for src, hi, lo in lo_splits:
                eng.tensor_tensor(lo, src, hi.bitcast(f32), ALU.subtract).then_inc(w_lo.sem, 1)

        def weights_ready(eng, *names):
            for name in names:
                eng.wait_ge(w_hi.sem, need[name][0])
                eng.wait_ge(w_lo.sem, need[name][1])

        slot_of = {name: pieces[name][0] for name in pieces}
        MAGIC = 1.5 * 2.0 ** 23
        TERN_VEC, TERN_ROUND = 8, 9
        NORM_SLOT = 10
        EPS32 = float(np.finfo(np.float32).eps)

        BEFORE = ["qkv", "gu0", "sp0", "gu1", "dn0"]
        IN_SLOT = {1: ["gu3", "dn3"], 2: ["sp1", "gu4"], 3: ["gu5"], 4: ["dn6"], 5: ["gu6"], 6: ["gu7"],
                   7: ["wo"], 8: ["dn9", "gu8"], 9: ["sp2", "gu9"], 10: ["dn12"]}
        LAST_SLOT = {0: ["router"], 1: ["sp3"], 3: ["x0"], 4: ["x1"], 6: ["x2"], 7: ["x3"], 9: ["x4"], 10: ["x5"], 11: ["xup"], 12: ["xdn"]}
        FREED_BY = {"x0": 2, "x1": 2, "x2": 5, "x3": 5, "x4": 8, "x5": 8, "xup": 9, "xdn": 10}
        assert BEFORE + ["gu2"] + sum((IN_SLOT[k] for k in sorted(IN_SLOT)), []) == [n for n, _ in order][:20]

        def gu_needs(i):
            last = min((i * P + tile_rows(i) - 1) // HE0, 9)
            return ["gu0"] if i == 0 else [f"gu{last}"]

        def dn_needs(i):
            return [f"dn{3 * (i // 3)}"]

        block = ctx.enter_context(nc.Block())

        @block.sync
        def _(sp):
            sp.dma_start(x_all[:, 0], x[0].rearrange("(t p) d -> p t d", p=P)).then_inc(x_in[0].sem, 16)
            sp.dma_start(cst[:, :], const_in).then_inc(cst_in.sem, 16)
            sp.dma_start(gates_nat[0:E0, :], gate_w).then_inc(gates_in.sem, 16)
            for row in range(E0, GATES):
                sp.dma_start(gates_nat[row:row + 1, :], shgate_w.rearrange("(a n) -> a n", a=1)).then_inc(gates_in.sem, 16)
            for n, (name, _) in enumerate(order):
                if n == 5:
                    for at, w in ((0, bgate1), (6, bup1)):
                        sp.dma_start(small_rows[at:at + R1, :], w).then_inc(small_in.sem, 16)
                    for at, w in ((12, bs_up), (14, qkv_norm_w), (16, proj_norm_w)):
                        sp.dma_start(small_rows[at:at + 2, :], w.rearrange("(a n) -> a n", a=2)).then_inc(small_in.sem, 16)
                    for dst, w, m in ((s_b, decay_s, H), (nw_b, norm_w, D), (bg_b, bg1, E1)):
                        sp.dma_start(dst[:, :], w.rearrange("(a n) -> a n", a=1).broadcast_to([P, m])).then_inc(small_in.sem, 16)
                    sp.wait_ge(prep_pool.sem, PREP_POOL)
                    for at in (0, 16):
                        sp.dma_start(bias_f[at:at + R1, :], bdown1).then_inc(small_in.sem, 16)
                    sp.dma_start(bias_f[R1:R1 + 1, :], bs_down.rearrange("(a n) -> a n", a=1)).then_inc(small_in.sem, 16)
                load_piece(sp, name)
                if n == 4:
                    for b in range(1, NB):
                        sp.dma_start(x_all[:, b], x[b].rearrange("(t p) d -> p t d", p=P)).then_inc(x_in[b].sem, 16)
            with sp.Fori(0, NB) as b:
                wait(sp, res1_vec, b, 1 + TT)
                sp.dma_start(out[bass.ds(b, 1)].rearrange("b (t p) d -> p (b t) d", p=P), tokens_of(b)).then_inc(out_done.sem, 16)
            sp.wait_ge(out_done.sem, 16 * NB)

        @block.gpsimd
        def _(pool):
            pool.memset(powers[:, 0:1], -0.5).then_inc(prep_pool.sem, 1)
            pool.memset(powers[:, 1:2], -1.0).then_inc(prep_pool.sem, 1)
            pool.memset(cw[:, :, :].bitcast(f32), 0.0).then_inc(prep_pool.sem, 1)
            pool.memset(kTz[:, :, :, :].bitcast(f32), 0.0).then_inc(prep_pool.sem, 1)
            pool.memset(ones[:, :], 1.0).then_inc(prep_pool.sem, 1)
            pool.memset(bias_f[:, :], 0.0).then_inc(prep_pool.sem, 1)
            pool.wait_ge(prep_pool.sem, PREP_POOL)

            def rsqrt_steps(b, steps, base, eps, src, tmp, dst):
                pool.tensor_scalar(tmp, src, eps, None, ALU.add).then_inc(steps.sem, 1)
                wait(pool, steps, b, base + 1)
                pool.tensor_tensor(dst, tmp, powers[:, 0:1].broadcast_to([P, TT]), ALU.pow).then_inc(steps.sem, 1)

            half = powers[:, 0:1].broadcast_to([P, TT])

            def norm_factors(b):
                wait(pool, stats_vec, b, 4)
                if b:
                    wait(pool, norm_vec, b - 1, TT)
                rsqrt_steps(b, rstd_pool, 0, 1e-5, mv[:, :, 1], ve[:, :], rstd[:, :])

            def norm1_factors(b):
                wait(pool, stats1_vec, b, 4)
                if not is_first(b):
                    wait_apart(pool, norm1_vec, b - 1, 2 * TT)
                else:
                    wait(pool, norm_vec, NB - 1, TT)
                rsqrt_steps(b, rstd1_pool, 0, 1e-5, mv[:, :, 1], ve[:, :], rstd[:, :])
                wait(pool, rstd1_pool, b, 2)
                pool.tensor_tensor(ve[:, :], rstd[:, :], rstd[:, :], ALU.mult).then_inc(rstd1_pool.sem, 1)
                wait(pool, rstd1_pool, b, 3)
                pool.tensor_tensor(ve[:, :], ve[:, :], mv[:, :, 1], ALU.mult).then_inc(rstd1_pool.sem, 1)
                wait_apart(pool, rstd1_pool, b, 4)
                pool.tensor_scalar(ve[:, :], ve[:, :], EPS32, None, ALU.add).then_inc(rstd1_pool.sem, 1)
                wait(pool, rstd1_pool, b, 5)
                pool.tensor_tensor(rh[:, :], ve[:, :], half, ALU.pow).then_inc(rstd1_pool.sem, 1)

            def out_factors(b):
                if not is_first(b):
                    wait(pool, res1_vec, b - 1, 1 + TT)
                wait_apart(pool, o_act, b, 2 * TT)
                k = 0

                def step1(ins):
                    nonlocal k
                    k += 1
                    ins.then_inc(o_pool.sem, 1)
                    wait_apart(pool, o_pool, b, k)

                step1(pool.tensor_scalar(r1[:, 0, :], ss[:, 0, :], 1.0 / D, 1e-6, ALU.mult, ALU.add))
                step1(pool.tensor_tensor(r1[:, 1, :], r1[:, 0, :], half, ALU.pow))
                step1(pool.tensor_tensor(r2[:, 0, :], r1[:, 1, :], r1[:, 1, :], ALU.mult))
                step1(pool.tensor_tensor(r2[:, 0, :], r2[:, 0, :], ss[:, 1, :], ALU.mult))
                step1(pool.tensor_scalar(r2[:, 0, :], r2[:, 0, :], 1.0 / D, EPS32, ALU.mult, ALU.add))
                step1(pool.tensor_tensor(r2[:, 1, :], r2[:, 0, :], half, ALU.pow))
                step1(pool.tensor_tensor(ra[:, :], r2[:, 1, :], r1[:, 1, :], ALU.mult))

            norm_factors(0)
            for b in range(NB):
                if b == 0:
                    for name in BEFORE:
                        split_lo(pool, name)
                for t in range(TT):
                    wait(pool, rope_vec, b, 3 * t + 3)
                    if b:
                        wait(pool, stack_lo, b - 1, 2 * TT)
                    pool.tensor_tensor(rot[:, t, :], rope_at(t, 0), rope_at(t, 1), ALU.add).then_inc(rope_pool.sem, 1)
                wait(pool, route_vec, b, 3 * TT)
                k = 0

                def step(ins):
                    nonlocal k
                    k += 1
                    ins.then_inc(route_pool.sem, 1)

                step(pool.tensor_tensor(dz[:, :, 0], top[:, :, 1], top[:, :, 0], ALU.subtract))
                step(pool.tensor_scalar(dz[:, :, 1], lg[:, :, E0], -1.0, None, ALU.mult))
                step(pool.tensor_copy(ixf[:, :, :], top_ix[:, :, :]))
                wait(pool, route_act, b, 1)
                step(pool.tensor_scalar(ez1[:, :, :], ez[:, :, :], 1.0, None, ALU.add))
                wait(pool, route_pool, b, k)
                step(pool.tensor_tensor(rc[:, :, :], ez1[:, :, :],
                                        powers[:, 1:2].unsqueeze(2).broadcast_to([P, TT, 2]), ALU.pow))
                wait(pool, route_pool, b, k)
                step(pool.tensor_tensor(w2nd[:, :], ez[:, :, 0], rc[:, :, 0], ALU.mult))
                wait(pool, route_pool, b, k)
                for t in range(TT):
                    step(pool.tensor_scalar(oh[:, t, 0, :], const("iota"), ixf[:, t, 0:1], rc[:, t, 0:1],
                                            ALU.is_equal, ALU.mult))
                    step(pool.tensor_scalar(oh[:, t, 1, :], const("iota"), ixf[:, t, 1:2], w2nd[:, t:t + 1],
                                            ALU.is_equal, ALU.mult))
                wait(pool, route_pool, b, k)
                step(pool.tensor_tensor(c9[:, :, 0:E0], oh[:, :, 0, :], oh[:, :, 1, :], ALU.add))
                step(pool.tensor_copy(c9[:, :, E0], rc[:, :, 1]))
                wait(pool, route_pool, b, k)
                if b:
                    wait(pool, cwT_pe, b - 1, 1)
                step(pool.tensor_copy(cw[:, :, 0:E0 + 1], c9[:, :, :]))
                wait(pool, route_pool, b, k)
                step(pool.tensor_tensor(cw[:, :, 16:16 + E0 + 1], c9[:, :, :], cw[:, :, 0:E0 + 1].bitcast(f32), ALU.subtract))
                assert k == route_pool.per, k
                if b == 0:
                    split_lo(pool, "gu2")
                for i in range(NT0):
                    if b in (0, NB - 1):
                        for name in (IN_SLOT if b == 0 else LAST_SLOT).get(i, []):
                            split_lo(pool, name)
                    m = tile_rows(i)
                    wait(pool, h_hi, b, i + 1)
                    pool.tensor_tensor(hT[0:m, i % 2, 1, :], hs[0:m, i % 2, :], hT[0:m, i % 2, 0, :].bitcast(f32),
                                       ALU.subtract).then_inc(h_lo.sem, 1)
                    if i == NORM_SLOT:
                        norm_factors(b + 1) if b + 1 < NB else norm1_factors(0)
                    if b == 2 and 2 <= i < 2 + TERN_ROUND:
                        n, k = divmod(i - 2, 3)
                        w = stage[:, slot_of[f"tern{n}"], 0:(3, 3, 2)[n] * D]
                        first, second, *ops = ((w_inv[:, n // 2:n // 2 + 1], 1.0, ALU.mult, ALU.min),
                                               (-1.0, MAGIC, ALU.max, ALU.add), (-MAGIC, None, ALU.add))[k]
                        pool.wait_ge(tern_round.sem, 3 * n + k) if k else pool.wait_ge(tern_vec.sem, TERN_VEC)
                        pool.tensor_scalar(w, w, first, second, *ops).then_inc(tern_round.sem, 1)

            def layer1_batch(b):
                wait_apart(pool, route1_vec, b, 8)
                pool.tensor_scalar(ntop[:, :], top[:, :, 0], -1.0, None, ALU.mult).then_inc(route1_pool.sem, 1)
                pool.tensor_copy(ixf[:, :, :], top_ix[:, :, :]).then_inc(route1_pool.sem, 1)

                def pad_queries(j, l):
                    t, g = divmod(j, 2)
                    if j >= 2:
                        wait(pool, ret_pe, b, 2 * (j - 1))
                    elif not is_first(b):
                        wait(pool, ret_pe, b - 1, 8)
                    else:
                        wait(pool, dn_pe, NB - 1, NT0)
                    wait(pool, (qk1_hi, qk1_lo)[l], b, 1)
                    pool.tensor_tensor(q_pad(j)[:, l, :, :], qT1[:, l, g, t * P:(t + 1) * P].bitcast(f32).unsqueeze(1).broadcast_to([P, 8, P]),
                                       const("block").unsqueeze(2).broadcast_to([P, 8, P]), ALU.mult).then_inc((pad_first, pad_lo)[l].sem, 1)

                for l in range(2):
                    pad_queries(0, l)
                if not is_first(b):
                    out_factors(b - 1)
                for l in range(2):
                    pad_queries(1, l)
                for u in range(8):
                    wait(pool, h1_hi, b, u + 1)
                    pool.tensor_tensor(hT[:, u % 2, 1, :], hs[:, u % 2, :], hT[:, u % 2, 0, :].bitcast(f32),
                                       ALU.subtract).then_inc(h1_lo.sem, 1)
                    if u in (2, 4):
                        pad_queries(u // 2 + 1, 1)
                    if u == 1 and not is_last(b):
                        norm1_factors(b + 1)

            batches(pool, layer1_batch)
            out_factors(NB - 1)

        @block.scalar
        def _(act):
            def tokens_hi(b):
                wait(act, xT_pe, b, 1)
                if b:
                    wait(act, gu_pe, b - 1, NT0)
                    wait(act, qkv_pe, b - 1, TT)
                act.activation(xT[:, 0, :, :], X[1][:, :].rearrange("p (k n) -> p k n", k=KT), ACT.Copy).then_inc(xT_hi.sem, 1)

            def tokens1_hi(b):
                wait(act, xT1_pe, b, 1)
                if not is_first(b):
                    wait(act, gu1_pe, b - 1, NT1)
                    wait(act, route1_pe, b - 1, TT)
                else:
                    wait(act, gu_pe, NB - 1, NT0)
                act.activation(xT[:, 0, :, :], GU[0][:, :].rearrange("p (k n) -> p k n", k=KT), ACT.Copy).then_inc(xT1_hi.sem, 1)

            def qkv_tokens1_hi(b):
                wait(act, xT1_pe, b, 2)
                if not is_first(b):
                    wait(act, kv1_pe, b - 1, TT)
                for k in range(KT):
                    act.activation(hT1[:, 0, k, :], GU[1][:, k * TOK:(k + 1) * TOK], ACT.Copy, scale=nwm[:, 0, k:k + 1]).then_inc(xT1_hi.sem, 1)

            def out_squares(b, t):
                wait(act, o_vec, b, 2 + 3 * t)
                for n, src in enumerate((o_tok, og)):
                    if t or n:
                        wait(act, o_act, b, 2 * t + n)
                    act.activation(sq, src[:, t, :], ACT.Square, accum_out=ss[:, n, t:t + 1]).then_inc(o_act.sem, 1)

            def out_hi(b):
                wait(act, oT_pe, b, 1)
                for k in range(KT):
                    act.activation(oT[:, 0, k, :], X[2][:, k * TOK:(k + 1) * TOK], ACT.Copy, scale=nwm[:, 1, k:k + 1]).then_inc(oT_hi.sem, 1)

            for b in range(NB):
                if b == 0:
                    split_hi(act, "qkv")
                    act.wait_ge(prep_pe.sem, 1)
                    tokens_hi(0)
                    for name in BEFORE[1:]:
                        split_hi(act, name)

                def ternary_out(first):
                    for n in range(first, first + 2):
                        act.wait_ge(tern_pe.sem, 2 + n)
                        src = X[3 if n % 2 == 0 else 0][:, :].rearrange("p (r k c) -> p k r c", r=2, k=KT)
                        dst = (proj_t[:, :, :] if n == 3 else qkv_t[:, :, n * D:(n + 1) * D]).rearrange("p k (r c) -> p k r c", r=2)
                        wait(act, qkv_pe, b, TT)
                        act.activation(dst, src, ACT.Copy).then_inc(tern_act.sem, 1)

                def gate_tanh(i):
                    m = tile_rows(i)
                    wait(act, gu_pe, b, i + 1)
                    act.activation(th[0:m, i % 2, :], GU[i % 2][0:m, 0:TOK], ACT.Tanh, scale=0.5).then_inc(tanh_act.sem, 1)

                if b == NB - 1:
                    ternary_out(0)
                for t in range(TT):
                    wait(act, rope_pool, b, t + 1)
                    if b:
                        wait(act, qkT_pe, b - 1, 5)
                        wait(act, yT_pe, b - 1, 1)
                        wait(act, wo_pe, b - 1, 1)
                    q4 = stack[:, t, 0:H * 64].rearrange("p (h r d) -> p h r d", h=H, r=4)
                    k4 = stack[:, t, H * 64:].rearrange("p (h r l d) -> p h r l d", h=HKV, r=2, l=2)
                    rq = rot[:, t, 0:H * DH].rearrange("p (h d) -> p h d", h=H).unsqueeze(2).broadcast_to([P, H, 2, DH])
                    rk = rot[:, t, H * DH:].rearrange("p (h d) -> p h d", h=HKV).unsqueeze(2).broadcast_to([P, HKV, 2, DH])
                    act.activation(q4[:, :, 0:2, :], rq, ACT.Copy).then_inc(stack_hi.sem, 1)
                    act.activation(k4[:, :, :, 0, :], rk, ACT.Copy).then_inc(stack_hi.sem, 1)
                if b == NB - 1:
                    ternary_out(2)
                wait(act, route_pool, b, 3)
                act.activation(ez[:, :, :], dz[:, :, :], ACT.Exp).then_inc(route_act.sem, 1)
                if b == 0:
                    split_hi(act, "gu2")
                gate_tanh(0)
                gate_tanh(1)
                for n in range(4):
                    wait(act, qkT_pe, b, n + 1)
                    if n == 0 and b:
                        wait(act, score_pe, b - 1, 2 * NPAIR)
                    t, half = divmod(n, 2)
                    act.activation(qT[:, 4 * half:4 * half + 4, t * P:(t + 1) * P],
                                   X[3 if n % 2 == 0 else 0][:, :].rearrange("p (r n) -> p r n", r=4), ACT.Copy).then_inc(qkT_act.sem, 1)
                wait(act, qkT_pe, b, 5)
                for r in range(2):
                    rows = slice(64 * r, 64 * r + 64)
                    src = X[3][rows, :].rearrange("p (t g n) -> p g t n", t=TT, g=2)
                    dst = kTz[rows, :, r, :].rearrange("p g (t n) -> p g t n", t=TT)
                    act.activation(dst, src, ACT.Copy).then_inc(qkT_act.sem, 1)
                for i in range(NT0 + 1):
                    if b in (0, NB - 1):
                        for name in (IN_SLOT if b == 0 else LAST_SLOT).get(i, []):
                            split_hi(act, name)
                    if i == NT0 - 1 and b + 1 < NB:
                        tokens_hi(b + 1)
                    if 1 <= i <= NT0:
                        j = i - 1
                        m = tile_rows(j)
                        wait(act, ffn_vec, b, 3 * j + 3)
                        if j >= 2:
                            wait(act, dn_pe, b, j - 1)
                        elif b:
                            wait(act, dn_pe, b - 1, NT0 - 1 + j)
                        act.activation(hT[0:m, j % 2, 0, :], hs[0:m, j % 2, :], ACT.Copy).then_inc(h_hi.sem, 1)
                    if 2 <= i < NT0:
                        gate_tanh(i)
                    if 2 <= i < 2 + NPAIR:
                        p = i - 2
                        wait(act, pT_pe, b, 2 * p + 1)
                        if p or b:
                            wait(act, pv_pe, b, p) if p else wait(act, pv_pe, b - 1, NPAIR)
                        act.activation(pT[:, 0, TOK:3 * TOK], X[2][:, :], ACT.Copy).then_inc(pT_hi.sem, 1)
                    if 2 <= i < 2 + NPAIR:
                        p = i - 2
                        wait(act, pT_pe, b, 2 * p + 2)
                        act.activation(pT[:, 0, 0:TOK], X[3][:, TOK:2 * TOK], ACT.Copy).then_inc(pT_hi.sem, 1)
                    if 1 <= i < 1 + NPAIR:
                        p = i - 1
                        wait(act, max_vec, b, 4 * p + 4)
                        if p >= 2:
                            wait(act, pT_pe, b, 2 * (p - 1))
                        elif b:
                            wait(act, pT_pe, b - 1, 2 * (NPAIR - 1 + p))
                        for t in range(TT):
                            for r in range(2):
                                n = (t + 1) * P
                                at = r * P if t == 0 else TOK + r * TOK
                                k = 2 * t + r
                                act.activation(pm[:, p % 2, at:at + n], sm_at(p)[:, at:at + n], ACT.Exp,
                                               bias=nmax[:, p % 2, k:k + 1], scale=-1.0,
                                               accum_out=rs[:, 4 * p + k:4 * p + k + 1]).then_inc(exp_act.sem, 1)
                    if i == 11:
                        wait(act, yT_pe, b, 1)
                        act.activation(yT[:, 0, :, :], X[0][:, :].rearrange("p (k n) -> p k n", k=KT), ACT.Copy).then_inc(yT_hi.sem, 1)
                    if b == 2 and 1 <= i < 1 + NPAIR:
                        if i == 1:
                            act.wait_ge(decay_vec.sem, 1)
                            for n in range(2):
                                act.activation(lam[:, n, :], s_b[:, :], ACT.Exp, scale=const("tcol")[:, n:n + 1]).then_inc(decay_act.sem, 1)
                        for h in (2 * i - 2, 2 * i - 1):
                            act.activation(dm[:, h, :], const("decay")[:, 0:P], ACT.Exp, scale=ns_b[:, h:h + 1]).then_inc(decay_act.sem, 1)

            tokens1_hi(0)
            qkv_tokens1_hi(0)
            def layer1_batch(b):
                if not is_first(b):
                    out_squares(b - 1, 0)
                    out_squares(b - 1, 1)
                for t in range(TT):
                    wait(act, kv1_pe, b, t + 1)
                    wait(act, kd_vec, b, 1)
                    if not is_first(b):
                        wait(act, rv_pe, b - 1, 8)
                    else:
                        wait(act, dn_pe, NB - 1, NT0)
                    src = X[t][:, D:2 * D] if t == 0 else X[t][:, 0:D]
                    act.activation(v2[:, t, :, 0, :], src.rearrange("p (h d) -> p h d", h=H), ACT.Copy).then_inc(v1_hi.sem, 1)
                wait(act, kd_vec, b, 1)
                act.activation(kd[:, 0, :], kdf, ACT.Copy).then_inc(kd_hi.sem, 1)
                for n, dst in enumerate((qT1, kT1)):
                    wait(act, qk1_pe, b, n + 1)
                    if n == 0:
                        if not is_first(b):
                            wait(act, ret_pe, b - 1, 8)
                            wait(act, pad_lo, b - 1, 4)
                            wait(act, pad_first, b - 1, 2)
                            wait(act, pad_hi, b - 1, 2)
                        else:
                            wait(act, gu_pe, NB - 1, NT0)
                    act.activation(dst[:, 0, :, :], X[2 + n][:, :].rearrange("p (g n) -> p g n", g=2), ACT.Copy).then_inc(qk1_hi.sem, 1)
                wait(act, route1_pool, b, 2)
                for t in range(TT):
                    act.activation(e1[:, t, :], lg1[:, t, :], ACT.Exp, bias=ntop[:, t:t + 1]).then_inc(route1_act.sem, 1)
                wait(act, state_vec, b, 1)
                act.activation(state[:, 0, :, :].rearrange("p g n -> p (g n)"), stf, ACT.Copy).then_inc(state_hi.sem, 1)
                if not is_first(b):
                    out_hi(b - 1)
                for u in range(8):
                    wait(act, gu1_pe, b, u + 1)
                    if u >= 2:
                        wait(act, h1_lo, b, u - 1)
                    elif not is_first(b):
                        wait(act, h1_lo, b - 1, NT1 - 1 + u)
                    if u < R1:
                        act.activation(th[:, u % 2, :], GU[u % 2][:, 0:TOK], ACT.Silu, bias=cols[:, u:u + 1]).then_inc(silu_act.sem, 1)
                    else:
                        act.activation(hs[:, u % 2, :], GU[u % 2][:, 0:TOK], ACT.Silu, bias=cols[:, 6 + u:7 + u]).then_inc(silu_act.sem, 1)
                    wait(act, ret_vec, b, u + 1)
                    if u >= 2:
                        wait(act, rv_pe, b, u - 1)
                    act.activation(aT[:, u % 2, 0, :], af_at(u), ACT.Copy).then_inc(ret_hi.sem, 1)
                    if u < R1:
                        wait(act, ffn1_vec, b, 2 * u + 2)
                    else:
                        wait(act, silu_act, b, u + 1)
                    if u >= 2:
                        wait(act, dn1_pe, b, u - 1)
                    elif not is_first(b):
                        wait(act, dn1_pe, b - 1, NT1 - 1 + u)
                    else:
                        wait(act, dn_pe, NB - 1, NT0 - 1 + u)
                    act.activation(hT[:, u % 2, 0, :], hs[:, u % 2, :], ACT.Copy).then_inc(h1_hi.sem, 1)
                    if u == 7 and not is_last(b):
                        tokens1_hi(b + 1)
                        qkv_tokens1_hi(b + 1)

            batches(act, layer1_batch)
            out_squares(NB - 1, 0)
            out_squares(NB - 1, 1)
            out_hi(NB - 1)

        @block.vector
        def _(dve):
            def norm_stats(b, steps):
                for t in range(TT):
                    dve.bn_stats(st[:, t, :], tokens_of(b)[:, t, :]).then_inc(steps.sem, 1)
                for t in range(TT):
                    wait_apart(dve, steps, b, t + 1)
                    dve.bn_aggr(mv[:, t, :], st[:, t, :]).then_inc(steps.sem, 1)

            for rows in (slice(32, 64), slice(64, P)):
                dve.memset(spread[rows, :].bitcast(f32), 0.0).then_inc(prep_vec.sem, 1)
            dve.wait_ge(cst_in.sem, 16)
            def token_stats(b):
                dve.wait_ge(x_in[b].sem, 16)
                if b:
                    wait(dve, norm_vec, b - 1, TT)
                norm_stats(b, stats_vec)

            def normalise(b):
                wait(dve, rstd_pool, b, 2)
                if b:
                    wait(dve, xT_pe, b - 1, 1)
                for t in range(TT):
                    dve.tensor_scalar(xn[:, t, :], x_all[:, b, t, :], mv[:, t, 0:1], rstd[:, t:t + 1],
                                      ALU.subtract, ALU.mult).then_inc(norm_vec.sem, 1)

            def tokens_lo(b):
                wait(dve, xT_hi, b, 1)
                dve.tensor_tensor(xT[:, 1, :, :], X[1][:, :].rearrange("p (k n) -> p k n", k=KT),
                                  xT[:, 0, :, :].bitcast(f32), ALU.subtract).then_inc(xT_lo.sem, 1)

            def residual(b):
                wait(dve, dn_pe, b, NT0)
                wait(dve, wo_pe, b, 1)
                dve.tensor_tensor(x_all[:, b], x_all[:, b], OB[:, :].rearrange("p (t d) -> p t d", t=TT), ALU.add).then_inc(res_vec.sem, 1)

            def token_stats1(b):
                wait(dve, res_vec, b, 1)
                if not is_first(b):
                    wait(dve, norm1_vec, b - 1, 2 * TT)
                else:
                    wait(dve, norm_vec, NB - 1, TT)
                norm_stats(b, stats1_vec)

            def normalise1(b):
                wait(dve, rstd1_pool, b, 2)
                if not is_first(b):
                    wait(dve, xT1_pe, b - 1, 2)
                else:
                    wait(dve, xT_pe, NB - 1, 1)
                    wait(dve, yT_pe, NB - 1, 1)
                for t in range(TT):
                    dve.tensor_scalar(xn[:, t, :], tokens_of(b)[:, t, :], mv[:, t, 0:1], rstd[:, t:t + 1],
                                      ALU.subtract, ALU.mult).then_inc(norm1_vec.sem, 1)
                wait(dve, rstd1_pool, b, 6)
                wait(dve, norm1_vec, b, TT)
                for t in range(TT):
                    dve.tensor_scalar(yn[:, t, :], xn[:, t, :], rh[:, t:t + 1], None, ALU.mult).then_inc(norm1_vec.sem, 1)

            def tokens1_lo(b):
                wait(dve, xT1_hi, b, 1)
                dve.tensor_tensor(xT[:, 1, :, :], GU[0][:, :].rearrange("p (k n) -> p k n", k=KT),
                                  xT[:, 0, :, :].bitcast(f32), ALU.subtract).then_inc(xT1_lo.sem, 1)
                for k in range(KT):
                    wait(dve, xT1_hi, b, 1 + KT)
                    dve.scalar_tensor_tensor(hT1[:, 1, k, :], GU[1][:, k * TOK:(k + 1) * TOK], nwm[:, 0, k:k + 1],
                                             hT1[:, 0, k, :].bitcast(f32), ALU.mult, ALU.subtract).then_inc(xT1_lo.sem, 1)

            def out_chunk(b, t):
                k = 2 * t
                wait(dve, rv_pe, b, 4 * (t + 1))
                dve.tensor_reduce(o_tok[:, t, :].rearrange("p (h d) -> p h d", h=H),
                                  X[2 + t][:, :].rearrange("p (h l d) -> p h d l", h=H, l=2), AX.X, ALU.add).then_inc(o_vec.sem, 1)
                wait(dve, o_vec, b, k + 1)
                if t:
                    dve.tensor_tensor(o_tok[:, 1, :], o_tok[:, 1, :], cross, ALU.add).then_inc(o_vec.sem, 1)
                    wait(dve, o_vec, b, k + 2)
                elif not is_first(b):
                    wait(dve, oT_pe, b - 1, 1)
                dve.tensor_tensor(og[:, t, :], o_tok[:, t, :], nw_b[:, :], ALU.mult).then_inc(o_vec.sem, 1)

            def out_lo(b):
                for k in range(KT):
                    wait(dve, oT_hi, b, KT)
                    dve.scalar_tensor_tensor(oT[:, 1, k, :], X[2][:, k * TOK:(k + 1) * TOK], nwm[:, 1, k:k + 1],
                                             oT[:, 0, k, :].bitcast(f32), ALU.mult, ALU.subtract).then_inc(oT_lo.sem, 1)

            def add_experts(b):
                wait(dve, dn1_pe, b, NT1 + 1)
                dve.tensor_tensor(tokens_of(b), tokens_of(b), OB[:, :].rearrange("p (t d) -> p t d", t=TT), ALU.add).then_inc(res1_vec.sem, 1)

            def add_projection(b):
                wait(dve, proj_pe, b, 1)
                wait(dve, o_pool, b, 7)
                wait(dve, res1_vec, b, 1)
                for t in range(TT):
                    dve.scalar_tensor_tensor(tokens_of(b)[:, t, :], X[3][:, t * D:(t + 1) * D], ra[:, t:t + 1], tokens_of(b)[:, t, :],
                                             ALU.mult, ALU.add).then_inc(res1_vec.sem, 1)

            token_stats(0)
            normalise(0)
            for b in range(NB):
                if b == 0:
                    dve.wait_ge(prep_pe.sem, 1)
                    dve.wait_ge(prep_pool.sem, PREP_POOL)
                    gsrc = X[3][:, 0:2 * 16].rearrange("p (k n) -> p k n", k=KT)[:, :, 0:GATES]
                    dve.tensor_copy(wqkv[:, 0, :, QKV:NQ], gsrc).then_inc(prep_vec.sem, 1)
                    dve.wait_ge(prep_vec.sem, PREP_VEC - 1)
                    dve.tensor_tensor(wqkv[:, 1, :, QKV:NQ], gsrc, wqkv[:, 0, :, QKV:NQ].bitcast(f32), ALU.subtract).then_inc(prep_vec.sem, 1)
                    tokens_lo(0)
                for t in range(TT):
                    wait(dve, qkv_pe, b, t + 1)
                    if b:
                        wait(dve, rope_pool, b - 1, TT)
                        wait(dve, pT_pe, b - 1, 2 * NPAIR)
                    n = H + HKV
                    half = DH // 2
                    qk = X[1 + t][:, 0:n * DH].rearrange("p (h s d) -> p h s d", h=n, s=2)
                    tab = const("rope").rearrange("p (t c d) -> p t c d", t=TT, c=3)
                    a = rope_at(t, 0).rearrange("p (h d) -> p h d", h=2 * n)
                    bb = rope_at(t, 1).rearrange("p (h s d) -> p h s d", h=n, s=2)
                    dve.tensor_tensor(a, X[1 + t][:, 0:n * DH].rearrange("p (h d) -> p h d", h=2 * n),
                                      tab[:, t, 0, :].unsqueeze(1).broadcast_to([P, 2 * n, half]), ALU.mult).then_inc(rope_vec.sem, 1)
                    for s in range(2):
                        dve.tensor_tensor(bb[:, :, s, :], qk[:, :, 1 - s, :],
                                          tab[:, t, 1 + s, :].unsqueeze(1).broadcast_to([P, n, half]), ALU.mult).then_inc(rope_vec.sem, 1)
                for t in range(TT):
                    dve.tensor_copy(lg[:, t, :], X[1 + t][:, QKV:NQ]).then_inc(route_vec.sem, 1)
                for t in range(TT):
                    wait(dve, route_vec, b, t + 1)
                    dve.max(top[:, t, :], lg[:, t, 0:8]).then_inc(route_vec.sem, 1)
                for t in range(TT):
                    wait(dve, route_vec, b, TT + t + 1)
                    dve.max_index(top_ix[:, t, :], top[:, t, :], lg[:, t, 0:8]).then_inc(route_vec.sem, 1)

                def v_split():
                    if b:
                        wait(dve, pv_pe, b - 1, NPAIR)
                    vp = [X[1 + t][:, H * DH + HKV * DH:QKV].rearrange("p (g d) -> p g d", g=HKV) for t in range(TT)]
                    va = [vr[:, t, 0, :].rearrange("p (g d) -> p g d", g=HKV) for t in range(TT)]
                    vb = [vr[:, t, 1, :].rearrange("p (g d) -> p g d", g=HKV) for t in range(TT)]
                    for t in range(TT):
                        dve.tensor_copy(v3[:, t, :, 0, :], vp[t]).then_inc(v_vec.sem, 1)
                    for t in range(TT):
                        wait(dve, v_vec, b, t + 1)
                        dve.tensor_tensor(va[t], vp[t], v3[:, t, :, 0, :], ALU.subtract).then_inc(v_vec.sem, 1)
                    for t in range(TT):
                        wait(dve, v_vec, b, TT + t + 1)
                        dve.tensor_copy(v3[:, t, :, 1, :], va[t]).then_inc(v_vec.sem, 1)
                    for t in range(TT):
                        wait(dve, v_vec, b, 2 * TT + t + 1)
                        dve.tensor_tensor(vb[t], va[t], v3[:, t, :, 1, :], ALU.subtract).then_inc(v_vec.sem, 1)
                    for t in range(TT):
                        wait(dve, v_vec, b, 3 * TT + t + 1)
                        dve.tensor_copy(v3[:, t, :, 2, :], vb[t]).then_inc(v_vec.sem, 1)

                if b == 1:
                    dve.wait_ge(small_pe.sem, 1)
                    dve.tensor_copy(cols[:, :], X[3][:, 64:64 + 18]).then_inc(small_vec.sem, 1)
                if b == 2:
                    dve.wait_ge(tern_pe.sem, 1)
                    dve.tensor_copy(abs_sum[:, :], X[3][:, 0:3]).then_inc(tern_vec.sem, 1)
                    dve.wait_ge(tern_vec.sem, 4)
                    dve.tensor_tensor(w_mean[:, 0:1], abs_sum[:, 0:1], abs_sum[:, 1:2], ALU.add).then_inc(tern_vec.sem, 1)
                    dve.wait_ge(tern_vec.sem, 5)
                    dve.tensor_scalar(w_mean[:, 0:1], w_mean[:, 0:1], 1.0 / (3 * D * D), 1e-5, ALU.mult, ALU.max).then_inc(tern_vec.sem, 1)
                    dve.tensor_scalar(w_mean[:, 1:2], abs_sum[:, 2:3], 1.0 / (D * D), 1e-5, ALU.mult, ALU.max).then_inc(tern_vec.sem, 1)
                    dve.wait_ge(tern_vec.sem, 7)
                    dve.reciprocal(w_inv[:, :], w_mean[:, :]).then_inc(tern_vec.sem, 1)
                    dve.wait_ge(small_vec.sem, 3)
                    for n in range(2):
                        dve.tensor_scalar(nwm[:, n, :], cols[:, 14 + 2 * n:16 + 2 * n], w_mean[:, n:n + 1], None, ALU.mult).then_inc(small_vec.sem, 1)
                for t in range(TT):
                    q4 = stack[:, t, 0:H * 64].rearrange("p (h r d) -> p h r d", h=H, r=4)
                    k4 = stack[:, t, H * 64:].rearrange("p (h r l d) -> p h r l d", h=HKV, r=2, l=2)
                    rq = rot[:, t, 0:H * DH].rearrange("p (h d) -> p h d", h=H).unsqueeze(2).broadcast_to([P, H, 2, DH])
                    rk = rot[:, t, H * DH:].rearrange("p (h d) -> p h d", h=HKV).unsqueeze(2).broadcast_to([P, HKV, 2, DH])
                    wait(dve, stack_hi, b, 2 * t + 2)
                    dve.tensor_tensor(q4[:, :, 2:4, :], rq, q4[:, :, 0:2, :].bitcast(f32), ALU.subtract).then_inc(stack_lo.sem, 1)
                    dve.tensor_tensor(k4[:, :, :, 1, :], rk, k4[:, :, :, 0, :].bitcast(f32), ALU.subtract).then_inc(stack_lo.sem, 1)
                if b == 0:
                    dve.wait_ge(small_in.sem, SMALL_IN)
                    dve.tensor_scalar(ns_b[:, :], s_b[:, :], -1.0, None, ALU.mult).then_inc(decay_vec.sem, 1)
                    dve.tensor_copy(bias_w[:, 0, :], bias_f[:, :]).then_inc(small_vec.sem, 1)
                    dve.wait_ge(small_vec.sem, 1)
                    dve.tensor_tensor(bias_w[:, 1, :], bias_f[:, :], bias_w[:, 0, :].bitcast(f32), ALU.subtract).then_inc(small_vec.sem, 1)
                v_split()
                if b:
                    residual(b - 1)
                if b == NB - 1:
                    dve.wait_ge(decay_act.sem, 2 + H)
                    dve.tensor_tensor(dm[:, :, :], dm[:, :, :], const("decay")[:, P:2 * P].unsqueeze(1).broadcast_to([P, H, P]), ALU.mult).then_inc(decay_vec.sem, 1)
                    dve.tensor_scalar(lam[:, 0, :], lam[:, 0, :], DH ** -0.5, None, ALU.mult).then_inc(decay_vec.sem, 1)
                wait(dve, cwT_pe, b, 1)
                if b:
                    wait(dve, cb_pe, b - 1, NT0)
                dve.tensor_copy(cwT[:, :], CB[:, 0:TOK]).then_inc(cwT_vec.sem, 1)
                for i in range(NT0):
                    if i == NORM_SLOT:
                        token_stats(b + 1) if b + 1 < NB else token_stats1(0)
                    if i == NT0 - 1 and b + 1 < NB:
                        tokens_lo(b + 1)
                    if 3 <= i < 3 + NPAIR:
                        p = i - 3
                        wait(dve, pv_pe, b, p + 1)
                        src = X[3][:, 0:4 * 3 * DH].rearrange("p (q j d) -> p q d j", q=4, j=3)
                        dve.tensor_reduce(y[:, p, :, :], src, AX.X, ALU.add).then_inc(y_vec.sem, 1)
                    if 1 <= i < 1 + NPAIR:
                        p = i - 1
                        if p >= 2:
                            wait(dve, exp_act, b, 4 * (p - 1))
                        elif b:
                            wait(dve, exp_act, b - 1, 4 * (NPAIR - 1 + p))
                        if p == 1:
                            wait(dve, xT_pe, b, 1)
                            if b:
                                wait(dve, yT_pe, b - 1, 1)
                        for t in range(TT):
                            wait(dve, score_pe, b, 2 * p + t + 1)
                            for r in range(2):
                                n = (t + 1) * P
                                at = r * P if t == 0 else TOK + r * TOK
                                dve.tensor_tensor_reduce(out=sm_at(p)[:, at:at + n], in0=X[t][:, r * n:(r + 1) * n],
                                                         in1=const("mask")[:, 2 * P - n:2 * P], scale=-(DH ** -0.5), scalar=3.0e38,
                                                         op0=ALU.add, op1=ALU.min,
                                                         accum_out=nmax[:, p % 2, 2 * t + r:2 * t + r + 1]).then_inc(max_vec.sem, 1)
                    m = tile_rows(i)
                    wait(dve, tanh_act, b, i + 1)
                    dve.scalar_tensor_tensor(th[0:m, i % 2, :], th[0:m, i % 2, :], 1.0, GU[i % 2][0:m, 0:TOK],
                                         ALU.add, ALU.mult).then_inc(ffn_vec.sem, 1)
                    if 2 <= i < 2 + NPAIR:
                        p = i - 2
                        wait(dve, pT_hi, b, 2 * p + 1)
                        dve.tensor_tensor(pT[:, 1, TOK:3 * TOK], X[2][:, :], pT[:, 0, TOK:3 * TOK], ALU.subtract).then_inc(pT_lo.sem, 1)
                    if 2 <= i < 2 + NPAIR:
                        p = i - 2
                        wait(dve, pT_hi, b, 2 * p + 2)
                        dve.tensor_tensor(pT[:, 1, 0:TOK], X[3][:, TOK:2 * TOK], pT[:, 0, 0:TOK], ALU.subtract).then_inc(pT_lo.sem, 1)
                    wait(dve, ffn_vec, b, 3 * i + 1)
                    dve.tensor_tensor(s2[0:m, i % 2, :], th[0:m, i % 2, :], GU[i % 2][0:m, TOK:2 * TOK], ALU.mult).then_inc(ffn_vec.sem, 1)
                    wait(dve, ffn_vec, b, 3 * i + 2)
                    wait(dve, cb_pe, b, i + 1)
                    if i >= 2:
                        wait(dve, h_lo, b, i - 1)
                    elif b:
                        wait(dve, h_lo, b - 1, NT0 - 1 + i)
                    dve.tensor_tensor(hs[0:m, i % 2, :], s2[0:m, i % 2, :], CB[0:m, 0:TOK], ALU.mult).then_inc(ffn_vec.sem, 1)
                    if i == 10:
                        wait(dve, exp_act, b, 4 * NPAIR)
                        dve.reciprocal(rinv[:, :], rs[:, :]).then_inc(yn_vec.sem, 1)
                        wait(dve, yn_vec, b, 1)
                        wait(dve, y_vec, b, NPAIR)
                        for t in range(TT):
                            r4 = rinv[:, :].rearrange("p (q t r) -> p q t r", q=NPAIR, t=TT)
                            y5 = y[:, :, :, :].rearrange("p q (t r) d -> p q t r d", t=TT)
                            dve.tensor_tensor(yn[:, t, :].rearrange("p (q r d) -> p q r d", q=NPAIR, r=2), y5[:, :, t, :, :],
                                              r4[:, :, t, :].unsqueeze(3).broadcast_to([P, NPAIR, 2, DH]), ALU.mult).then_inc(yn_vec.sem, 1)
                    if i == 11:
                        wait(dve, yT_hi, b, 1)
                        dve.tensor_tensor(yT[:, 1, :, :], X[0][:, :].rearrange("p (k n) -> p k n", k=KT),
                                          yT[:, 0, :, :].bitcast(f32), ALU.subtract).then_inc(yT_lo.sem, 1)
                    if i == NORM_SLOT + 1:
                        normalise(b + 1) if b + 1 < NB else normalise1(0)
                    if b == 1 and 10 <= i < 13:
                        n = i - 10
                        slot, landed = pieces[f"tern{n}"][0:2]
                        dve.wait_ge(stage_in[slot].sem, landed)
                        dve.tensor_reduce(abs_sum[:, n:n + 1], stage[:, slot, 0:(3, 3, 2)[n] * D], AX.X, ALU.add,
                                          apply_absolute_value=True).then_inc(tern_vec.sem, 1)

            tokens1_lo(0)
            residual(NB - 1)
            def layer1_batch(b):
                def pad_queries(j):
                    t, g = divmod(j, 2)
                    wait(dve, ret_pe, b, 2 * (j - 1))
                    dve.tensor_tensor(q_pad(j)[:, 0, :, :], qT1[:, 0, g, t * P:(t + 1) * P].bitcast(f32).unsqueeze(1).broadcast_to([P, 8, P]),
                                      const("block").unsqueeze(2).broadcast_to([P, 8, P]), ALU.mult).then_inc(pad_hi.sem, 1)

                k = 0

                def rstep(ins):
                    nonlocal k
                    k += 1
                    ins.then_inc(route1_vec.sem, 1)

                wait(dve, route1_pe, b, TT)
                for t in range(TT):
                    rstep(dve.tensor_tensor(lg1[:, t, :], CB[:, 16 * t:16 * t + 8], bg_b[:, :], ALU.add))
                wait(dve, route1_vec, b, k)
                for t in range(TT):
                    rstep(dve.tensor_tensor(lg1[:, t, :], CB[:, 16 * t + 8:16 * t + 16], lg1[:, t, :], ALU.add))
                wait_apart(dve, route1_vec, b, k)
                for t in range(TT):
                    rstep(dve.max(top[:, t, :], lg1[:, t, :]))
                wait_apart(dve, route1_vec, b, k)
                for t in range(TT):
                    rstep(dve.max_index(top_ix[:, t, :], top[:, t, :], lg1[:, t, :]))
                wait(dve, kv1_pe, b, 1)
                if not is_first(b):
                    wait(dve, kd_lo, b - 1, 1)
                dve.tensor_tensor(kdf.rearrange("p (h d) -> p h d", h=H), X[0][:, 0:D].rearrange("p (h d) -> p h d", h=H),
                                  lam[:, 1, :].unsqueeze(2).broadcast_to([P, H, DH]), ALU.mult).then_inc(kd_vec.sem, 1)
                for t in range(TT):
                    wait(dve, v1_hi, b, t + 1)
                    src = X[t][:, D:2 * D] if t == 0 else X[t][:, 0:D]
                    dve.tensor_tensor(v2[:, t, :, 1, :], src.rearrange("p (h d) -> p h d", h=H), v2[:, t, :, 0, :].bitcast(f32),
                                      ALU.subtract).then_inc(v1_lo.sem, 1)
                wait(dve, kd_hi, b, 1)
                dve.tensor_tensor(kd[:, 1, :], kdf, kd[:, 0, :].bitcast(f32), ALU.subtract).then_inc(kd_lo.sem, 1)
                for n, dst in enumerate((qT1, kT1)):
                    wait(dve, qk1_hi, b, n + 1)
                    dve.tensor_tensor(dst[:, 1, :, :], X[2 + n][:, :].rearrange("p (g n) -> p g n", g=2),
                                      dst[:, 0, :, :].bitcast(f32), ALU.subtract).then_inc(qk1_lo.sem, 1)
                wait(dve, route1_pool, b, 2)
                for n in range(2):
                    for t in range(TT):
                        wait(dve, route1_act, b, t + 1)
                        rstep(dve.scalar_tensor_tensor(em[:, n, t, :], const("iota"), ixf[:, t, 6 + n:7 + n], e1[:, t, :] if n == 0 else em[:, 0, t, :],
                                                       ALU.not_equal, ALU.mult))
                    wait(dve, route1_vec, b, k)
                rstep(dve.tensor_reduce(esum[:, :], em[:, 1, :, :], AX.X, ALU.add))
                wait(dve, route1_vec, b, k)
                rstep(dve.reciprocal(erec[:, :], esum[:, :]))
                wait(dve, route1_vec, b, k)
                rstep(dve.tensor_tensor(c1[:, :, 0:R1], em[:, 1, :, 0:R1], erec[:, :].unsqueeze(2).broadcast_to([P, TT, R1]), ALU.mult))
                wait(dve, route1_vec, b, k)
                if not is_first(b):
                    wait(dve, cw1_pe, b - 1, 1)
                rstep(dve.tensor_copy(cw[:, :, 0:R1], c1[:, :, 0:R1]))
                wait(dve, route1_vec, b, k)
                rstep(dve.tensor_tensor(cw[:, :, 16:16 + R1], c1[:, :, 0:R1], cw[:, :, 0:R1].bitcast(f32), ALU.subtract))
                assert k == route1_vec.per, k
                if is_first(b):
                    dve.memset(cw[:, :, R1:R1 + 1].bitcast(f32), 1.0).then_inc(small_vec.sem, 1)
                wait(dve, state_pe, b, 1)
                if not is_first(b):
                    wait(dve, state_lo, b - 1, 1)
                dve.tensor_tensor(stf.rearrange("p (g h d) -> p g h d", g=2, h=8), X[0][:, 0:2 * P].rearrange("p (g h d) -> p g h d", g=2, h=8),
                                  const("block").unsqueeze(1).unsqueeze(3).broadcast_to([P, 2, 8, DH]), ALU.mult).then_inc(state_vec.sem, 1)
                wait(dve, state_hi, b, 1)
                dve.tensor_tensor(state[:, 1, :, :].rearrange("p g n -> p (g n)"), stf, state[:, 0, :, :].rearrange("p g n -> p (g n)").bitcast(f32),
                                  ALU.subtract).then_inc(state_lo.sem, 1)
                wait(dve, cw1_pe, b, 1)
                if not is_first(b):
                    wait(dve, cb1_pe, b - 1, R1)
                    wait(dve, dn1_pe, b - 1, NT1 + 1)
                dve.tensor_copy(cwT[:, :], CB[:, 0:TOK]).then_inc(cw1_vec.sem, 1)

                if not is_first(b):
                    out_lo(b - 1)
                wait(dve, cross_pe, b, 1)
                dve.tensor_tensor(cross.rearrange("p (h d) -> p h d", h=H), X[1][:, 0:D].rearrange("p (h d) -> p h d", h=H),
                                  lam[:, 0, :].unsqueeze(2).broadcast_to([P, H, DH]), ALU.mult).then_inc(cross_vec.sem, 1)
                for u in range(8):
                    if u == 0 and not is_first(b):
                        add_experts(b - 1)
                    if u == 1 and not is_first(b):
                        add_projection(b - 1)
                    if u < R1:
                        wait(dve, silu_act, b, u + 1)
                        dve.scalar_tensor_tensor(s2[:, u % 2, :], GU[u % 2][:, TOK:2 * TOK], cols[:, 6 + u:7 + u], th[:, u % 2, :],
                                                 ALU.add, ALU.mult).then_inc(ffn1_vec.sem, 1)
                    wait(dve, ret_pe, b, u + 1)
                    if u >= 2:
                        wait(dve, ret_lo, b, u - 1)
                    elif not is_first(b):
                        wait(dve, ret_lo, b - 1, 7 + u)
                    h0 = (u // 2 % 2) * 8 + (u % 2) * 4
                    dve.tensor_tensor(af_at(u).rearrange("p (h n) -> p h n", h=4), X[u % 2][:, :].rearrange("p (h n) -> p h n", h=4),
                                      dm[:, h0:h0 + 4, :], ALU.mult).then_inc(ret_vec.sem, 1)
                    if u < R1:
                        wait(dve, ffn1_vec, b, 2 * u + 1)
                        wait(dve, cb1_pe, b, u + 1)
                        if u >= 2:
                            wait(dve, h1_lo, b, u - 1)
                        elif not is_first(b):
                            wait(dve, h1_lo, b - 1, NT1 - 1 + u)
                        else:
                            wait(dve, h_lo, NB - 1, NT0 - 1 + u)
                        dve.tensor_tensor(hs[:, u % 2, :], s2[:, u % 2, :], CB[:, 0:TOK], ALU.mult).then_inc(ffn1_vec.sem, 1)
                    wait(dve, ret_hi, b, u + 1)
                    dve.tensor_tensor(aT[:, u % 2, 1, :], af_at(u), aT[:, u % 2, 0, :].bitcast(f32), ALU.subtract).then_inc(ret_lo.sem, 1)
                    if u in (2, 4):
                        pad_queries(u // 2 + 1)
                    if u == 7:
                        out_chunk(b, 0)
                    if not is_last(b):
                        if u == 1:
                            token_stats1(b + 1)
                        elif u == 3:
                            normalise1(b + 1)
                        elif u == 7:
                            tokens1_lo(b + 1)
                out_chunk(b, 1)

            batches(dve, layer1_batch)
            add_experts(NB - 1)
            out_lo(NB - 1)
            add_projection(NB - 1)

        @block.tensor
        def _(pe):
            PASSES = ((0, 0), (1, 0), (0, 1))
            pe.wait_ge(cst_in.sem, 16)
            pe.wait_ge(gates_in.sem, 48)
            for k in range(KT):
                mm = pe.transpose(X[3][:, 16 * k:16 * k + GATES], gates_nat[:, k * P:(k + 1) * P], ident[0:GATES, 0:GATES])
            mm.then_inc(prep_pe.sem, 1)

            opened = [False]

            def add_to_out(t, lhsT, rhs):
                mm = pe.matmul(OB[:, t * D:(t + 1) * D], lhsT, rhs, start=not opened[0], stop=True,
                               skip_group_check=opened[0])
                opened[0] = True
                return mm

            def transpose_tokens(b):
                wait(pe, norm_vec, b, TT)
                if b:
                    wait(pe, max_vec, b - 1, 4 * NPAIR)
                for k in range(KT):
                    for t in range(TT):
                        mm = pe.transpose(X[1][:, k * TOK + t * P:k * TOK + (t + 1) * P], xn[:, t, k * P:(k + 1) * P], ident)
                mm.then_inc(xT_pe.sem, 1)

            def down(b, i):
                m = tile_rows(i)
                if i == 0:
                    opened[0] = False
                wait(pe, h_lo, b, i + 1)
                if b == 0:
                    weights_ready(pe, *dn_needs(i))
                elif i == 0:
                    wait(pe, res_vec, b - 1, 1)
                for t in range(TT):
                    for l, r in PASSES:
                        mm = add_to_out(t, hT[0:m, i % 2, l, t * P:(t + 1) * P], dn_w[0:m, i, r, :])
                mm.then_inc(dn_pe.sem, 1)

            transpose_tokens(0)
            for b in range(NB):
                wait(pe, xT_lo, b, 1)
                if b == 0:
                    weights_ready(pe, "qkv")
                    pe.wait_ge(prep_vec.sem, PREP_VEC)
                else:
                    wait(pe, pT_lo, b - 1, 2 * NPAIR)
                    wait(pe, max_vec, b - 1, 4 * NPAIR)
                for t in range(TT):
                    for n, (l, r) in enumerate((PASSES[m][0], PASSES[m][1]) for m in range(3)):
                        for k in range(KT):
                            mm = pe.matmul(X[1 + t][:, 0:NQ], xT[:, l, k, t * P:(t + 1) * P], wqkv[:, r, k, :],
                                           start=(n == 0 and k == 0), stop=(n == 2 and k == KT - 1))
                    mm.then_inc(qkv_pe.sem, 1)

                if b == 1:
                    pe.wait_ge(small_in.sem, SMALL_IN)
                    wait(pe, y_vec, b - 1, NPAIR)
                    pe.transpose(X[3][:, 64:64 + 18], small_rows[:, :], ident[0:18, 0:18]).then_inc(small_pe.sem, 1)
                if b:
                    down(b - 1, NT0 - 1)

                def transpose_ternary(first):
                    pe.wait_ge(tern_round.sem, TERN_ROUND)
                    wait(pe, y_vec, b - 1, NPAIR)
                    for n in range(first, first + 2):
                        if n >= 2:
                            pe.wait_ge(tern_act.sem, n - 1)
                        for m in range(4):
                            r, k = divmod(m, 2)
                            r += 2 * (n % 3)
                            name, row = ("tern2", r) if n == 3 else (f"tern{r // 3}", r % 3)
                            mm = pe.transpose(X[3 if n % 2 == 0 else 0][:, m * P:(m + 1) * P],
                                              stage[:, slot_of[name], row * D + k * P:row * D + (k + 1) * P], ident)
                        mm.then_inc(tern_pe.sem, 1)

                def gate_up(i):
                    m = tile_rows(i)
                    if b == 0:
                        weights_ready(pe, *gu_needs(i))
                    if i >= 2:
                        wait(pe, ffn_vec, b, 3 * (i - 2) + 2)
                    elif b:
                        wait(pe, ffn_vec, b - 1, 3 * (NT0 - 2 + i) + 2)
                    for g in range(2):
                        for n, (l, r) in enumerate(PASSES):
                            for k in range(KT):
                                mm = pe.matmul(GU[i % 2][0:m, g * TOK:(g + 1) * TOK], gu_w[:, i, l, 2 * g + k, 0:m], xT[:, r, k, :],
                                               start=(n == 0 and k == 0), stop=(n == 2 and k == KT - 1))
                    mm.then_inc(gu_pe.sem, 1)

                def spread_weights(i):
                    m = tile_rows(i)
                    wait(pe, cwT_vec, b, 1)
                    if b == 0:
                        pe.wait_ge(w_hi.sem, need[f"sp{i * P // 768}"][0])
                    if i:
                        wait(pe, ffn_vec, b, 3 * i)
                    pe.matmul(CB[0:m, 0:TOK], spread[:, i * P:i * P + m], cwT[:, :], start=True, stop=True).then_inc(cb_pe.sem, 1)

                def scores(p):
                    gp = p // 4
                    if p:
                        wait(pe, max_vec, b, 4 * p)
                    else:
                        wait(pe, qkT_act, b, 6)
                        wait(pe, v_vec, b, 5 * TT)
                        wait(pe, rope_vec, b, 3 * TT)
                        wait(pe, route_vec, b, 3 * TT)
                    for t in range(TT):
                        n = (t + 1) * P
                        pe.matmul(X[t][:, 0:2 * n], qT[:, p, t * P:(t + 1) * P], kTz[:, gp, :, 0:n],
                                  start=True, stop=True).then_inc(score_pe.sem, 1)

                def prob_transposes(p, t):
                    if t == 1:
                        wait(pe, exp_act, b, 4 * p + 4)
                        if p:
                            wait(pe, pT_lo, b, 2 * p - 1)
                    else:
                        if p:
                            wait(pe, y_vec, b, p)
                    n = 0
                    for r in range(2):
                        for s in range(t + 1):
                            at = (r * P if t == 0 else TOK + r * TOK) + s * P
                            mm = pe.transpose(X[2][:, n * P:(n + 1) * P] if t else X[3][:, (2 + n) * P:(3 + n) * P], pm[:, p % 2, at:at + P], ident)
                            n += 1
                    mm.then_inc(pT_pe.sem, 1)

                def prob_values(p):
                    gp = p // 4
                    wait(pe, pT_lo, b, 2 * p + 2)
                    if p:
                        wait(pe, y_vec, b, p)
                    first = True
                    for t in range(TT):
                        for r in range(2):
                            q = 2 * t + r
                            o = X[3][:, q * 3 * DH:(q + 1) * 3 * DH]
                            for s in range(t + 1):
                                at = (r * P if t == 0 else TOK + r * TOK) + s * P
                                vv = v3[:, s, 2 * gp + r, :, :].rearrange("p j d -> p (j d)")
                                for l in range(2):
                                    mm = pe.matmul(o, pT[:, l, at:at + P], vv, start=first, stop=True, skip_group_check=not first)
                                    first = False
                    mm.then_inc(pv_pe.sem, 1)

                if b == NB - 1:
                    transpose_ternary(0)
                gate_up(0)
                if b == NB - 1:
                    transpose_ternary(2)
                    pe.wait_ge(tern_act.sem, 4)
                gate_up(1)
                wait(pe, stack_lo, b, 2 * TT)
                if b:
                    wait(pe, y_vec, b - 1, NPAIR)
                else:
                    pe.wait_ge(prep_vec.sem, PREP_VEC)
                if b == 1:
                    pe.wait_ge(small_vec.sem, 3)
                if b == 2:
                    pe.wait_ge(tern_vec.sem, 4)
                for n in range(4):
                    t, half = divmod(n, 2)
                    if n >= 2:
                        wait(pe, qkT_act, b, n - 1)
                    for m in range(4):
                        at = (4 * half + m) * P
                        mm = pe.transpose(X[3 if n % 2 == 0 else 0][:, m * P:(m + 1) * P], stack[:, t, at:at + P].bitcast(f32), ident)
                    mm.then_inc(qkT_pe.sem, 1)
                wait(pe, route_pool, b, route_pool.per)
                if b:
                    wait(pe, ffn_vec, b - 1, 3 * NT0)
                else:
                    pe.wait_ge(prep_pool.sem, PREP_POOL)
                for t in range(TT):
                    mm = pe.transpose(CB[:, t * P:(t + 1) * P], cw[:, t, :].bitcast(f32), ident)
                mm.then_inc(cwT_pe.sem, 1)
                wait(pe, qkT_act, b, 3)
                for t in range(TT):
                    for g in range(2):
                        at = H * 64 + g * P
                        mm = pe.transpose(X[3][:, (2 * t + g) * P:(2 * t + g + 1) * P], stack[:, t, at:at + P].bitcast(f32), ident)
                mm.then_inc(qkT_pe.sem, 1)
                for i in range(NT0):
                    if 2 <= i < 2 + NPAIR:
                        prob_transposes(i - 2, 1)
                    spread_weights(i)
                    if 2 <= i < 2 + NPAIR:
                        prob_transposes(i - 2, 0)
                    if i + 1 < NT0 and i:
                        gate_up(i + 1)
                    if i < NPAIR:
                        scores(i)
                    if i == 11:
                        wait(pe, yn_vec, b, 1 + TT)
                        for k in range(KT):
                            for t in range(TT):
                                mm = pe.transpose(X[0][:, k * TOK + t * P:k * TOK + (t + 1) * P], yn[:, t, k * P:(k + 1) * P], ident)
                        mm.then_inc(yT_pe.sem, 1)
                    if i == 12 and b + 1 < NB:
                        transpose_tokens(b + 1)
                    if i >= 1:
                        down(b, i - 1)
                    if 2 <= i < 2 + NPAIR:
                        prob_values(i - 2)
                wait(pe, yT_lo, b, 1)
                if b == 0:
                    weights_ready(pe, "wo")
                for t in range(TT):
                    for l, r in PASSES:
                        for k in range(KT):
                            mm = add_to_out(t, yT[:, l, k, t * P:(t + 1) * P], wo_r[:, r, k, :])
                mm.then_inc(wo_pe.sem, 1)
                if b == 1:
                    pe.wait_ge(tern_vec.sem, 3)
                    wait(pe, y_vec, b, NPAIR)
                    pe.matmul(X[3][:, 0:3], ones[:, :], abs_sum[:, :], start=True, stop=True).then_inc(tern_pe.sem, 1)

            HALVES = (0, 1)

            def transpose_tokens1(b, k1):
                wait(pe, norm1_vec, b, (k1 + 1) * TT)
                if not is_first(b):
                    wait(pe, silu_act, b - 1, NT1 - 1 + k1)
                else:
                    wait(pe, ffn_vec, NB - 1, 3 * (NT0 - 2 + k1) + 2)
                src = (xn, yn)[k1]
                for k in range(KT):
                    for t in range(TT):
                        mm = pe.transpose(GU[k1][:, k * TOK + t * P:k * TOK + (t + 1) * P], src[:, t, k * P:(k + 1) * P], ident)
                mm.then_inc(xT1_pe.sem, 1)

            def project(b, half):
                if half == 0:
                    wait(pe, o_vec, b, 5)
                    for k in range(KT):
                        for t in range(TT):
                            mm = pe.transpose(X[2][:, k * TOK + t * P:k * TOK + (t + 1) * P], og[:, t, k * P:(k + 1) * P], ident)
                    mm.then_inc(oT_pe.sem, 1)
                else:
                    wait(pe, oT_lo, b, KT)
                    for t in range(TT):
                        for l in HALVES:
                            for k in range(KT):
                                mm = pe.matmul(X[3][:, t * D:(t + 1) * D], oT[:, l, k, t * P:(t + 1) * P], proj_t[:, k, :],
                                               start=l == 0 and k == 0, stop=l == 1 and k == KT - 1)
                    mm.then_inc(proj_pe.sem, 1)

            transpose_tokens1(0, 0)
            transpose_tokens1(0, 1)
            down(NB - 1, NT0 - 1)
            def layer1_batch(b):
                def gate_up(i):
                    if i < 2:
                        wait(pe, xT1_lo, b, 1 if i == 0 else 1 + KT)
                    if is_first(b):
                        weights_ready(pe, f"x{i}" if i < R1 else "xup")
                    if i >= 2:
                        wait(pe, ffn1_vec, b, 2 * (i - 2) + 1)
                    for g in range(2 if i < R1 else 1):
                        for n, (l, r) in enumerate(PASSES):
                            for k in range(KT):
                                w = gu1_w(i)[:, l, 2 * g + k, :] if i < R1 else up1_w(i - R1)[:, l, k, :]
                                mm = pe.matmul(GU[i % 2][:, g * TOK:(g + 1) * TOK], w, xT[:, r, k, :],
                                               start=(n == 0 and k == 0), stop=(n == 2 and k == KT - 1))
                    mm.then_inc(gu1_pe.sem, 1)

                gate_up(0)
                if not is_first(b):
                    wait(pe, ffn1_vec, b - 1, 2 * R1)
                else:
                    wait(pe, ffn_vec, NB - 1, 3 * NT0)
                    weights_ready(pe, "router")
                for t in range(TT):
                    for m, (l, k) in enumerate((l, k) for l in HALVES for k in range(KT)):
                        mm = pe.matmul(CB[:, 16 * t:16 * t + 16], xT[:, l, k, t * P:(t + 1) * P], router_w[:, k, :, :].rearrange("p l n -> p (l n)"),
                                       start=m == 0, stop=m == 3)
                    mm.then_inc(route1_pe.sem, 1)
                wait(pe, xT1_lo, b, 1 + KT)
                if not is_first(b):
                    wait(pe, ret_vec, b - 1, 8)
                for t in range(TT):
                    c0, n = (D, 2 * D) if t == 0 else (2 * D, D)
                    for m, (l, k) in enumerate((l, k) for l in HALVES for k in range(KT)):
                        mm = pe.matmul(X[t][:, 0:n], hT1[:, l, k, t * P:(t + 1) * P], qkv_t[:, k, c0:c0 + n], start=m == 0, stop=m == 3)
                    mm.then_inc(kv1_pe.sem, 1)

                def spread_weights(i):
                    wait(pe, cw1_vec, b, 1)
                    if is_first(b):
                        pe.wait_ge(w_hi.sem, need["sp3"][0])
                    if i:
                        wait(pe, ffn1_vec, b, 2 * i)
                    pe.matmul(CB[:, 0:TOK], spread[:, NT0 * P + i * P:NT0 * P + (i + 1) * P], cwT[:, :], start=True, stop=True).then_inc(cb1_pe.sem, 1)

                def down1(i):
                    wait(pe, h1_lo, b, i + 1)
                    if is_first(b):
                        weights_ready(pe, f"x{i}" if i < R1 else "xdn")
                        if i == 0:
                            wait(pe, res_vec, NB - 1, 1)
                    elif i == 0:
                        wait(pe, res1_vec, b - 1, 1)
                    if i == 0:
                        opened[0] = False
                    for t in range(TT):
                        for l, r in PASSES:
                            mm = add_to_out(t, hT[:, i % 2, l, t * P:(t + 1) * P], dn1_w(i)[:, r, :])
                    mm.then_inc(dn1_pe.sem, 1)

                def retention_scores(u):
                    t, g, half = u // 4, u // 2 % 2, u % 2
                    if u < 4:
                        wait(pe, pad_first, b, u // 2 + 1)
                    else:
                        wait(pe, pad_hi, b, u // 2 - 1)
                    wait(pe, pad_lo, b, u // 2 + 1)
                    wait(pe, qk1_lo, b, 2)
                    if u >= 2:
                        wait(pe, ret_vec, b, u - 1)
                    for m, (l, r) in enumerate(PASSES):
                        mm = pe.matmul(X[u % 2][:, :], kT1[:, l, g, t * P:(t + 1) * P], q_pad(u // 2)[:, r, 4 * half:4 * half + 4, :],
                                       start=m == 0, stop=m == 2)
                    mm.then_inc(ret_pe.sem, 1)

                def retention_values(u):
                    t = u // 4
                    h0 = (u // 2 % 2) * 8 + (u % 2) * 4
                    wait(pe, ret_lo, b, u + 1)
                    if u == 4 and not is_first(b):
                        wait(pe, res1_vec, b - 1, 1 + TT)
                    for hh in range(4):
                        h = h0 + hh
                        for l in HALVES:
                            first = u % 4 == 0 and hh == 0 and l == 0
                            mm = pe.matmul(X[2 + t][:, 2 * DH * h:2 * DH * (h + 1)], aT[:, u % 2, l, hh * P:(hh + 1) * P],
                                           v2[:, t, h, :, :].rearrange("p l d -> p (l d)"), start=first, stop=True, skip_group_check=not first)
                    mm.then_inc(rv_pe.sem, 1)

                wait(pe, xT1_lo, b, 1 + KT)
                if not is_first(b):
                    wait(pe, o_vec, b - 1, 3)
                else:
                    wait(pe, y_vec, NB - 1, NPAIR)
                for n in range(2):
                    for g in range(2):
                        for m, (l, k) in enumerate((l, k) for l in HALVES for k in range(KT)):
                            mm = pe.matmul(X[2 + n][:, g * TOK:(g + 1) * TOK], qkv_t[:, k, n * D + g * P:n * D + (g + 1) * P], hT1[:, l, k, :],
                                           start=m == 0, stop=m == 3)
                    mm.then_inc(qk1_pe.sem, 1)
                gate_up(1)
                if not is_first(b):
                    wait(pe, qk1_lo, b, 1)
                    project(b - 1, 0)
                wait(pe, kd_lo, b, 1)
                wait(pe, v1_lo, b, TT)
                for g in range(2):
                    for m, (l, r) in enumerate(PASSES):
                        mm = pe.matmul(X[0][:, g * P:(g + 1) * P], kd[:, l, g * P:(g + 1) * P], v2[:, 0, 8 * g:8 * g + 8, r, :],
                                       start=m == 0, stop=m == 2)
                mm.then_inc(state_pe.sem, 1)
                wait(pe, route1_vec, b, route1_vec.per)
                if is_first(b):
                    pe.wait_ge(small_vec.sem, 6)
                for t in range(TT):
                    mm = pe.transpose(CB[:, t * P:(t + 1) * P], cw[:, t, :].bitcast(f32), ident)
                mm.then_inc(cw1_pe.sem, 1)
                wait(pe, state_lo, b, 1)
                wait(pe, qk1_lo, b, 2)
                for g in range(2):
                    for m, (l, r) in enumerate(PASSES):
                        mm = pe.matmul(X[1][:, g * P:(g + 1) * P], qT1[:, l, g, P:2 * P], state[:, r, g, :], start=m == 0, stop=m == 2)
                mm.then_inc(cross_pe.sem, 1)
                for u in range(8):
                    if u == 1:
                        wait(pe, cross_vec, b, 1)
                    retention_scores(u)
                    if u == 0 and not is_first(b):
                        wait(pe, qk1_lo, b, 2)
                        project(b - 1, 1)
                    if u < R1:
                        spread_weights(u)
                    if u:
                        retention_values(u - 1)
                        down1(u - 1)
                    if u + 2 < NT1:
                        gate_up(u + 2)
                if not is_last(b):
                    transpose_tokens1(b + 1, 0)
                retention_values(7)
                if not is_last(b):
                    transpose_tokens1(b + 1, 1)
                down1(7)
                for t in range(TT):
                    for r in HALVES:
                        mm = add_to_out(t, cwT[:, t * P:(t + 1) * P], bias_w[:, r, :])
                mm.then_inc(dn1_pe.sem, 1)

            batches(pe, layer1_batch)
            project(NB - 1, 0)
            project(NB - 1, 1)


_INS = ['L0_attn_x', 'L0_attn_Wq', 'L0_attn_Wk', 'L0_attn_Wv', 'L0_attn_Wo', 'L0_ffn_gate_w', 'L0_ffn_w_gate',
        'L0_ffn_w_up', 'L0_ffn_w_down', 'L0_ffn_shgate_w', 'L0_ffn_shw_gate', 'L0_ffn_shw_up', 'L0_ffn_shw_down',
        'L1_attn_qkv_w', 'L1_attn_qkv_norm_w', 'L1_attn_proj_w', 'L1_attn_proj_norm_w', 'L1_attn_norm_w',
        'L1_attn_s', 'L1_ffn_Wg', 'L1_ffn_bg', 'L1_ffn_Wgate', 'L1_ffn_bgate', 'L1_ffn_Wup', 'L1_ffn_bup',
        'L1_ffn_Wdown', 'L1_ffn_bdown', 'L1_ffn_Ws_up', 'L1_ffn_bs_up', 'L1_ffn_Ws_down', 'L1_ffn_bs_down']
_OUTS = [((4, 256, 256), 'float32')]


def kernel(**inputs):
    import numpy as _np
    import concourse.bacc as _bacc
    from concourse import mybir as _mybir
    from concourse.bass_utils import run_bass_kernel_spmd as _run

    nc = _bacc.Bacc("TRN2", target_bir_lowering=False, num_devices=1)
    consts, spread = constants()
    named = [(name, inputs[name]) for name in _INS] + [("consts", consts), ("spread", spread)]
    arrays, args = {}, []
    for name, a in named:
        a = _np.ascontiguousarray(a)
        arrays[f"in_{name}_dram"] = a
        args.append(nc.dram_tensor(f"in_{name}_dram", a.shape, _mybir.dt.from_np(a.dtype), kind="ExternalInput").ap())
    for i, (shape, dtype) in enumerate(_OUTS):
        dt = _mybir.dt.from_np(_np.dtype(dtype))
        args.append(nc.dram_tensor(f"out_{i}_dram", shape, dt, kind="ExternalOutput").ap())
    bass_two_layer_kernel(nc, *args)
    r = _run(nc, [arrays], core_ids=[0])
    got = tuple(r.results[0][f"out_{i}_dram"] for i in range(len(_OUTS)))
    return got[0]
```
